# Optimizing a Trainium2 kernel written in Bass

```python
import numpy as np
import jax
import jax.numpy as jnp

def _softmax(x, axis=-1):
    return jax.nn.softmax(x, axis=axis)

def _gelu(x):
    return jax.nn.gelu(x, approximate=True)

def _silu(x):
    return jax.nn.silu(x)

def _sigmoid(x):
    return jax.nn.sigmoid(x)

def _layernorm(x, axis=-1, eps=1e-05):
    m = jnp.mean(x, axis=axis, keepdims=True)
    v = jnp.var(x, axis=axis, keepdims=True)
    return (x - m) / jnp.sqrt(v + eps)

def _scatter_add(tgt, idx, src, axis=0):
    return tgt.at[idx].add(src)

def _segment_sum(src, seg, n):
    return jax.ops.segment_sum(src, seg, n)
kernel_name = 'mk_decoder_preln_d2_seqx_r4_f2d535'

def setup_inputs(seed: int=0):
    np.random.seed(seed)
    _w = jnp.asarray

    def _rec_inputs():
        import jax
        import jax.numpy as jnp
        _rk = jax.random.key(seed)
        x = -0.0003929 + 0.9999 * jax.random.normal(jax.random.fold_in(_rk, 1), (8, 256, 256), jnp.float32)
        _lenS = 256 - jax.random.randint(jax.random.fold_in(_rk, 7), (8,), 0, max(1, 256 // 4) + 1, jnp.int32)
        _lenS2 = 256 - jax.random.randint(jax.random.fold_in(_rk, 8), (8,), 0, max(1, 256 // 4) + 1, jnp.int32)
        _ctx_1024P = jax.random.normal(jax.random.fold_in(_rk, 11), (8, 16, 256), jnp.float32)
        _ctx_1024c = jax.random.dirichlet(jax.random.fold_in(_rk, 511), 0.3 * jnp.ones((16,), jnp.float32), (8, 256))
        _ctx_1024t = jnp.einsum('bsk,bkd->bsd', _ctx_1024c, _ctx_1024P)
        _ctx_1024t = _ctx_1024t * jax.lax.rsqrt(jnp.mean(jnp.square(_ctx_1024t)) + 1e-12) * 0.953939
        ctx_1024 = 2.81802e-05 + 1.00001 * (_ctx_1024t + 0.3 * jax.random.normal(jax.random.fold_in(_rk, 611), (8, 256, 256), jnp.float32))
        _validS = jnp.arange(256)[None, :] < _lenS[:, None]
        _validS2 = jnp.arange(256)[None, :] < _lenS2[:, None]
        _causal = jnp.tril(jnp.ones((256, 256), dtype=bool))
        mask_SxS2_ik0 = jnp.where(jnp.broadcast_to(_validS2[0:1, :], (256, 256)), 0, 1).astype(jnp.int32)
        return (x, ctx_1024, mask_SxS2_ik0)
    x, ctx_1024, mask_SxS2_ik0 = _rec_inputs()

    def _L0_attn_setup():
        import jax, jax.numpy as jnp
        import numpy as np
        import math
        D_MODEL = 256
        N_HEAD = 16
        N_BR = 4
        DH = D_MODEL // N_HEAD
        H_TOT = N_BR * N_HEAD
        B, T = (1, 256)
        SCALE = math.pi / math.sqrt(3.0)
        ATTNSCALE = DH ** (-0.5)

        def _rope(x):
            t_len, d = (x.shape[2], x.shape[-1])
            inv_freq = 1.0 / 10000.0 ** (jnp.arange(0, d, 2, dtype=jnp.float32) / d)
            freqs = jnp.arange(t_len, dtype=jnp.float32)[:, None] * inv_freq[None, :]
            cos, sin = (jnp.cos(freqs), jnp.sin(freqs))
            x1, x2 = (x[..., 0::2], x[..., 1::2])
            return jnp.concatenate([-x2 * sin + x1 * cos, x1 * sin + x2 * cos], axis=-1)
        key = jax.random.key(seed)
        ks = jax.random.split(key, 12)
        s = D_MODEL ** (-0.5)
        return {'X': jax.random.normal(ks[0], (B, T, D_MODEL), jnp.float32), 'W_Q': jax.random.normal(ks[1], (D_MODEL, D_MODEL * N_BR), jnp.float32) * s, 'b_Q': jax.random.normal(ks[2], (D_MODEL * N_BR,), jnp.float32) * 0.02, 'W_K': jax.random.normal(ks[3], (D_MODEL, D_MODEL), jnp.float32) * s, 'b_K': jax.random.normal(ks[4], (D_MODEL,), jnp.float32) * 0.02, 'W_V': jax.random.normal(ks[5], (D_MODEL, D_MODEL), jnp.float32) * s, 'b_V': jax.random.normal(ks[6], (D_MODEL,), jnp.float32) * 0.02, 'sink_scalars': jax.random.uniform(ks[7], (H_TOT,), jnp.float32, 0.0, 0.1), 'v_nulls': jax.random.normal(ks[8], (N_BR, D_MODEL), jnp.float32) * 0.02, 'W_O': jax.random.normal(ks[9], (N_BR, D_MODEL, D_MODEL), jnp.float32) * s, 'W_O_bias': jax.random.normal(ks[10], (N_BR, D_MODEL), jnp.float32) * 0.02}
    _L0_attn_all = _L0_attn_setup()
    _L0_attn_in = {k: v for k, v in _L0_attn_all.items() if k in ('W_Q', 'b_Q', 'W_K', 'b_K', 'W_V', 'b_V', 'sink_scalars', 'v_nulls', 'W_O', 'W_O_bias')}
    del _L0_attn_all

    def _L0_xattn_setup():
        import jax, jax.numpy as jnp
        import numpy as np
        D_MODEL = 256
        NUM_HEADS = 16
        FOCUS = 3
        EPS = 1e-06

        def _focused_feature_map(x, scale):
            x = jax.nn.relu(x) + EPS
            x = x / scale
            x_norm = jnp.linalg.norm(x, axis=-1, keepdims=True)
            xp = x ** FOCUS
            return xp / jnp.linalg.norm(xp, axis=-1, keepdims=True) * x_norm
        key = jax.random.key(seed)
        ks = jax.random.split(key, 10)
        b, n, d = (4, 1024, D_MODEL)
        s = 0.02
        return {'input_q': jax.random.normal(ks[0], (b, n, d), jnp.float32), 'input_k': jax.random.normal(ks[1], (b, n, d), jnp.float32), 'input_v': jax.random.normal(ks[2], (b, n, d), jnp.float32), 'Wq': jax.random.normal(ks[3], (d, d), jnp.float32) * s, 'bq': jnp.zeros((d,), jnp.float32), 'Wk': jax.random.normal(ks[4], (d, d), jnp.float32) * s, 'bk': jnp.zeros((d,), jnp.float32), 'Wv': jax.random.normal(ks[5], (d, d), jnp.float32) * s, 'bv': jnp.zeros((d,), jnp.float32), 'scale': jnp.zeros((1, 1, d), jnp.float32)}
    _L0_xattn_all = _L0_xattn_setup()
    _L0_xattn_in = {k: v for k, v in _L0_xattn_all.items() if k in ('Wq', 'bq', 'Wk', 'bk', 'Wv', 'bv', 'scale')}
    del _L0_xattn_all

    def _L0_ffn_setup():
        import jax, jax.numpy as jnp
        import numpy as np
        B, T, DIM = (2, 512, 256)
        H, DH, E, K = (16, 64, 8, 2)
        key = jax.random.key(seed)
        ks = jax.random.split(key, 7)
        s = 0.02
        return {'x': jax.random.normal(ks[0], (B, T, DIM), jnp.float32), 'Wq': jax.random.normal(ks[1], (H, DH, DIM), jnp.float32) * s, 'Wk': jax.random.normal(ks[2], (H, DH, DIM), jnp.float32) * s, 'Wv': jax.random.normal(ks[3], (E, DH, DIM), jnp.float32) * s, 'Ws': jax.random.normal(ks[4], (H, E, DIM), jnp.float32) * s, 'Wd': jax.random.normal(ks[5], (H, E, DIM), jnp.float32) * s, 'Wo': jax.random.normal(ks[6], (E, DIM, DH), jnp.float32) * s}
    _L0_ffn_all = _L0_ffn_setup()
    _L0_ffn_in = {k: v for k, v in _L0_ffn_all.items() if k in ('Wq', 'Wk', 'Wv', 'Ws', 'Wd', 'Wo')}
    del _L0_ffn_all

    def _L1_attn_setup():
        import jax, jax.numpy as jnp
        import numpy as np
        HEADS = 8
        DIM_HEAD = 128
        ATTN_MATRIX_SCALE = 1.5
        SCALE = DIM_HEAD ** (-0.5)

        def _split_heads(t):
            b, n, _ = t.shape
            t = t.reshape(b, n, HEADS, DIM_HEAD)
            return t.transpose(2, 0, 1, 3).reshape(HEADS, b * n, DIM_HEAD)
        key = jax.random.key(seed)
        ks = jax.random.split(key, 7)
        b, n, m = (2, 512, 512)
        qd, cd, inner = (256, 192, HEADS * DIM_HEAD)
        x = jax.random.normal(ks[0], (b, n, qd), dtype=jnp.float32)
        context = jax.random.normal(ks[1], (b, m, cd), dtype=jnp.float32)
        Wq = jax.random.normal(ks[2], (qd, inner), dtype=jnp.float32) * qd ** (-0.5)
        Wk = jax.random.normal(ks[3], (cd, inner), dtype=jnp.float32) * cd ** (-0.5)
        Wv = jax.random.normal(ks[4], (cd, inner), dtype=jnp.float32) * cd ** (-0.5)
        Wout = jax.random.normal(ks[5], (inner, qd), dtype=jnp.float32) * inner ** (-0.5)
        bout = jnp.zeros((qd,), dtype=jnp.float32)
        return {'x': x, 'context': context, 'Wq': Wq, 'Wk': Wk, 'Wv': Wv, 'Wout': Wout, 'bout': bout}
    _L1_attn_all = _L1_attn_setup()
    _L1_attn_in = {k: v for k, v in _L1_attn_all.items() if k in ('context', 'Wq', 'Wk', 'Wv', 'Wout', 'bout')}
    del _L1_attn_all

    def _L1_xattn_setup():
        import jax, jax.numpy as jnp
        import numpy as np
        EMB = 256
        ATTN = 64
        HEADS = 16
        B, S = (2, 512)
        key = jax.random.key(seed)
        ks = jax.random.split(key, 8)
        xavier = np.sqrt((EMB + ATTN * HEADS) / 2).astype(np.float32)
        q = jax.random.normal(ks[0], (B, S, EMB), dtype=jnp.float32)
        k = jax.random.normal(ks[1], (B, S, EMB), dtype=jnp.float32)
        v = jax.random.normal(ks[2], (B, S, EMB), dtype=jnp.float32)
        mask = jnp.tril(jnp.ones((S, S), dtype=jnp.int32))
        w_q = jax.random.normal(ks[3], (EMB, ATTN * HEADS), dtype=jnp.float32) / xavier
        w_k = jax.random.normal(ks[4], (EMB, ATTN * HEADS), dtype=jnp.float32) / xavier
        w_v = jax.random.normal(ks[5], (EMB, ATTN * HEADS), dtype=jnp.float32) / xavier
        lim = 1.0 / np.sqrt(ATTN * HEADS)
        out_w = jax.random.uniform(ks[6], (EMB, ATTN * HEADS), dtype=jnp.float32, minval=-lim, maxval=lim)
        out_b = jax.random.uniform(ks[7], (EMB,), dtype=jnp.float32, minval=-lim, maxval=lim)
        return {'q': q, 'k': k, 'v': v, 'mask': mask, 'w_q': w_q, 'w_k': w_k, 'w_v': w_v, 'out_w': out_w, 'out_b': out_b}
    _L1_xattn_all = _L1_xattn_setup()
    _L1_xattn_in = {k: v for k, v in _L1_xattn_all.items() if k in ('w_q', 'w_k', 'w_v', 'out_w', 'out_b')}
    del _L1_xattn_all

    def _L1_ffn_setup():
        import jax, jax.numpy as jnp
        import numpy as np
        MODEL_DIM = 256
        HIDDEN = 512
        NUM_GROUPS = 2
        EXPERTS_PER_GP = 4
        NUM_EXPERTS = NUM_GROUPS * EXPERTS_PER_GP
        TOP_K = 2
        B, T = (2, 512)

        def _swiglu(x):
            a, b = jnp.split(x, 2, axis=-1)
            return jax.nn.silu(a) * b
        key = jax.random.key(seed)
        ks = jax.random.split(key, 7)
        s = 0.02
        return {'x': jax.random.normal(ks[0], (B, T, MODEL_DIM), jnp.float32), 'w_in': jax.random.normal(ks[1], (HIDDEN * 2, MODEL_DIM), jnp.float32) * s, 'w_out': jax.random.normal(ks[2], (MODEL_DIM, HIDDEN), jnp.float32) * s, 'w1': jax.random.normal(ks[3], (HIDDEN * 2, MODEL_DIM), jnp.float32) * s, 'w2': jax.random.normal(ks[4], (NUM_EXPERTS, MODEL_DIM, HIDDEN), jnp.float32) * s, 'wg': jax.random.normal(ks[5], (NUM_GROUPS, MODEL_DIM), jnp.float32) * s, 'we': jax.random.normal(ks[6], (NUM_EXPERTS, MODEL_DIM), jnp.float32) * s, 'gb': jnp.zeros((NUM_GROUPS,), jnp.float32), 'eb': jnp.zeros((NUM_EXPERTS,), jnp.float32)}
    _L1_ffn_all = _L1_ffn_setup()
    _L1_ffn_in = {k: v for k, v in _L1_ffn_all.items() if k in ('w_in', 'w_out', 'w1', 'w2', 'wg', 'we', 'gb', 'eb')}
    del _L1_ffn_all
    return {'x': x, 'ctx_1024': ctx_1024, 'mask_SxS2_ik0': mask_SxS2_ik0, 'L0_attn_W_Q': _L0_attn_in['W_Q'], 'L0_attn_b_Q': _L0_attn_in['b_Q'], 'L0_attn_W_K': _L0_attn_in['W_K'], 'L0_attn_b_K': _L0_attn_in['b_K'], 'L0_attn_W_V': _L0_attn_in['W_V'], 'L0_attn_b_V': _L0_attn_in['b_V'], 'L0_attn_sink_scalars': _L0_attn_in['sink_scalars'], 'L0_attn_v_nulls': _L0_attn_in['v_nulls'], 'L0_attn_W_O': _L0_attn_in['W_O'], 'L0_attn_W_O_bias': _L0_attn_in['W_O_bias'], 'L0_xattn_Wq': _L0_xattn_in['Wq'], 'L0_xattn_bq': _L0_xattn_in['bq'], 'L0_xattn_Wk': _L0_xattn_in['Wk'], 'L0_xattn_bk': _L0_xattn_in['bk'], 'L0_xattn_Wv': _L0_xattn_in['Wv'], 'L0_xattn_bv': _L0_xattn_in['bv'], 'L0_xattn_scale': _L0_xattn_in['scale'], 'L0_ffn_Wq': _L0_ffn_in['Wq'], 'L0_ffn_Wk': _L0_ffn_in['Wk'], 'L0_ffn_Wv': _L0_ffn_in['Wv'], 'L0_ffn_Ws': _L0_ffn_in['Ws'], 'L0_ffn_Wd': _L0_ffn_in['Wd'], 'L0_ffn_Wo': _L0_ffn_in['Wo'], 'L1_attn_context': _L1_attn_in['context'], 'L1_attn_Wq': _L1_attn_in['Wq'], 'L1_attn_Wk': _L1_attn_in['Wk'], 'L1_attn_Wv': _L1_attn_in['Wv'], 'L1_attn_Wout': _L1_attn_in['Wout'], 'L1_attn_bout': _L1_attn_in['bout'], 'L1_xattn_w_q': _L1_xattn_in['w_q'], 'L1_xattn_w_k': _L1_xattn_in['w_k'], 'L1_xattn_w_v': _L1_xattn_in['w_v'], 'L1_xattn_out_w': _L1_xattn_in['out_w'], 'L1_xattn_out_b': _L1_xattn_in['out_b'], 'L1_ffn_w_in': _L1_ffn_in['w_in'], 'L1_ffn_w_out': _L1_ffn_in['w_out'], 'L1_ffn_w1': _L1_ffn_in['w1'], 'L1_ffn_w2': _L1_ffn_in['w2'], 'L1_ffn_wg': _L1_ffn_in['wg'], 'L1_ffn_we': _L1_ffn_in['we'], 'L1_ffn_gb': _L1_ffn_in['gb'], 'L1_ffn_eb': _L1_ffn_in['eb']}

def reference(x, ctx_1024, mask_SxS2_ik0, L0_attn_W_Q, L0_attn_b_Q, L0_attn_W_K, L0_attn_b_K, L0_attn_W_V, L0_attn_b_V, L0_attn_sink_scalars, L0_attn_v_nulls, L0_attn_W_O, L0_attn_W_O_bias, L0_xattn_Wq, L0_xattn_bq, L0_xattn_Wk, L0_xattn_bk, L0_xattn_Wv, L0_xattn_bv, L0_xattn_scale, L0_ffn_Wq, L0_ffn_Wk, L0_ffn_Wv, L0_ffn_Ws, L0_ffn_Wd, L0_ffn_Wo, L1_attn_context, L1_attn_Wq, L1_attn_Wk, L1_attn_Wv, L1_attn_Wout, L1_attn_bout, L1_xattn_w_q, L1_xattn_w_k, L1_xattn_w_v, L1_xattn_out_w, L1_xattn_out_b, L1_ffn_w_in, L1_ffn_w_out, L1_ffn_w1, L1_ffn_w2, L1_ffn_wg, L1_ffn_we, L1_ffn_gb, L1_ffn_eb):
    import jax
    import jax.numpy as jnp

    def _L0_attn_ref(X, W_Q, b_Q, W_K, b_K, W_V, b_V, sink_scalars, v_nulls, W_O, W_O_bias):
        import jax, jax.numpy as jnp
        import numpy as np
        import math
        D_MODEL = 256
        N_HEAD = 16
        N_BR = 4
        DH = D_MODEL // N_HEAD
        H_TOT = N_BR * N_HEAD
        B, T = (1, 256)
        SCALE = math.pi / math.sqrt(3.0)
        ATTNSCALE = DH ** (-0.5)

        def _rope(x):
            t_len, d = (x.shape[2], x.shape[-1])
            inv_freq = 1.0 / 10000.0 ** (jnp.arange(0, d, 2, dtype=jnp.float32) / d)
            freqs = jnp.arange(t_len, dtype=jnp.float32)[:, None] * inv_freq[None, :]
            cos, sin = (jnp.cos(freqs), jnp.sin(freqs))
            x1, x2 = (x[..., 0::2], x[..., 1::2])
            return jnp.concatenate([-x2 * sin + x1 * cos, x1 * sin + x2 * cos], axis=-1)
        Bv, Tv, C = X.shape
        q = (X @ W_Q + b_Q).reshape(Bv, Tv, H_TOT, DH).transpose(0, 2, 1, 3)
        k_base = (X @ W_K + b_K).reshape(Bv, Tv, N_HEAD, DH).transpose(0, 2, 1, 3)
        v_base = (X @ W_V + b_V).reshape(Bv, Tv, N_HEAD, DH).transpose(0, 2, 1, 3)
        k = jnp.tile(k_base, (1, N_BR, 1, 1))
        v = jnp.tile(v_base, (1, N_BR, 1, 1))
        q, k = (_rope(q), _rope(k))
        scores = jnp.einsum('bhtd,bhsd->bhts', q, k) * ATTNSCALE
        key_self = jnp.clip(jnp.sum(k * k, axis=-1), 1e-06, None)
        w = jax.nn.softplus(scores / jnp.sqrt(key_self)[:, :, None, :])
        causal = jnp.tril(jnp.ones((Tv, Tv), bool))
        w = jnp.where(causal, w, 0.0)
        w = w * jax.nn.sigmoid(SCALE * w)
        sinks = sink_scalars.reshape(1, H_TOT, 1, 1)
        w = jnp.where(w < sinks, 0.0, w)
        total = jnp.sum(w, axis=-1, keepdims=True) + sinks + 1e-06
        probs_tokens = w / total
        probs_sink = sinks / total
        out = jnp.einsum('bhts,bhsd->bhtd', probs_tokens, v)
        v_null = v_nulls.reshape(H_TOT, DH)[None, :, None, :]
        out = out + probs_sink * v_null
        context = out.reshape(Bv, N_BR, N_HEAD, Tv, DH).transpose(0, 1, 3, 2, 4)
        context = context.reshape(Bv, N_BR, Tv, C)
        y = jnp.einsum('bntc,ncd->bntd', context, W_O) + W_O_bias[None, :, None, :]
        return y.mean(axis=1)

    def _L0_xattn_ref(input_q, input_k, input_v, Wq, bq, Wk, bk, Wv, bv, scale):
        import jax, jax.numpy as jnp
        import numpy as np
        D_MODEL = 256
        NUM_HEADS = 16
        FOCUS = 3
        EPS = 1e-06

        def _focused_feature_map(x, scale):
            x = jax.nn.relu(x) + EPS
            x = x / scale
            x_norm = jnp.linalg.norm(x, axis=-1, keepdims=True)
            xp = x ** FOCUS
            return xp / jnp.linalg.norm(xp, axis=-1, keepdims=True) * x_norm
        b, n_q, d = input_q.shape
        h = NUM_HEADS
        c = d // h
        q = input_q @ Wq + bq
        k = input_k @ Wk + bk
        v = input_v @ Wv + bv
        sp = jax.nn.softplus(scale)
        q = _focused_feature_map(q, sp)
        k = _focused_feature_map(k, sp)
        q = q.reshape(b, n_q, h, c).transpose(0, 2, 1, 3)
        k = k.reshape(b, -1, h, c).transpose(0, 2, 1, 3)
        v = v.reshape(b, -1, h, c).transpose(0, 2, 1, 3)
        z = 1.0 / (jnp.einsum('bhic,bhc->bhi', q, k.sum(axis=2)) + EPS)
        kv = jnp.einsum('bhjc,bhjd->bhcd', k, v)
        x = jnp.einsum('bhic,bhcd->bhid', q, kv) * z[..., None]
        return x.transpose(0, 2, 1, 3).reshape(b, n_q, d)

    def _L0_ffn_ref(x, Wq, Wk, Wv, Ws, Wd, Wo):
        import jax, jax.numpy as jnp
        import numpy as np
        B, T, DIM = (2, 512, 256)
        H, DH, E, K = (16, 64, 8, 2)
        scale = DH ** (-0.5)
        q = jnp.einsum('btc,hdc->bhtd', x, Wq)
        k = jnp.einsum('btc,hdc->bhtd', x, Wk)
        gate_v = jnp.einsum('btc,hec->bthe', x, Ws)
        w, sel = jax.lax.top_k(gate_v, K)
        wsig = jax.nn.sigmoid(w)
        oh = jax.nn.one_hot(sel, E, dtype=x.dtype)
        mix_v = jnp.einsum('bthk,bthke->bthe', wsig, oh)
        proj_v = jnp.einsum('btc,edc->bted', x, Wv)
        v = jnp.einsum('bthe,bted->bhtd', mix_v, proj_v)
        scores = jnp.einsum('bhid,bhjd->bhij', q * scale, k)
        probs = jax.nn.softmax(scores, axis=-1)
        attn = jnp.einsum('bhij,bhjd->bihd', probs, v)
        gate_o = jnp.einsum('btc,hec->bthe', x, Wd)
        _, sel_o = jax.lax.top_k(gate_o, K)
        mask_o = jax.nn.one_hot(sel_o, E, dtype=x.dtype).sum(axis=3)
        res = jnp.einsum('bthe,bthd,efd->bthf', mask_o, attn, Wo)
        return res.sum(axis=2)

    def _L1_attn_ref(x, context, Wq, Wk, Wv, Wout, bout):
        import jax, jax.numpy as jnp
        import numpy as np
        HEADS = 8
        DIM_HEAD = 128
        ATTN_MATRIX_SCALE = 1.5
        SCALE = DIM_HEAD ** (-0.5)

        def _split_heads(t):
            b, n, _ = t.shape
            t = t.reshape(b, n, HEADS, DIM_HEAD)
            return t.transpose(2, 0, 1, 3).reshape(HEADS, b * n, DIM_HEAD)
        b, n, _ = x.shape
        qh = _split_heads(jnp.einsum('bnq,qi->bni', x, Wq))
        kh = _split_heads(jnp.einsum('bmc,ci->bmi', context, Wk))
        vh = _split_heads(jnp.einsum('bmc,ci->bmi', context, Wv))
        sim = jnp.einsum('hid,hjd->hij', qh, kh) * SCALE
        mean = jnp.mean(sim, axis=-1, keepdims=True)
        sim = (sim - mean) * ATTN_MATRIX_SCALE + mean
        attn = jax.nn.softmax(sim, axis=-1)
        out = jnp.einsum('hij,hjd->hid', attn, vh)
        out = out.reshape(HEADS, b, n, DIM_HEAD).transpose(1, 2, 0, 3)
        out = out.reshape(b, n, HEADS * DIM_HEAD)
        return jnp.einsum('bni,iq->bnq', out, Wout) + bout

    def _L1_xattn_ref(q, k, v, mask, w_q, w_k, w_v, out_w, out_b):
        import jax, jax.numpy as jnp
        import numpy as np
        EMB = 256
        ATTN = 64
        HEADS = 16
        B, S = (2, 512)
        batch, seq_q, _ = q.shape
        seq_k = k.shape[1]
        fq = (q @ w_q).reshape(batch, seq_q, HEADS, ATTN).transpose(0, 2, 1, 3)
        fk = (k @ w_k).reshape(batch, seq_k, HEADS, ATTN).transpose(0, 2, 1, 3)
        fv = (v @ w_v).reshape(batch, seq_k, HEADS, ATTN).transpose(0, 2, 1, 3)
        f = jnp.einsum('bhqd,bhkd->bhqk', fq, fk) / jnp.sqrt(jnp.float32(ATTN))
        f = f + jnp.where(mask == 0, jnp.float32(-1000000000.0), jnp.float32(0.0))
        ps = jax.nn.softmax(f, axis=-1)
        attns = jnp.einsum('bhqk,bhkd->bhqd', ps, fv)
        attns = attns.transpose(0, 2, 1, 3).reshape(batch, seq_q, HEADS * ATTN)
        return attns @ out_w.T + out_b

    def _L1_ffn_ref(x, w_in, w_out, w1, w2, wg, we, gb, eb):
        import jax, jax.numpy as jnp
        import numpy as np
        MODEL_DIM = 256
        HIDDEN = 512
        NUM_GROUPS = 2
        EXPERTS_PER_GP = 4
        NUM_EXPERTS = NUM_GROUPS * EXPERTS_PER_GP
        TOP_K = 2
        B, T = (2, 512)

        def _swiglu(x):
            a, b = jnp.split(x, 2, axis=-1)
            return jax.nn.silu(a) * b
        Bs, Ts, C = x.shape
        S = Bs * Ts
        flat = x.reshape(S, C)
        shared = _swiglu(flat @ w_in.T) @ w_out.T
        g_probs = jax.nn.softmax(flat @ wg.T + gb, axis=-1)
        g_idx = jnp.argmax(g_probs, axis=-1)
        e_logits = flat @ we.T + eb
        egid = jnp.arange(NUM_EXPERTS) // EXPERTS_PER_GP
        masked = jnp.where(g_idx[:, None] == egid[None, :], e_logits, -jnp.inf)
        e_probs = jax.nn.softmax(masked, axis=-1)
        g_prob = jnp.take_along_axis(g_probs, g_idx[:, None], axis=1)
        p_expert = e_probs * g_prob
        topv, topi = jax.lax.top_k(p_expert, TOP_K)
        w_se = jnp.zeros((S, NUM_EXPERTS), x.dtype).at[jnp.arange(S)[:, None], topi].add(topv)
        h = _swiglu(flat @ w1.T)
        routed = jnp.zeros_like(shared)
        for e in range(NUM_EXPERTS):
            routed = routed + h * w_se[:, e:e + 1] @ w2[e].T
        return (shared + routed).reshape(Bs, Ts, C)
    x = x + _L0_attn_ref(_layernorm(x, axis=-1), L0_attn_W_Q, L0_attn_b_Q, L0_attn_W_K, L0_attn_b_K, L0_attn_W_V, L0_attn_b_V, L0_attn_sink_scalars, L0_attn_v_nulls, L0_attn_W_O, L0_attn_W_O_bias)
    x = x + _L0_xattn_ref(_layernorm(x, axis=-1), ctx_1024, ctx_1024, L0_xattn_Wq, L0_xattn_bq, L0_xattn_Wk, L0_xattn_bk, L0_xattn_Wv, L0_xattn_bv, L0_xattn_scale)
    x = x + _L0_ffn_ref(_layernorm(x, axis=-1), L0_ffn_Wq, L0_ffn_Wk, L0_ffn_Wv, L0_ffn_Ws, L0_ffn_Wd, L0_ffn_Wo)
    x = x + _L1_attn_ref(_layernorm(x, axis=-1), L1_attn_context, L1_attn_Wq, L1_attn_Wk, L1_attn_Wv, L1_attn_Wout, L1_attn_bout)
    x = x + _L1_xattn_ref(_layernorm(x, axis=-1), ctx_1024, ctx_1024, mask_SxS2_ik0, L1_xattn_w_q, L1_xattn_w_k, L1_xattn_w_v, L1_xattn_out_w, L1_xattn_out_b)
    x = x + _L1_ffn_ref(_layernorm(x, axis=-1), L1_ffn_w_in, L1_ffn_w_out, L1_ffn_w1, L1_ffn_w2, L1_ffn_wg, L1_ffn_we, L1_ffn_gb, L1_ffn_eb)
    return x

_drawn_inputs = setup_inputs


def setup_inputs(seed=0):
    import zlib

    import numpy as np

    out = dict(_drawn_inputs(seed))
    spreads = {'L0_xattn_bq': (0.0, 0.1),
     'L0_xattn_bk': (0.0, 0.313),
     'L0_xattn_bv': (0.0, 0.1),
     'L0_xattn_scale': (0.0, 0.448),
     'L1_attn_bout': (0.0, 0.1),
     'L1_ffn_gb': (0.0, 0.8),
     'L1_ffn_eb': (0.0, 0.8)}
    factors = {'L0_attn_W_Q': 3.598,
     'L0_attn_b_Q': 8.0,
     'L0_attn_W_K': 3.609,
     'L0_attn_b_K': 8.0,
     'L0_attn_b_V': 5.181,
     'L0_attn_sink_scalars': 8.0,
     'L0_attn_v_nulls': 8.0,
     'L0_attn_W_O_bias': 5.596,
     'L0_ffn_Wq': 8.0,
     'L0_ffn_Wk': 8.0,
     'L0_ffn_Ws': 3.458,
     'L1_xattn_out_b': 3.269,
     'L1_ffn_w1': 8.0,
     'L1_ffn_w2': 8.0,
     'L1_ffn_wg': 8.0,
     'L1_ffn_we': 8.0,
     'L1_ffn_w_in': 8.0,
     'L1_ffn_w_out': 8.0}
    for name, (base, spread) in spreads.items():
        noise = np.random.default_rng([zlib.crc32(name.encode()), seed]).standard_normal(out[name].shape)
        drawn = base * np.exp(spread * noise) if base else spread * noise
        out[name] = jnp.asarray(drawn.astype(out[name].dtype))
    for name, factor in factors.items():
        out[name] = (out[name] * factor).astype(out[name].dtype)
    return out
```

```python
from contextlib import ExitStack
import math

import numpy as np
import concourse.bass as bass
from concourse import mybir

F32 = mybir.dt.float32
I32 = mybir.dt.int32
ALU = mybir.AluOpType
ACT = mybir.ActivationFunctionType
AX = mybir.AxisListType

P = 128
B, T, D = 8, 256, 256
TILES = B * T // P
TT = T // P
CC = D // P
LN_EPS = 1e-5


class Scope:

    semaphores = None

    def __init__(self, nc, stack, prefix):
        self.nc, self.stack, self.prefix = nc, stack, prefix

    def sb(self, name, shape, dtype=F32):
        return self.stack.enter_context(self.nc.sbuf_tensor(f"{self.prefix}_{name}", shape, dtype))

    def sem(self, name):
        return (Scope.semaphores or self.stack).enter_context(self.nc.semaphore(f"{self.prefix}_{name}"))

    def sems(self, name, n):
        return [self.sem(f"{name}{i}") for i in range(n)]


class Steps:

    def __init__(self, eng, sem, base=0, per=None):
        self.eng, self.sem, self.base, self.per, self.n = eng, sem, base, per, 0

    def did(self, instruction):
        instruction.then_inc(self.sem, 1)
        self.n += 1

    def wait(self):
        self.eng.wait_ge(self.sem, self.base + self.n)

    def link(self, instruction):
        self.did(instruction)
        self.wait()

    def end(self):
        assert self.per is None or self.n == self.per, (self.n, self.per)


def alone(eng, sem, value, passed):
    eng.wait_ge(sem, value)
    eng.sem_inc(passed, 1)


def chunked(w):
    return w.rearrange("(k p) n -> p k n", p=P)


def over_partitions(v, n):
    return v.rearrange("(a n) -> a n", a=1).to_broadcast([P, n])


class Norm:

    def __init__(self, s):
        self.runs = 0
        self.own, self.variance_ready, self.std_ready = s.sem("own"), s.sem("variance_ready"), s.sem("std_ready")
        self.normalised, self.transposed, self.copied = (s.sems(n, TT) for n in ("normalised", "transposed", "copied"))


def normalise(nc, norm, x_all, xnT_all, ident, psum, loads, loaded):
    with ExitStack() as stack:
        run = norm.runs
        norm.runs += 1
        b0 = run * B
        s = Scope(nc, stack, f"ln{run}")
        stats = s.sb("stats", [P, TILES, 6])
        mean_var = s.sb("mean_var", [P, TILES, 2])
        std = s.sb("std", [P, TILES])
        rstd = s.sb("rstd", [P, TILES])
        shift = s.sb("shift", [P, TILES])
        eps = s.sb("eps", [P, 1])
        xn = s.sb("xn", [P, TT, D])
        psT = psum[:, 0:TT, :].rearrange("p t (c n) -> p t c n", n=P)
        variance_ready, std_ready = norm.variance_ready, norm.std_ready
        normalised, transposed, copied = norm.normalised, norm.transposed, norm.copied
        block = stack.enter_context(nc.Block())

        @block.sync
        def _(sp):
            for dst, src in loads:
                sp.dma_start(dst, src).then_inc(loaded, 16)

        @block.vector
        def _(dve):
            step = Steps(dve, norm.own, run * (TILES + 3))
            step.did(dve.memset(eps[:], LN_EPS))
            for t in range(TILES):
                step.did(dve.bn_stats(stats[:, t, :], x_all[:, t, :]))
            step.wait()
            for t in range(TILES):
                ins = dve.bn_aggr(mean_var[:, t, :], stats[:, t, :])
            ins.then_inc(variance_ready, 1)
            dve.wait_ge(std_ready, run + 1)
            step.link(dve.reciprocal(rstd[:], std[:]))
            step.link(dve.scalar_tensor_tensor(shift[:], mean_var[:, :, 0], -1.0, rstd[:], ALU.mult, ALU.mult))
            with dve.Fori(0, B) as b:
                for t in range(TT):
                    dve.wait_ge(transposed[t], b0 + b)
                    tile = b * TT + t
                    dve.tensor_scalar(xn[:, t, :], x_all[:, bass.ds(tile, 1), :], rstd[:, bass.ds(tile, 1)],
                                      shift[:, bass.ds(tile, 1)], ALU.mult, ALU.add).then_inc(normalised[t], 1)

        @block.tensor
        def _(pe):
            with pe.Fori(0, B) as b:
                for t in range(TT):
                    pe.wait_ge(normalised[t], b0 + b + 1)
                    pe.wait_ge(copied[t], b0 + b)
                    for c in range(CC):
                        ins = pe.transpose(psT[:, t, c, :], xn[:, t, c * P:(c + 1) * P], ident[:])
                    ins.then_inc(transposed[t], 1)

        @block.scalar
        def _(act):
            act.wait_ge(variance_ready, run + 1)
            act.activation(std[:], mean_var[:, :, 1], ACT.Sqrt, bias=eps[:, 0:1]).then_inc(std_ready, 1)
            with act.Fori(0, B) as b:
                for t in range(TT):
                    act.wait_ge(transposed[t], b0 + b + 1)
                    act.activation(xnT_all[:, bass.ds(b, 1), :, t * P:(t + 1) * P], psT[:, t, 0:CC, :],
                                   ACT.Copy).then_inc(copied[t], 1)


BR, NH, DH = 4, 16, 16
NU = NH
GROUP = 4
RING = 2 * GROUP
SILU_SCALE = math.pi / math.sqrt(3.0)
CAP = 44.0


def attention0(nc, norm, x_all, xnT_all, ident, psum, a):
    with ExitStack() as stack:
        s = Scope(nc, stack, "a0")
        wq, wqs = s.sb("wq", [P, CC, BR * D]), s.sb("wqs", [P, CC, BR * D])
        wk, wks, wv = s.sb("wk", [P, CC, D]), s.sb("wks", [P, CC, D]), s.sb("wv", [P, CC, D])
        wo = s.sb("wo", [P, BR * CC, D])
        bq = s.sb("bq", [P, 2, 8])
        bk = s.sb("bk", [P, 2, CC])
        bv = s.sb("bv", [P, D])
        rope = s.sb("rope", [P, 2, T])
        same_head = s.sb("same_head", [P, P])
        head_mask = s.sb("head_mask", [P, 8])
        sinks = s.sb("sinks", [P, BR * NH])
        sinks_eps = s.sb("sinks_eps", [P, BR * NH])
        vnull = s.sb("vnull", [P, BR * NH, DH])
        bo = s.sb("bo", [P, BR, D])
        ln_quarter = s.sb("ln_quarter", [P, 1])
        xnT = s.sb("xnT", [P, CC, T])
        rot_a, rot_b = s.sb("rot_a", [P, 2, T]), s.sb("rot_b", [P, 2, T])
        qT = s.sb("qT", [P, CC, BR, T])
        kT = s.sb("kT", [P, CC, T])
        ksq = s.sb("ksq", [P, CC, T])
        kT_head = s.sb("kT_head", [P, NH, T])
        v1 = s.sb("v1", [P, TT, NH, DH + 1])
        w = s.sb("w", [P, RING, BR, T + P])
        ctx = s.sb("ctx", [P, TT, BR * NH, DH + 1])
        total = s.sb("total", [P, TT, BR * NH])
        ctxn = s.sb("ctxn", [P, TT, BR * NH, DH])
        ctxT = s.sb("ctxT", [P, TT, 8, P])
        psS = psum[:, 0:6, :].rearrange("p (s k) n -> p s k n", s=2)
        psO = psum[:, 6:8, :]
        bank = [psum[:, i, :] for i in range(6)]

        loaded = s.sem("loaded")
        x_here = s.sem("x_here")
        projected, taken = s.sem("projected"), s.sem("taken")
        ksq_ready, knorm_ready, kheads_ready = s.sem("ksq_ready"), s.sem("knorm_ready"), s.sem("kheads_ready")
        scored, clamped, ln_done, softplus_done = (s.sem(n) for n in ("scored", "clamped", "ln_done", "softplus_done"))
        masked, silu_done, weights_done = s.sem("masked"), s.sem("silu_done"), s.sem("weights_done")
        summed, ctx_taken, ctx_ready = s.sem("summed"), s.sem("ctx_taken"), s.sem("ctx_ready")
        ctx_turned, turned_taken = s.sem("ctx_turned"), s.sem("turned_taken")
        out_ready, out_taken = s.sem("out_ready"), s.sem("out_taken")
        own_dve, own_act = s.sem("own_dve"), s.sem("own_act")
        consts, passed = s.sem("consts"), s.sem("passed")

        loads = [(wk[:], chunked(a["wk"])), (wks[:], chunked(a["wks"])), (wv[:], chunked(a["wv"])),
                 (wq[:], chunked(a["wq"])), (wqs[:], chunked(a["wqs"])), (wo[:], chunked(a["wo"])),
                 (bq[:], a["bq"]), (bk[:], a["bk"]), (bv[:], over_partitions(a["bv"], D)),
                 (rope[:], a["rope"]), (same_head[:], a["same_head"]), (head_mask[:], a["head_mask"]),
                 (sinks[:], over_partitions(a["sinks"], BR * NH)),
                 (vnull[:].rearrange("p h d -> p (h d)"), over_partitions(a["vnull"], BR * D)),
                 (bo[:].rearrange("p r d -> p (r d)"), over_partitions(a["bo"], BR * D))]
        normalise(nc, norm, x_all, xnT_all, ident, psum, loads, loaded)
        block = stack.enter_context(nc.Block())
        order = [("k", 0), ("k", 1), ("v", 0), ("q", 0), ("q", 1), ("n", 0)] + [("q", i) for i in range(2, 8)]
        NP = len(order)

        @block.sync
        def _(sp):
            with sp.Fori(0, B) as b:
                sp.wait_ge(projected, b * NP)
                sp.dma_start(xnT[:], xnT_all[:, bass.ds(b, 1), :, :]).then_inc(x_here, 16)

        @block.tensor
        def _(pe):
            pe.wait_ge(loaded, 16 * len(loads))
            with pe.Fori(0, B) as b:
                pe.wait_ge(x_here, b * 16 + 16)
                for n, (kind, i) in enumerate(order):
                    if n < 6:
                        pe.wait_ge(out_taken, b)
                    else:
                        pe.wait_ge(taken, b * NP + (n - 5))
                    if kind == "v":
                        for t in range(TT):
                            for c in range(CC):
                                ins = pe.matmul(bank[n % 6][:, t * D:(t + 1) * D], xnT[:, c, t * P:(t + 1) * P],
                                                wv[:, c, :], start=(c == 0), stop=(c == CC - 1))
                    elif kind == "n":
                        pe.wait_ge(ksq_ready, b * CC + CC)
                        for g in range(CC):
                            ins = pe.matmul(bank[n % 6][:, g * T:(g + 1) * T], same_head[:], ksq[:, g, :],
                                            start=True, stop=True)
                    else:
                        for v, weights in enumerate((wk, wks) if kind == "k" else (wq, wqs)):
                            for c in range(CC):
                                ins = pe.matmul(bank[n % 6][:, v * T:(v + 1) * T], weights[:, c, i * P:(i + 1) * P],
                                                xnT[:, c, :], start=(c == 0), stop=(c == CC - 1))
                    ins.then_inc(projected, 1)

                def sums(u):
                    pe.wait_ge(weights_done, b * NU + u + 1)
                    if u >= 2:
                        pe.wait_ge(ctx_taken, b * NU + u - 1)
                    for t in range(TT):
                        for r in range(BR):
                            out = psO[:, u % 2, (t * BR + r) * 17:(t * BR + r) * 17 + 17]
                            if t == 0:
                                ins = pe.matmul(out, w[:, u % RING, r, 0:P], v1[:, 0, u, :], start=True, stop=True)
                            else:
                                pe.matmul(out, w[:, u % RING, r, P:T], v1[:, 0, u, :], start=True, stop=False)
                                ins = pe.matmul(out, w[:, u % RING, r, T:T + P], v1[:, 1, u, :], start=False, stop=True)
                    ins.then_inc(summed, 1)

                for u in range(NU):
                    g, slot = u // 8, u % 2
                    if u == 0:
                        pe.wait_ge(taken, b * NP + NP)
                    if u % 8 == 0:
                        pe.wait_ge(kheads_ready, b * CC + g + 1)
                    if u >= 2:
                        pe.wait_ge(softplus_done, b * NU + u - 1)
                    for half in range(2):
                        pe.matmul(psS[:, slot, half, :], kT_head[:, u, 0:P], qT[:, g, 2 * half:2 * half + 2, :],
                                  start=True, stop=True)
                    pe.matmul(psS[:, slot, 2, :], kT_head[:, u, P:T], qT[:, g, :, P:T],
                              start=True, stop=True).then_inc(scored, 1)
                    if u >= GROUP:
                        sums(u - GROUP)
                for u in range(NU - GROUP, NU):
                    sums(u)
                pe.wait_ge(ctx_ready, b + 1)
                for t in range(TT):
                    for h in range(2):
                        for i in range(4):
                            k = 4 * h + i
                            ins = pe.transpose(bank[2 * t + h][:, i * P:(i + 1) * P],
                                               ctxn[:, t, 8 * k:8 * k + 8, :].rearrange("p h d -> p (h d)"), ident[:])
                        ins.then_inc(ctx_turned, 1)
                pe.wait_ge(turned_taken, b * 4 + 4)
                for t in range(TT):
                    for k in range(8):
                        ins = pe.matmul(bank[4][:, t * D:(t + 1) * D], ctxT[:, t, k, :], wo[:, k, :],
                                        start=(k == 0), stop=(k == 7))
                ins.then_inc(out_ready, 1)

        @block.scalar
        def _(act):
            act.preload_act_table_set("natural_log_exp_and_others")
            act.wait_ge(consts, 1)
            with act.Fori(0, B) as b:
                per = 1 + NU
                step = Steps(act, own_act, b * per, per)
                act.preload_act_table_set("natural_log_exp_and_others")
                act.wait_ge(taken, b * NP + order.index(("n", 0)) + 1)
                step.link(act.activation(ksq[:], ksq[:], ACT.Ln))
                act.activation(ksq[:], ksq[:], ACT.Exp, scale=-0.5, bias=ln_quarter[:, 0:1]).then_inc(knorm_ready, 1)
                for group in range(NU // GROUP):
                    if group:
                        act.preload_act_table_set("natural_log_exp_and_others")
                    for u in range(group * GROUP, group * GROUP + GROUP):
                        wu = w[:, u % RING, :, :]
                        act.wait_ge(clamped, b * NU + u + 1)
                        step.link(act.activation(wu, wu, ACT.Exp))
                        act.activation(wu, wu, ACT.Ln, bias=1.0).then_inc(ln_done, 1)
                    for u in range(group * GROUP, group * GROUP + GROUP):
                        wu = w[:, u % RING, :, :]
                        act.wait_ge(masked, b * NU + u + 1)
                        act.activation(wu, wu, ACT.Silu, scale=SILU_SCALE).then_inc(silu_done, 1)
                for i in range(4):
                    act.wait_ge(ctx_turned, b * 4 + i + 1)
                    act.activation(ctxT[:, i // 2, 4 * (i % 2):4 * (i % 2) + 4, :], bank[i], ACT.Copy)\
                       .then_inc(turned_taken, 1)
                step.end()

        @block.gpsimd
        def _(pool):
            pool.wait_ge(consts, 1)
            with pool.Fori(0, B) as b:
                for u in range(NU):
                    alone(pool, softplus_done, b * NU + u + 1, passed)
                    for lo in (0, T):
                        part = w[:, u % RING, :, lo:lo + P]
                        ins = pool.affine_select(out=part, in_=part, compare_op=ALU.is_ge, fill=0.0, base=0,
                                                 pattern=[[0, BR], [1, P]], channel_multiplier=-1)
                    ins.then_inc(masked, 1)

        @block.vector
        def _(dve):
            dve.wait_ge(loaded, 16 * len(loads))
            pre = Steps(dve, consts)
            own = s.sem("own_setup")
            step = Steps(dve, own)
            step.did(dve.memset(ln_quarter[:], math.log(0.25)))
            step.did(dve.memset(v1[:, :, :, DH:DH + 1], 1.0))
            step.link(dve.tensor_scalar(sinks[:], sinks[:], SILU_SCALE, None, ALU.mult))
            step.did(dve.tensor_scalar(sinks_eps[:], sinks[:], 1e-6 * SILU_SCALE, None, ALU.add))
            step.did(dve.tensor_tensor(vnull[:], vnull[:], sinks[:].unsqueeze(2).to_broadcast([P, BR * NH, DH]), ALU.mult))
            step.link(dve.tensor_tensor(bo[:, 0:2, :], bo[:, 0:2, :], bo[:, 2:4, :], ALU.add))
            step.link(dve.tensor_tensor(bo[:, 0, :], bo[:, 0, :], bo[:, 1, :], ALU.add))
            pre.did(dve.tensor_scalar(bo[:, 0, :], bo[:, 0, :], 1.0 / BR, None, ALU.mult))
            dve.wait_ge(consts, 1)
            with dve.Fori(0, B) as b:
                per = 16
                step = Steps(dve, own_dve, b * per, per)
                step.wait()
                dve.wait_ge(kheads_ready, b * CC)
                added = {}

                def rotate(n, i, bias, out):
                    ps = bank[n % 6].rearrange("p (v t) -> p v t", v=2)
                    r = (rot_a, rot_b)[n % 2]
                    if n - 2 in added:
                        dve.wait_ge(own_dve, b * per + added[n - 2])
                    for v in range(2):
                        ins = dve.scalar_tensor_tensor(r[:, v, :], ps[:, v, :], bias[:, v, i:i + 1], rope[:, v, :],
                                                       ALU.add, ALU.mult)
                    ins.then_inc(taken, 1)
                    dve.wait_ge(taken, b * NP + n + 1)
                    step.did(dve.tensor_tensor(out, r[:, 0, :], r[:, 1, :], ALU.add))
                    added[n] = step.n

                for n, (kind, i) in enumerate(order):
                    dve.wait_ge(projected, b * NP + n + 1)
                    if kind == "k":
                        rotate(n, i, bk, kT[:, i, :])
                        step.wait()
                        dve.tensor_tensor(ksq[:, i, :], kT[:, i, :], kT[:, i, :], ALU.mult).then_inc(ksq_ready, 1)
                    elif kind == "v":
                        for t in range(TT):
                            ins = dve.tensor_tensor(v1[:, t, :, 0:DH],
                                                    bank[n % 6][:, t * D:(t + 1) * D].rearrange("p (h d) -> p h d", d=DH),
                                                    bv[:].rearrange("p (h d) -> p h d", d=DH), ALU.add)
                        ins.then_inc(taken, 1)
                    elif kind == "n":
                        dve.tensor_scalar(ksq[:].rearrange("p g t -> p (g t)"), bank[n % 6], 1e-6, None, ALU.max)\
                           .then_inc(taken, 1)
                    else:
                        rotate(n, i, bq, qT[:, i % 2, i // 2, :])
                dve.wait_ge(knorm_ready, b + 1)
                step.link(dve.tensor_tensor(kT[:], kT[:], ksq[:], ALU.mult))
                for u in range(NH):
                    ins = dve.tensor_scalar(kT_head[:, u, :], kT[:, u // 8, :], head_mask[:, u % 8:u % 8 + 1], None,
                                            ALU.mult)
                    if u % 8 == 7:
                        ins.then_inc(kheads_ready, 1)

                def softplus_end(u):
                    dve.wait_ge(ln_done, b * NU + u + 1)
                    for r0, out in ((0, w[:, u % RING, :, 0:T]), (2, w[:, u % RING, :, T:T + P])):
                        z = (psS[:, u % 2, 0:2, :].rearrange("p h (r t) -> p (h r) t", r=2) if r0 == 0
                             else psS[:, u % 2, 2, :].rearrange("p (r t) -> p r t", r=BR))
                        ins = dve.tensor_tensor(out, z, out, ALU.max)
                    ins.then_inc(softplus_done, 1)

                def take_sums(u):
                    dve.wait_ge(summed, b * NU + u + 1)
                    dve.tensor_copy(ctx[:, :, u:BR * NH:NH, :],
                                    psO[:, u % 2, 0:TT * BR * 17].rearrange("p (t r d) -> p t r d", t=TT, r=BR))\
                       .then_inc(ctx_taken, 1)

                def threshold(u):
                    dve.wait_ge(silu_done, b * NU + u + 1)
                    for r in range(BR):
                        part = w[:, u % RING, r, :]
                        ins = dve.scalar_tensor_tensor(part, part, sinks[:, r * NH + u:r * NH + u + 1], part,
                                                       ALU.is_ge, ALU.mult)
                    ins.then_inc(weights_done, 1)

                for u in range(NU):
                    dve.wait_ge(scored, b * NU + u + 1)
                    dve.tensor_scalar(w[:, u % RING, :, 0:T], psS[:, u % 2, 0:2, :].rearrange("p h (r t) -> p (h r) t", r=2),
                                      CAP, None, ALU.min)
                    dve.tensor_scalar(w[:, u % RING, :, T:T + P], psS[:, u % 2, 2, :].rearrange("p (r t) -> p r t", r=BR),
                                      CAP, None, ALU.min).then_inc(clamped, 1)
                    if u >= 1:
                        softplus_end(u - 1)
                    if u >= GROUP:
                        threshold(u - GROUP)
                    if u > GROUP:
                        take_sums(u - GROUP - 1)
                softplus_end(NU - 1)
                for u in range(NU - GROUP - 1, NU):
                    if u >= NU - GROUP:
                        threshold(u)
                    take_sums(u)
                dve.wait_ge(ctx_taken, b * NU + NU)
                step.link(dve.tensor_tensor(total[:], ctx[:, :, :, DH],
                                            sinks_eps[:].unsqueeze(1).to_broadcast([P, TT, BR * NH]), ALU.add))
                step.did(dve.reciprocal(total[:], total[:]))
                for t in range(TT):
                    step.did(dve.tensor_tensor(ctxn[:, t], ctx[:, t, :, 0:DH], vnull[:], ALU.add))
                step.wait()
                for t in range(TT):
                    ins = dve.tensor_tensor(ctxn[:, t], ctxn[:, t],
                                            total[:, t, :].unsqueeze(2).to_broadcast([P, BR * NH, DH]), ALU.mult)
                ins.then_inc(ctx_ready, 1)
                x_b = x_all[:, bass.ds(b * TT, TT), :]
                step.did(dve.tensor_tensor(x_b, x_b, bo[:, 0:1, :].to_broadcast([P, TT, D]), ALU.add))
                dve.wait_ge(out_ready, b + 1)
                step.wait()
                dve.scalar_tensor_tensor(x_b, bank[4].rearrange("p (t d) -> p t d", t=TT), 1.0 / BR, x_b,
                                         ALU.mult, ALU.add).then_inc(out_taken, 1)
                step.end()


FOCUS_EPS = 1e-6
XH = 16
HEADS_IN_CHUNK = P // (D // XH)


def linear_attention(nc, norm, x_all, xnT_all, ident, psum, a):
    with ExitStack() as stack:
        s = Scope(nc, stack, "x0")
        wq, wk, wv = (s.sb(n, [P, CC, D]) for n in ("wq", "wk", "wv"))
        bq, bk, bv = (s.sb(n, [P, D]) for n in ("bq", "bk", "bv"))
        inv_scale = s.sb("inv_scale", [P, D])
        scale_e = s.sb("scale_e", [P, D])
        same_head = s.sb("same_head", [P, P])
        head_mask = s.sb("head_mask", [P, HEADS_IN_CHUNK])
        xnT, ctxT = s.sb("xnT", [P, CC, T]), s.sb("ctxT", [P, CC, T])
        f, f2, f3 = (s.sb(n, [P, 2 * TT, D]) for n in ("f", "f2", "f3"))
        norm2, norm6, factor = (s.sb(n, [P, 2 * TT]) for n in ("norm2", "norm6", "factor"))
        v1 = s.sb("v1", [P, TT, CC, P + 1])
        KVW = P + HEADS_IN_CHUNK
        kv = s.sb("kv", [P, CC, KVW])
        qT = s.sb("qT", [P, CC, T])
        z = s.sb("z", [P, TT, CC, HEADS_IN_CHUNK])
        o = s.sb("o", [P, TT, D])
        loaded, x_here, ctx_here = s.sem("loaded"), s.sem("x_here"), s.sem("ctx_here")
        consts, own_dve, own_setup = s.sem("consts"), s.sem("own_dve"), s.sem("own_setup")
        projected, taken, features_raw = s.sem("projected"), s.sem("taken"), s.sem("features_raw")
        squared, cubed, sixth, ratio_ready, factor_ready = (
            s.sem(n) for n in ("squared", "cubed", "sixth", "ratio_ready", "factor_ready"))
        features, kv_summed, kv_ready = s.sem("features"), s.sem("kv_summed"), s.sem("kv_ready")
        q_turned, qT_ready, out_ready, out_taken = (s.sem(n) for n in ("q_turned", "qT_ready", "out_ready", "out_taken"))
        own_act = s.sem("own_act")
        loads = [(wq[:], chunked(a["wq"])), (wk[:], chunked(a["wk"])), (wv[:], chunked(a["wv"])),
                 (bq[:], over_partitions(a["bq"], D)), (bk[:], over_partitions(a["bk"], D)),
                 (bv[:], over_partitions(a["bv"], D)), (inv_scale[:], over_partitions(a["scale"], D)),
                 (same_head[:], a["same_head"]), (head_mask[:], a["head_mask"])]
        normalise(nc, norm, x_all, xnT_all, ident, psum, loads, loaded)
        block = stack.enter_context(nc.Block())

        @block.sync
        def _(sp):
            with sp.Fori(0, B) as b:
                sp.wait_ge(projected, b * 3)
                sp.dma_start(xnT[:], xnT_all[:, bass.ds(b, 1), :, :]).then_inc(x_here, 16)
                sp.dma_start(ctxT[:], a["ctxT"][bass.ds(b * D, D), :].rearrange("(k p) n -> p k n", p=P))\
                  .then_inc(ctx_here, 16)

        @block.tensor
        def _(pe):
            pe.wait_ge(loaded, 16 * len(loads))
            with pe.Fori(0, B) as b:
                pe.wait_ge(x_here, b * 16 + 16)
                pe.wait_ge(ctx_here, b * 16 + 16)
                pe.wait_ge(out_taken, b)
                for n, (src, weights) in enumerate(((ctxT, wk), (xnT, wq), (ctxT, wv))):
                    for t in range(TT):
                        for c in range(CC):
                            ins = pe.matmul(psum[:, n, t * D:(t + 1) * D], src[:, c, t * P:(t + 1) * P], weights[:, c, :],
                                            start=(c == 0), stop=(c == CC - 1))
                    ins.then_inc(projected, 1)
                pe.wait_ge(features, b + 1)
                for c in range(CC):
                    for t in range(TT):
                        ins = pe.matmul(psum[:, 3, c * (P + 1):(c + 1) * (P + 1)], f3[:, TT + t, c * P:(c + 1) * P],
                                        v1[:, t, c, :], start=(t == 0), stop=(t == TT - 1))
                ins.then_inc(kv_summed, 1)
                for c in range(CC):
                    for t in range(TT):
                        ins = pe.transpose(psum[:, 4, c * T + t * P:c * T + (t + 1) * P], f3[:, t, c * P:(c + 1) * P],
                                           ident[:])
                ins.then_inc(q_turned, 1)
                pe.wait_ge(kv_ready, b + 1)
                pe.wait_ge(qT_ready, b + 1)
                for t in range(TT):
                    for c in range(CC):
                        ins = pe.matmul(psum[:, 5 + t, c * KVW:(c + 1) * KVW], qT[:, c, t * P:(t + 1) * P], kv[:, c, :],
                                        start=True, stop=True)
                ins.then_inc(out_ready, 1)

        @block.scalar
        def _(act):
            act.wait_ge(consts, 1)
            step = Steps(act, own_act)
            act.preload_act_table_set("natural_log_exp_and_others")
            step.link(act.activation(scale_e[:], scale_e[:], ACT.Exp))
            step.link(act.activation(scale_e[:], scale_e[:], ACT.Ln, bias=1.0))
            act.preload_act_table_set("sqrt_and_others")
            with act.Fori(0, B) as b:
                act.wait_ge(features_raw, b + 1)
                for i in range(2 * TT):
                    ins = act.activation(f2[:, i, :], f[:, i, :], ACT.Square, accum_out=norm2[:, i:i + 1])
                ins.then_inc(squared, 1)
                act.wait_ge(cubed, b + 1)
                act.wait_ge(squared, b + 1)
                for i in range(2 * TT):
                    ins = act.activation(f2[:, i, :], f3[:, i, :], ACT.Square, accum_out=norm6[:, i:i + 1])
                ins.then_inc(sixth, 1)
                act.wait_ge(ratio_ready, b + 1)
                act.activation(factor[:], factor[:], ACT.Sqrt).then_inc(factor_ready, 1)
                act.wait_ge(q_turned, b + 1)
                act.activation(qT[:], psum[:, 4, :].rearrange("p (c t) -> p c t", c=CC), ACT.Copy).then_inc(qT_ready, 1)

        @block.vector
        def _(dve):
            dve.wait_ge(loaded, 16 * len(loads))
            step = Steps(dve, own_setup)
            step.did(dve.memset(v1[:, :, :, P:P + 1], 1.0))
            dve.tensor_scalar(scale_e[:], inv_scale[:], CAP, None, ALU.min).then_inc(consts, 1)
            dve.wait_ge(own_act, 2)
            step.link(dve.tensor_tensor(inv_scale[:], inv_scale[:], scale_e[:], ALU.max))
            step.link(dve.reciprocal(inv_scale[:], inv_scale[:]))
            with dve.Fori(0, B) as b:
                step = Steps(dve, own_dve, b * 9, 9)
                step.wait()
                dve.wait_ge(out_taken, b)
                dve.wait_ge(projected, b * 3 + 1)
                bias = lambda v: v[:].unsqueeze(1).to_broadcast([P, TT, D])
                tile = lambda n: psum[:, n, :].rearrange("p (t d) -> p t d", t=TT)
                step.did(dve.tensor_tensor(f[:, TT:2 * TT, :], tile(0), bias(bk), ALU.add))
                dve.wait_ge(projected, b * 3 + 2)
                step.link(dve.tensor_tensor(f[:, 0:TT, :], tile(1), bias(bq), ALU.add))
                step.link(dve.tensor_scalar(f[:], f[:], 0.0, FOCUS_EPS, ALU.max, ALU.add))
                dve.tensor_tensor(f[:], f[:], inv_scale[:].unsqueeze(1).to_broadcast([P, 2 * TT, D]), ALU.mult)\
                   .then_inc(features_raw, 1)
                dve.wait_ge(projected, b * 3 + 3)
                for t in range(TT):
                    step.did(dve.tensor_tensor(v1[:, t, :, 0:P], psum[:, 2, t * D:(t + 1) * D].rearrange("p (c d) -> p c d", c=CC),
                                               bv[:].rearrange("p (c d) -> p c d", c=CC), ALU.add))
                dve.wait_ge(squared, b + 1)
                dve.wait_ge(features_raw, b + 1)
                dve.tensor_tensor(f3[:], f2[:], f[:], ALU.mult).then_inc(cubed, 1)
                dve.wait_ge(sixth, b + 1)
                step.link(dve.reciprocal(factor[:], norm6[:]))
                dve.tensor_tensor(factor[:], factor[:], norm2[:], ALU.mult).then_inc(ratio_ready, 1)
                dve.wait_ge(factor_ready, b + 1)
                dve.wait_ge(cubed, b + 1)
                for i in range(2 * TT):
                    ins = dve.tensor_scalar(f3[:, i, :], f3[:, i, :], factor[:, i:i + 1], None, ALU.mult)
                ins.then_inc(features, 1)
                dve.wait_ge(kv_summed, b + 1)
                for c in range(CC):
                    lo = c * (P + 1)
                    dve.tensor_tensor(kv[:, c, 0:P], psum[:, 3, lo:lo + P], same_head[:], ALU.mult)
                    ins = dve.tensor_tensor(kv[:, c, P:KVW], psum[:, 3, lo + P:lo + P + 1].to_broadcast([P, HEADS_IN_CHUNK]),
                                            head_mask[:], ALU.mult)
                ins.then_inc(kv_ready, 1)
                dve.wait_ge(out_ready, b + 1)
                outs = psum[:, 5:5 + TT, 0:CC * KVW].rearrange("p t (c n) -> p t c n", c=CC)
                step.link(dve.tensor_scalar(z[:], outs[:, :, :, P:KVW], FOCUS_EPS, None, ALU.add))
                step.link(dve.reciprocal(z[:], z[:]))
                for t in range(TT):
                    ins = dve.tensor_tensor(o[:, t, :].rearrange("p (c h d) -> p c h d", c=CC, h=HEADS_IN_CHUNK),
                                            outs[:, t, :, 0:P].rearrange("p c (h d) -> p c h d", h=HEADS_IN_CHUNK),
                                            z[:, t].unsqueeze(3).to_broadcast([P, CC, HEADS_IN_CHUNK, P // HEADS_IN_CHUNK]),
                                            ALU.mult)
                step.link(ins)
                x_b = x_all[:, bass.ds(b * TT, TT), :]
                dve.tensor_tensor(x_b, x_b, o[:], ALU.add).then_inc(out_taken, 1)
                step.end()


def scores_softmax_value_order(units):
    for u in range(units + 2):
        if u < units:
            yield "scores", u
        if 1 <= u <= units:
            yield "turn", u - 1
        if u >= 2:
            yield "values", u - 2


def top2(dve, step, v, mask, work, red, rev, groups):
    wide = lambda r: r.unsqueeze(2).to_broadcast([P, groups, 8])
    eq, rest = work
    for rank in range(2):
        src = v if rank == 0 else rest
        step.link(dve.tensor_reduce(red, src, AX.X, ALU.max))
        step.link(dve.tensor_tensor(eq, src, wide(red), ALU.is_equal))
        step.link(dve.tensor_tensor(eq, eq, rev.unsqueeze(1).to_broadcast([P, groups, 8]), ALU.mult))
        step.link(dve.tensor_reduce(red, eq, AX.X, ALU.max))
        step.link(dve.tensor_tensor(eq, eq, wide(red), ALU.is_equal))
        if rank == 0:
            step.did(dve.tensor_copy(mask, eq))
            step.link(dve.scalar_tensor_tensor(rest, eq, -3e38, v, ALU.mult, ALU.add))
        else:
            step.link(dve.tensor_tensor(mask, mask, eq, ALU.add))


TOP2_STEPS = 13


SH, SDH, SE = 16, 64, 8
QK_GROUPS = SH * SDH // P // 2
SG = SH * SE


def switch_attention(nc, norm, x_all, xnT_all, ident, psum, a):
    with ExitStack() as stack:
        s = Scope(nc, stack, "f0")
        loaded = s.sem("loaded")
        pv_all = s.sb("pv_all", [P, TILES, SE * SDH])
        mix_all = s.sb("mix_all", [P, TILES, SG])
        pick_all = s.sb("pick_all", [P, TILES, SG])
        u_all = s.sb("u_all", [P, TILES, SE * SDH])
        wo = s.sb("wo", [P, SE * SDH // P, D])
        xnT = s.sb("xnT", [P, CC, T])

        with ExitStack() as stage:
            g = Scope(nc, stage, "f0g")
            wg, wv = g.sb("wg", [P, CC, 2 * SG]), g.sb("wv", [P, CC, SE * SDH])
            rev = g.sb("rev", [P, 8])
            NG = TT * 2 * SH
            gate, mask, eq, rest = (g.sb(n, [P, NG, 8]) for n in ("gate", "mask", "eq", "rest"))
            sig = g.sb("sig", [P, TT, SG])
            red = g.sb("red", [P, NG])
            x_here, projected, gates_taken, values_taken, sig_ready, own = (
                g.sem(n) for n in ("x_here", "projected", "gates_taken", "values_taken", "sig_ready", "own"))
            chosen = g.sem("chosen")
            loads = [(wg[:], chunked(a["wg"])), (wv[:], chunked(a["wv"])), (rev[:], over_partitions(a["rev"], 8)),
                     (wo[:], chunked(a["wo"]))]
            normalise(nc, norm, x_all, xnT_all, ident, psum, loads, loaded)
            block = stage.enter_context(nc.Block())

            @block.sync
            def _(sp):
                with sp.Fori(0, B) as b:
                    sp.wait_ge(projected, b * 3)
                    sp.dma_start(xnT[:], xnT_all[:, bass.ds(b, 1), :, :]).then_inc(x_here, 16)

            @block.tensor
            def _(pe):
                pe.wait_ge(loaded, 16 * len(loads))
                with pe.Fori(0, B) as b:
                    pe.wait_ge(x_here, b * 16 + 16)
                    pe.wait_ge(gates_taken, b)
                    for t in range(TT):
                        for c in range(CC):
                            ins = pe.matmul(psum[:, 0, t * D:(t + 1) * D], xnT[:, c, t * P:(t + 1) * P], wg[:, c, :],
                                            start=(c == 0), stop=(c == CC - 1))
                    ins.then_inc(projected, 1)
                    pe.wait_ge(values_taken, b)
                    for t in range(TT):
                        for c in range(CC):
                            ins = pe.matmul(psum[:, 1 + t, :], xnT[:, c, t * P:(t + 1) * P], wv[:, c, :],
                                            start=(c == 0), stop=(c == CC - 1))
                        ins.then_inc(projected, 1)

            @block.scalar
            def _(act):
                with act.Fori(0, B) as b:
                    act.wait_ge(projected, b * 3 + 1)
                    act.wait_ge(chosen, b)
                    act.activation(sig[:], psum[:, 0, :].rearrange("p (t n) -> p t n", t=TT)[:, :, 0:SG], ACT.Sigmoid)\
                       .then_inc(sig_ready, 1)
                    act.wait_ge(projected, b * 3 + 3)
                    act.activation(pv_all[:, bass.ds(b * TT, TT), :], psum[:, 1:1 + TT, :], ACT.Copy)\
                       .then_inc(values_taken, 1)

            @block.vector
            def _(dve):
                dve.wait_ge(loaded, 16 * len(loads))
                with dve.Fori(0, B) as b:
                    step = Steps(dve, own, b * TOP2_STEPS, TOP2_STEPS)
                    dve.wait_ge(chosen, b)
                    step.wait()
                    dve.wait_ge(projected, b * 3 + 1)
                    dve.wait_ge(sig_ready, b + 1)
                    dve.tensor_copy(gate[:].rearrange("p g e -> p (g e)"), psum[:, 0, :]).then_inc(gates_taken, 1)
                    dve.wait_ge(gates_taken, b + 1)
                    top2(dve, step, gate[:], mask[:], (eq[:], rest[:]), red[:], rev[:], NG)
                    m = mask[:].rearrange("p (t n) e -> p t (n e)", t=TT)
                    dve.tensor_tensor(mix_all[:, bass.ds(b * TT, TT), :], sig[:], m[:, :, 0:SG], ALU.mult)
                    dve.tensor_copy(pick_all[:, bass.ds(b * TT, TT), :], m[:, :, SG:2 * SG]).then_inc(chosen, 1)
                    step.end()

        with ExitStack() as stage:
            h = Scope(nc, stage, "f0h")
            wq, wk = h.sb("wq", [P, CC, SH * SDH]), h.sb("wk", [P, CC, SH * SDH])
            qT, kT = h.sb("qT", [P, 2 * QK_GROUPS, T]), h.sb("kT", [P, 2 * QK_GROUPS, T])
            pv = h.sb("pv", [P, TT, SE, SDH])
            mix, pick = h.sb("mix", [P, TT, SH, SE]), h.sb("pick", [P, TT, SH, SE])
            HALF = 4
            prod = h.sb("prod", [P, HALF, SE, SDH])
            v = [h.sb(f"v{i}", [P, TT, SH, SDH]) for i in range(2)]
            weights = [h.sb(f"weights{i}", [P, TT, T]) for i in range(2)]
            turned_w = [h.sb(f"turned_w{i}", [P, TT, T]) for i in range(2)]
            negmax, sums = h.sb("negmax", [P, SH, TT]), h.sb("sums", [P, SH, TT])
            pick_s = h.sb("pick_s", [P, 2, TT, SE])
            picked = h.sb("picked", [P, 2, TT, SE, SDH])
            u = h.sb("u", [P, TT, SE, SDH])
            w_loaded, x_here, qk_ready, qk_taken = (h.sem(n) for n in ("w_loaded", "x_here", "qk_ready", "qk_taken"))
            mix_here = h.sem("mix_here")
            v_ready, summed = h.sems("v_ready", 2), h.sems("summed", 2)
            scored, max_ready, exp_done, turned, turned_taken, out_taken = (
                h.sem(n) for n in ("scored", "max_ready", "exp_done", "turned", "turned_taken", "out_taken"))
            own_pool, own_dve, passed, u_ready = (h.sem(n) for n in ("own_pool", "own_dve", "passed", "u_ready"))
            block = stage.enter_context(nc.Block())
            PAIRS = B // 2
            QK_BANKS = (0, 1, 2, 3, 4)
            NQK = 2 * QK_GROUPS

            @block.sync
            def _(sp):
                sp.dma_start(wq[:], chunked(a["wq"])).then_inc(w_loaded, 16)
                sp.dma_start(wk[:], chunked(a["wk"])).then_inc(w_loaded, 16)
                with sp.Fori(0, PAIRS) as pair:
                    for i in range(2):
                        b = pair * 2 + i
                        sp.wait_ge(v_ready[1 - i], pair + i)
                        sp.dma_start(pv[:].rearrange("p t e d -> p t (e d)"), pv_all[:, bass.ds(b * TT, TT), :])\
                          .then_inc(mix_here, 16)
                        sp.dma_start(mix[:].rearrange("p t h e -> p t (h e)"), mix_all[:, bass.ds(b * TT, TT), :])\
                          .then_inc(mix_here, 16)
                        sp.wait_ge(qk_ready, b * NQK)
                        sp.dma_start(xnT[:], xnT_all[:, bass.ds(b, 1), :, :]).then_inc(x_here, 16)

            @block.gpsimd
            def _(pool):
                per = TT * (SH // HALF) * 4 - 1
                with pool.Fori(0, PAIRS) as pair:
                    step = Steps(pool, own_pool, pair * 2 * per, 2 * per)
                    for i in range(2):
                        alone(pool, mix_here, pair * 64 + 32 * i + 32, passed)
                        alone(pool, summed[i], pair * SH, passed)
                        alone(pool, v_ready[1 - i], pair + i, passed)
                        for t in range(TT):
                            for h0 in range(0, SH, HALF):
                                alone(pool, own_pool, step.base + step.n, passed)
                                step.did(pool.tensor_tensor(
                                    prod[:], pv[:, t].unsqueeze(1).to_broadcast([P, HALF, SE, SDH]),
                                    mix[:, t, h0:h0 + HALF, :].unsqueeze(3).to_broadcast([P, HALF, SE, SDH]), ALU.mult))
                                for half in (4, 2, 1):
                                    alone(pool, own_pool, step.base + step.n, passed)
                                    out = (prod[:, :, 0:half, :] if half > 1
                                           else v[i][:, t, h0:h0 + HALF, :].unsqueeze(2))
                                    ins = pool.tensor_tensor(out, prod[:, :, 0:half, :], prod[:, :, half:2 * half, :],
                                                             ALU.add)
                                    if half > 1 or t < TT - 1 or h0 + HALF < SH:
                                        step.did(ins)
                        ins.then_inc(v_ready[i], 1)
                    step.end()

            @block.tensor
            def _(pe):
                pe.wait_ge(w_loaded, 32)
                with pe.Fori(0, PAIRS) as pair:
                    for i in range(2):
                        S0 = pair * 2 * SH + i * SH
                        Q0 = pair * 2 * NQK + i * NQK
                        pe.wait_ge(x_here, pair * 32 + 16 * i + 16)
                        pe.wait_ge(out_taken, S0)
                        for n in range(NQK):
                            w, m = (wq, wk)[n % 2], n // 2
                            bank = psum[:, QK_BANKS[n % 5], :]
                            if n >= 5:
                                pe.wait_ge(qk_taken, Q0 + n - 4)
                            for j in range(2):
                                lo = (2 * m + j) * P
                                for c in range(CC):
                                    ins = pe.matmul(bank[:, j * T:(j + 1) * T], w[:, c, lo:lo + P], xnT[:, c, :],
                                                    start=(c == 0), stop=(c == CC - 1))
                            ins.then_inc(qk_ready, 1)
                        for what, k in scores_softmax_value_order(SH):
                            r0 = SDH * (k % 2)
                            if what == "scores":
                                if k == 0:
                                    pe.wait_ge(qk_taken, Q0 + NQK)
                                if k >= 2:
                                    pe.wait_ge(exp_done, S0 + k - 1)
                                for t in range(TT):
                                    ins = pe.matmul(psum[:, 6 + k % 2, t * T:(t + 1) * T],
                                                    qT[r0:r0 + SDH, k // 2, t * P:(t + 1) * P], kT[r0:r0 + SDH, k // 2, :],
                                                    start=True, stop=True)
                                ins.then_inc(scored, 1)
                            elif what == "turn":
                                pe.wait_ge(exp_done, S0 + k + 1)
                                if k >= 2:
                                    pe.wait_ge(turned_taken, S0 + k - 1)
                                for j in range(TT):
                                    for t in range(TT):
                                        lo = j * T + t * P
                                        ins = pe.transpose(psum[:, 4 + k % 2, lo:lo + P],
                                                           weights[k % 2][:, t, j * P:(j + 1) * P], ident[:])
                                ins.then_inc(turned, 1)
                            else:
                                if k == 0:
                                    pe.wait_ge(v_ready[i], pair + 1)
                                pe.wait_ge(turned_taken, S0 + k + 1)
                                if k >= 4:
                                    pe.wait_ge(out_taken, S0 + k - 3)
                                for t in range(TT):
                                    for j in range(TT):
                                        ins = pe.matmul(psum[:, k % 4, t * SDH:(t + 1) * SDH],
                                                        turned_w[k % 2][:, j, t * P:(t + 1) * P], v[i][:, j, k, :],
                                                        start=(j == 0), stop=(j == TT - 1))
                                ins.then_inc(summed[i], 1)

            @block.scalar
            def _(act):
                with act.Fori(0, PAIRS) as pair:
                  for i in range(2):
                    b = pair * 2 + i
                    for n in range(NQK):
                        act.wait_ge(qk_ready, b * NQK + n + 1)
                        dst, m = (qT, kT)[n % 2], n // 2
                        act.activation(dst[:, 2 * m:2 * m + 2, :], psum[:, QK_BANKS[n % 5], :].rearrange("p (j t) -> p j t", j=2),
                                       ACT.Copy, scale=(SDH ** -0.5 if n % 2 == 0 else 1.0)).then_inc(qk_taken, 1)

                    def exps(k):
                        act.wait_ge(max_ready, b * SH + k + 1)
                        if k >= 2:
                            act.wait_ge(turned, b * SH + k - 1)
                        for t in range(TT):
                            ins = act.activation(weights[k % 2][:, t, :], psum[:, 6 + k % 2, t * T:(t + 1) * T], ACT.Exp,
                                                 bias=negmax[:, k, t:t + 1], accum_out=sums[:, k, t:t + 1])
                        ins.then_inc(exp_done, 1)

                    def take_turned(k):
                        act.wait_ge(turned, b * SH + k + 1)
                        if k >= 2:
                            act.wait_ge(summed[i], pair * SH + k - 1)
                        act.activation(turned_w[k % 2][:], psum[:, 4 + k % 2, :].rearrange("p (j t) -> p j t", j=TT),
                                       ACT.Copy).then_inc(turned_taken, 1)

                    for k in range(SH):
                        exps(k)
                        if k >= 1:
                            take_turned(k - 1)
                    take_turned(SH - 1)

            @block.vector
            def _(dve):
                per = 3 * SH
                with dve.Fori(0, PAIRS) as pair:
                    step = Steps(dve, own_dve, pair * 2 * per, 2 * per)
                    for i in range(2):
                        b = pair * 2 + i
                        S0 = b * SH
                        step.wait()
                        dve.wait_ge(u_ready, b)
                        step.link(dve.tensor_copy(pick[:].rearrange("p t h e -> p t (h e)"),
                                                  pick_all[:, bass.ds(b * TT, TT), :]))

                        def row_max(k):
                            dve.wait_ge(scored, S0 + k + 1)
                            dve.tensor_reduce(negmax[:, k, :], psum[:, 6 + k % 2, :].rearrange("p (t j) -> p t j", t=TT),
                                              AX.X, ALU.max, negate=True).then_inc(max_ready, 1)

                        def to_experts(k):
                            dve.wait_ge(exp_done, S0 + k + 1)
                            step.link(dve.reciprocal(sums[:, k, :], sums[:, k, :]))
                            step.link(dve.tensor_tensor(pick_s[:, k % 2], pick[:, :, k, :],
                                                        sums[:, k, :].unsqueeze(2).to_broadcast([P, TT, SE]), ALU.mult))
                            dve.wait_ge(summed[i], pair * SH + k + 1)
                            for t in range(TT):
                                ins = dve.tensor_tensor(
                                    u[:, t] if k == 0 else picked[:, k % 2, t],
                                    psum[:, k % 4, t * SDH:(t + 1) * SDH].unsqueeze(1).to_broadcast([P, SE, SDH]),
                                    pick_s[:, k % 2, t].unsqueeze(2).to_broadcast([P, SE, SDH]), ALU.mult)
                            ins.then_inc(out_taken, 1)
                            dve.wait_ge(out_taken, S0 + k + 1)
                            if k:
                                step.did(dve.tensor_tensor(u[:], u[:], picked[:, k % 2], ALU.add))

                        for k in range(SH):
                            row_max(k)
                            if k >= 2:
                                to_experts(k - 2)
                        to_experts(SH - 2)
                        to_experts(SH - 1)
                        step.wait()
                        dve.tensor_copy(u_all[:, bass.ds(b * TT, TT), :], u[:].rearrange("p t e d -> p t (e d)"))\
                           .then_inc(u_ready, 1)
                    step.end()

        with ExitStack() as stage:
            o = Scope(nc, stage, "f0o")
            KO = SE * SDH // P
            u_b = o.sb("u", [P, TT, SE * SDH])
            uT = o.sb("uT", [P, TT, KO, P])
            u_here, turned, taken, out_ready, out_taken = (
                o.sem(n) for n in ("u_here", "turned", "taken", "out_ready", "out_taken"))
            block = stage.enter_context(nc.Block())

            @block.sync
            def _(sp):
                with sp.Fori(0, B) as b:
                    sp.wait_ge(turned, b * TT)
                    sp.dma_start(u_b[:], u_all[:, bass.ds(b * TT, TT), :]).then_inc(u_here, 16)

            @block.tensor
            def _(pe):
                with pe.Fori(0, B) as b:
                    pe.wait_ge(u_here, b * 16 + 16)
                    pe.wait_ge(taken, b * TT)
                    for t in range(TT):
                        for k in range(KO):
                            ins = pe.transpose(psum[:, t, k * P:(k + 1) * P], u_b[:, t, k * P:(k + 1) * P], ident[:])
                        ins.then_inc(turned, 1)
                    pe.wait_ge(taken, b * TT + TT)
                    pe.wait_ge(out_taken, b)
                    for t in range(TT):
                        for k in range(KO):
                            ins = pe.matmul(psum[:, 2, t * D:(t + 1) * D], uT[:, t, k, :], wo[:, k, :],
                                            start=(k == 0), stop=(k == KO - 1))
                    ins.then_inc(out_ready, 1)

            @block.scalar
            def _(act):
                with act.Fori(0, B) as b:
                    act.wait_ge(out_ready, b)
                    for t in range(TT):
                        act.wait_ge(turned, b * TT + t + 1)
                        act.activation(uT[:, t], psum[:, t, :].rearrange("p (k n) -> p k n", k=KO), ACT.Copy)\
                           .then_inc(taken, 1)

            @block.vector
            def _(dve):
                with dve.Fori(0, B) as b:
                    dve.wait_ge(out_ready, b + 1)
                    x_b = x_all[:, bass.ds(b * TT, TT), :]
                    dve.tensor_tensor(x_b, psum[:, 2, :].rearrange("p (t d) -> p t d", t=TT), x_b, ALU.add)\
                       .then_inc(out_taken, 1)


def turn_and_project(pe, psum, ident, o, oT, w, turned, turned_taken, out_ready, b, chunks):
    for t in range(TT):
        for g in range(chunks // 4):
            for i in range(4):
                lo = (4 * g + i) * P
                ins = pe.transpose(psum[:, 2 * t + g, i * P:(i + 1) * P], o[:, t, lo:lo + P], ident[:])
            ins.then_inc(turned, 1)
    pe.wait_ge(turned_taken, b * 4 + 4)
    for t in range(TT):
        for k in range(chunks):
            ins = pe.matmul(psum[:, 4, t * D:(t + 1) * D], oT[:, t, k, :], w[:, k, :], start=(k == 0),
                            stop=(k == chunks - 1))
    ins.then_inc(out_ready, 1)


def take_turned_output(act, psum, oT, turned, turned_taken, b):
    for n in range(4):
        act.wait_ge(turned, b * 4 + n + 1)
        act.activation(oT[:, n // 2, 4 * (n % 2):4 * (n % 2) + 4, :], psum[:, n, :].rearrange("p (k n) -> p k n", n=P),
                       ACT.Copy).then_inc(turned_taken, 1)


AH, AD = 8, 128
KEYS, CTX = 1024, 192
KB = KEYS // P
SHARPEN = 1.5


def attention1(nc, norm, x_all, xnT_all, ident, psum, a):
    with ExitStack() as stack:
        s = Scope(nc, stack, "a1")
        wq, wo = s.sb("wq", [P, CC, AH * AD]), s.sb("wo", [P, AH, D])
        wk, wv = s.sb("wk", [P, 2, AH * AD]), s.sb("wv", [P, 2, AH * AD])
        bo = s.sb("bo", [P, D])
        ctxT = s.sb("ctxT", [P, 2, KEYS])
        kT, v = s.sb("kT", [P, AH, KEYS]), s.sb("v", [P, KB, AH * AD])
        xnT, qT = s.sb("xnT", [P, CC, T]), s.sb("qT", [P, AH, T])
        weights = [s.sb(f"weights{i}", [P, KEYS]) for i in range(2)]
        turned_w = [s.sb(f"turned_w{i}", [P, KEYS]) for i in range(2)]
        U = AH * TT
        negmax, sums = s.sb("negmax", [P, U]), s.sb("sums", [P, U])
        o, oT = s.sb("o", [P, TT, AH * AD]), s.sb("oT", [P, TT, AH, P])
        loaded, x_here = s.sem("loaded"), s.sem("x_here")
        kv_ready, kv_act, kv_dve = s.sem("kv_ready"), s.sem("kv_act"), s.sem("kv_dve")
        q_ready, q_taken, scored, max_ready, exp_done, turned = (
            s.sem(n) for n in ("q_ready", "q_taken", "scored", "max_ready", "exp_done", "turned"))
        half_taken = s.sems("half_taken", 2)
        summed, head_taken, own = s.sem("summed"), s.sem("head_taken"), s.sem("own")
        o_turned, o_turned_taken, out_ready, out_taken = (
            s.sem(n) for n in ("o_turned", "o_turned_taken", "out_ready", "out_taken"))
        loads = []
        for dst, src in ((ctxT, a["ctxT"]), (wk, a["wk"]), (wv, a["wv"])):
            loads += [(dst[:, 0, :], src[0:P, :]), (dst[0:CTX - P, 1, :], src[P:CTX, :])]
        loads += [(wq[:], chunked(a["wq"])), (wo[:], chunked(a["wo"])), (bo[:], over_partitions(a["bo"], D))]
        normalise(nc, norm, x_all, xnT_all, ident, psum, loads, loaded)
        block = stack.enter_context(nc.Block())
        HALF = KEYS // 2
        parts = [("k", h, half) for h in range(AH) for half in range(2)] + \
                [("v", st, half) for st in range(KB) for half in range(2)]

        @block.sync
        def _(sp):
            with sp.Fori(0, B) as b:
                sp.wait_ge(q_ready, b * 4)
                sp.dma_start(xnT[:], xnT_all[:, bass.ds(b, 1), :, :]).then_inc(x_here, 16)

        @block.tensor
        def _(pe):
            pe.wait_ge(loaded, 16 * len(loads))
            for n, (kind, i, half) in enumerate(parts):
                if n >= 8:
                    pe.wait_ge((kv_act, kv_dve)[n % 2], (n - 8) // 2 + 1)
                for c, rows in enumerate((P, CTX - P)):
                    if kind == "k":
                        ins = pe.matmul(psum[:, n % 8, :], wk[0:rows, c, i * AD:(i + 1) * AD],
                                        ctxT[0:rows, c, half * HALF:(half + 1) * HALF], start=(c == 0), stop=(c == 1))
                    else:
                        ins = pe.matmul(psum[:, n % 8, :], ctxT[0:rows, c, i * P:(i + 1) * P],
                                        wv[0:rows, c, half * HALF:(half + 1) * HALF], start=(c == 0), stop=(c == 1))
                ins.then_inc(kv_ready, 1)
            pe.wait_ge(kv_act, len(parts) // 2)
            pe.wait_ge(kv_dve, len(parts) // 2)
            with pe.Fori(0, B) as b:
                S0 = b * U
                pe.wait_ge(x_here, b * 16 + 16)
                pe.wait_ge(out_taken, b)
                for m in range(AH // 2):
                    if m >= 2:
                        pe.wait_ge(q_taken, b * 4 + m - 1)
                    for j in range(2):
                        for c in range(CC):
                            lo = (2 * m + j) * AD
                            ins = pe.matmul(psum[:, 6 + m % 2, j * T:(j + 1) * T], wq[:, c, lo:lo + AD], xnT[:, c, :],
                                            start=(c == 0), stop=(c == CC - 1))
                    ins.then_inc(q_ready, 1)
                for what, k in scores_softmax_value_order(U):
                    h, t = k // TT, k % TT
                    if what == "scores":
                        if k == 0:
                            pe.wait_ge(q_taken, b * 4 + 4)
                        if k >= 2:
                            pe.wait_ge(exp_done, S0 + k - 1)
                        for half in range(2):
                            ins = pe.matmul(psum[:, 2 * (k % 2) + half, :], qT[:, h, t * P:(t + 1) * P],
                                            kT[:, h, half * HALF:(half + 1) * HALF], start=True, stop=True)
                        ins.then_inc(scored, 1)
                    elif what == "turn":
                        pe.wait_ge(exp_done, S0 + k + 1)
                        for half in range(2):
                            pe.wait_ge(half_taken[half], S0 + k)
                            for j in range(4):
                                lo = half * HALF + j * P
                                ins = pe.transpose(psum[:, 4 + half, j * P:(j + 1) * P], weights[k % 2][:, lo:lo + P],
                                                   ident[:])
                            ins.then_inc(turned, 1)
                    else:
                        for half in range(2):
                            pe.wait_ge(half_taken[half], S0 + k + 1)
                        if k >= 2:
                            pe.wait_ge(head_taken, S0 + k - 1)
                        for j in range(KB):
                            ins = pe.matmul(psum[:, 6 + k % 2, 0:AD], turned_w[k % 2][:, j * P:(j + 1) * P],
                                            v[:, j, h * AD:(h + 1) * AD], start=(j == 0), stop=(j == KB - 1))
                        ins.then_inc(summed, 1)
                pe.wait_ge(head_taken, S0 + U)
                turn_and_project(pe, psum, ident, o, oT, wo, o_turned, o_turned_taken, out_ready, b, AH)

        def take_context(eng, n, copy, done):
            kind, i, half = parts[n]
            dst = kT[:, i, half * HALF:(half + 1) * HALF] if kind == "k" else v[:, i, half * HALF:(half + 1) * HALF]
            eng.wait_ge(kv_ready, n + 1)
            copy(dst, psum[:, n % 8, :]).then_inc(done, 1)

        @block.scalar
        def _(act):
            for n in range(0, len(parts), 2):
                take_context(act, n, lambda out, in_: act.activation(out, in_, ACT.Copy), kv_act)
            with act.Fori(0, B) as b:
                S0 = b * U
                for m in range(AH // 2):
                    act.wait_ge(q_ready, b * 4 + m + 1)
                    act.activation(qT[:, 2 * m:2 * m + 2, :], psum[:, 6 + m % 2, :].rearrange("p (j t) -> p j t", j=2),
                                   ACT.Copy, scale=SHARPEN * AD ** -0.5).then_inc(q_taken, 1)

                def exps(k):
                    act.wait_ge(max_ready, S0 + k + 1)
                    if k >= 2:
                        act.wait_ge(turned, 2 * (S0 + k - 1))
                    act.activation(weights[k % 2][:], psum[:, 2 * (k % 2):2 * (k % 2) + 2, :].rearrange("p a n -> p (a n)"),
                                   ACT.Exp, bias=negmax[:, k:k + 1], accum_out=sums[:, k:k + 1]).then_inc(exp_done, 1)

                def take_half(k):
                    act.wait_ge(turned, 2 * (S0 + k) + 2)
                    if k >= 2:
                        act.wait_ge(summed, S0 + k - 1)
                    act.activation(turned_w[k % 2][:, HALF:KEYS], psum[:, 5, :], ACT.Copy).then_inc(half_taken[1], 1)

                for k in range(U):
                    exps(k)
                    if k >= 1:
                        take_half(k - 1)
                take_half(U - 1)
                take_turned_output(act, psum, oT, o_turned, o_turned_taken, b)

        @block.vector
        def _(dve):
            for n in range(1, len(parts), 2):
                take_context(dve, n, dve.tensor_copy, kv_dve)
            with dve.Fori(0, B) as b:
                step = Steps(dve, own, b * (U + 1), U + 1)
                S0 = b * U
                dve.wait_ge(out_taken, b)
                x_b = x_all[:, bass.ds(b * TT, TT), :]
                step.did(dve.tensor_tensor(x_b, x_b, bo[:].unsqueeze(1).to_broadcast([P, TT, D]), ALU.add))

                def row_max(k):
                    dve.wait_ge(scored, S0 + k + 1)
                    dve.tensor_reduce(negmax[:, k:k + 1], psum[:, 2 * (k % 2):2 * (k % 2) + 2, :].rearrange("p a n -> p (a n)"),
                                      AX.X, ALU.max, negate=True).then_inc(max_ready, 1)

                def take_half(k):
                    dve.wait_ge(turned, 2 * (S0 + k) + 1)
                    if k >= 2:
                        dve.wait_ge(summed, S0 + k - 1)
                    dve.tensor_copy(turned_w[k % 2][:, 0:HALF], psum[:, 4, :]).then_inc(half_taken[0], 1)

                def take_head(k):
                    h, t = k // TT, k % TT
                    dve.wait_ge(exp_done, S0 + k + 1)
                    step.link(dve.reciprocal(sums[:, k:k + 1], sums[:, k:k + 1]))
                    dve.wait_ge(summed, S0 + k + 1)
                    dve.tensor_scalar(o[:, t, h * AD:(h + 1) * AD], psum[:, 6 + k % 2, 0:AD], sums[:, k:k + 1], None,
                                      ALU.mult).then_inc(head_taken, 1)

                for k in range(U):
                    row_max(k)
                    if k >= 1:
                        take_half(k - 1)
                    if k >= 2:
                        take_head(k - 2)
                take_half(U - 1)
                take_head(U - 2)
                take_head(U - 1)
                step.wait()
                dve.wait_ge(out_ready, b + 1)
                dve.tensor_tensor(x_b, psum[:, 4, :].rearrange("p (t d) -> p t d", t=TT), x_b, ALU.add).then_inc(out_taken, 1)
                step.end()


CH, CD = 16, 64
MASKED = -1e9


def cross_attention1(nc, norm, x_all, xnT_all, ident, psum, a):
    with ExitStack() as stack:
        s = Scope(nc, stack, "x1")
        HD = CH * CD
        TILES_QK = HD // P
        wq, wk, wv = (s.sb(n, [P, CC, HD]) for n in ("wq", "wk", "wv"))
        wo, bo = s.sb("wo", [P, HD // P, D]), s.sb("bo", [P, D])
        mask_i, mask = s.sb("mask_i", [P, TT, T], I32), s.sb("mask", [P, TT, T])
        xnT, ctxT = s.sb("xnT", [P, CC, T]), s.sb("ctxT", [P, CC, T])
        qT, kT = s.sb("qT", [P, TILES_QK, T]), s.sb("kT", [P, TILES_QK, T])
        v = s.sb("v", [P, TT, HD])
        masked_s = [s.sb(f"masked_s{i}", [P, TT, T]) for i in range(2)]
        weights = [s.sb(f"weights{i}", [P, TT, T]) for i in range(2)]
        turned_w = [s.sb(f"turned_w{i}", [P, TT, T]) for i in range(2)]
        rowmax, negmax, sums = (s.sb(n, [P, CH, TT]) for n in ("rowmax", "negmax", "sums"))
        o, oT = s.sb("o", [P, TT, HD]), s.sb("oT", [P, TT, HD // P, P])
        loaded, x_here, ctx_here = s.sem("loaded"), s.sem("x_here"), s.sem("ctx_here")
        projected, v_taken, qk_taken = s.sem("projected"), s.sem("v_taken"), s.sem("qk_taken")
        scored, maxed, max_ready, exp_done, turned, turned_taken, summed, head_taken = (
            s.sem(n) for n in ("scored", "maxed", "max_ready", "exp_done", "turned", "turned_taken", "summed",
                               "head_taken"))
        own, own_setup, passed = s.sem("own"), s.sem("own_setup"), s.sem("passed")
        o_turned, o_turned_taken, out_ready, out_taken = (
            s.sem(n) for n in ("o_turned", "o_turned_taken", "out_ready", "out_taken"))
        loads = [(wv[:], chunked(a["wv"])), (wq[:], chunked(a["wq"])), (wk[:], chunked(a["wk"])),
                 (wo[:], chunked(a["wo"])), (bo[:], over_partitions(a["bo"], D)), (mask_i[:], chunked(a["mask"]))]
        normalise(nc, norm, x_all, xnT_all, ident, psum, loads, loaded)
        block = stack.enter_context(nc.Block())
        order = [("v", 0, 0), ("v", 0, 1), ("v", 1, 0), ("v", 1, 1)] + \
                [(kind, m, 0) for m in range(TILES_QK // 2) for kind in ("q", "k")]
        NP, NV = len(order), 4

        @block.sync
        def _(sp):
            with sp.Fori(0, B) as b:
                sp.wait_ge(projected, b * NP)
                sp.dma_start(ctxT[:], a["ctxT"][bass.ds(b * D, D), :].rearrange("(k p) n -> p k n", p=P))\
                  .then_inc(ctx_here, 16)
                sp.dma_start(xnT[:], xnT_all[:, bass.ds(b, 1), :, :]).then_inc(x_here, 16)

        @block.tensor
        def _(pe):
            pe.wait_ge(loaded, 16 * len(loads))
            with pe.Fori(0, B) as b:
                S0 = b * CH
                pe.wait_ge(ctx_here, b * 16 + 16)
                pe.wait_ge(x_here, b * 16 + 16)
                pe.wait_ge(out_taken, b)
                for n, (kind, m, half) in enumerate(order):
                    if 6 <= n < 6 + NV:
                        pe.wait_ge(v_taken, b * NV + n - 5)
                    elif n >= 6 + NV:
                        pe.wait_ge(qk_taken, b * (NP - NV) + n - 5 - NV)
                    for c in range(CC):
                        if kind == "v":
                            ins = pe.matmul(psum[:, n % 6, :], ctxT[:, c, m * P:(m + 1) * P],
                                            wv[:, c, half * 512:(half + 1) * 512], start=(c == 0), stop=(c == CC - 1))
                    if kind != "v":
                        w, src = (wq, xnT) if kind == "q" else (wk, ctxT)
                        for j in range(2):
                            lo = (2 * m + j) * P
                            for c in range(CC):
                                ins = pe.matmul(psum[:, n % 6, j * T:(j + 1) * T], w[:, c, lo:lo + P], src[:, c, :],
                                                start=(c == 0), stop=(c == CC - 1))
                    ins.then_inc(projected, 1)
                for what, k in scores_softmax_value_order(CH):
                    r0 = CD * (k % 2)
                    if what == "scores":
                        if k == 0:
                            pe.wait_ge(qk_taken, b * (NP - NV) + NP - NV)
                            pe.wait_ge(v_taken, b * NV + NV)
                        if k >= 2:
                            pe.wait_ge(max_ready, S0 + k - 1)
                        for t in range(TT):
                            ins = pe.matmul(psum[:, 6 + k % 2, t * T:(t + 1) * T],
                                            qT[r0:r0 + CD, k // 2, t * P:(t + 1) * P], kT[r0:r0 + CD, k // 2, :],
                                            start=True, stop=True)
                        ins.then_inc(scored, 1)
                    elif what == "turn":
                        pe.wait_ge(exp_done, S0 + k + 1)
                        if k >= 2:
                            pe.wait_ge(turned_taken, S0 + k - 1)
                        for j in range(TT):
                            for t in range(TT):
                                lo = j * T + t * P
                                ins = pe.transpose(psum[:, 4 + k % 2, lo:lo + P], weights[k % 2][:, t, j * P:(j + 1) * P],
                                                   ident[:])
                        ins.then_inc(turned, 1)
                    else:
                        pe.wait_ge(turned_taken, S0 + k + 1)
                        if k >= 4:
                            pe.wait_ge(head_taken, S0 + k - 3)
                        for t in range(TT):
                            for j in range(TT):
                                ins = pe.matmul(psum[:, k % 4, t * CD:(t + 1) * CD],
                                                turned_w[k % 2][:, j, t * P:(t + 1) * P], v[:, j, k * CD:(k + 1) * CD],
                                                start=(j == 0), stop=(j == TT - 1))
                        ins.then_inc(summed, 1)
                pe.wait_ge(head_taken, S0 + CH)
                turn_and_project(pe, psum, ident, o, oT, wo, o_turned, o_turned_taken, out_ready, b, HD // P)

        @block.scalar
        def _(act):
            with act.Fori(0, B) as b:
                S0 = b * CH
                for n in range(NV, NP):
                    kind, m, _ = order[n]
                    act.wait_ge(projected, b * NP + n + 1)
                    act.activation((qT if kind == "q" else kT)[:, 2 * m:2 * m + 2, :],
                                   psum[:, n % 6, :].rearrange("p (j t) -> p j t", j=2), ACT.Copy,
                                   scale=(CD ** -0.5 if kind == "q" else 1.0)).then_inc(qk_taken, 1)

                def exps(k):
                    act.wait_ge(max_ready, S0 + k + 1)
                    if k >= 2:
                        act.wait_ge(turned, S0 + k - 1)
                    for t in range(TT):
                        ins = act.activation(weights[k % 2][:, t, :], masked_s[k % 2][:, t, :], ACT.Exp,
                                             bias=negmax[:, k, t:t + 1], accum_out=sums[:, k, t:t + 1])
                    ins.then_inc(exp_done, 1)

                def take_turned(k):
                    act.wait_ge(turned, S0 + k + 1)
                    if k >= 2:
                        act.wait_ge(summed, S0 + k - 1)
                    act.activation(turned_w[k % 2][:], psum[:, 4 + k % 2, :].rearrange("p (j t) -> p j t", j=TT),
                                   ACT.Copy).then_inc(turned_taken, 1)

                for k in range(CH):
                    exps(k)
                    if k >= 1:
                        take_turned(k - 1)
                take_turned(CH - 1)
                take_turned_output(act, psum, oT, o_turned, o_turned_taken, b)

        @block.vector
        def _(dve):
            dve.wait_ge(loaded, 16 * len(loads))
            step = Steps(dve, own_setup)
            step.link(dve.tensor_copy(mask[:], mask_i[:]))
            step.link(dve.tensor_scalar(mask[:], mask[:], 0.0, MASKED, ALU.is_equal, ALU.mult))
            with dve.Fori(0, B) as b:
                per = CH + 1
                step = Steps(dve, own, b * per, per)
                S0 = b * CH
                dve.wait_ge(out_taken, b)
                x_b = x_all[:, bass.ds(b * TT, TT), :]
                step.did(dve.tensor_tensor(x_b, x_b, bo[:].unsqueeze(1).to_broadcast([P, TT, D]), ALU.add))
                for n in range(NV):
                    _, m, half = order[n]
                    dve.wait_ge(projected, b * NP + n + 1)
                    dve.tensor_copy(v[:, m, half * 512:(half + 1) * 512], psum[:, n, :]).then_inc(v_taken, 1)

                def row_max(k):
                    if k >= 2:
                        dve.wait_ge(exp_done, S0 + k - 1)
                    alone(dve, scored, S0 + k + 1, passed)
                    for t in range(TT):
                        ins = dve.tensor_tensor_reduce(masked_s[k % 2][:, t, :], psum[:, 6 + k % 2, t * T:(t + 1) * T],
                                                       mask[:, t, :], 1.0, -3e38, ALU.add, ALU.max, rowmax[:, k, t:t + 1])
                    ins.then_inc(maxed, 1)
                    dve.wait_ge(maxed, S0 + k + 1)
                    dve.tensor_scalar(negmax[:, k, :], rowmax[:, k, :], -1.0, None, ALU.mult).then_inc(max_ready, 1)

                def take_head(k):
                    dve.wait_ge(exp_done, S0 + k + 1)
                    step.link(dve.reciprocal(sums[:, k, :], sums[:, k, :]))
                    dve.wait_ge(summed, S0 + k + 1)
                    dve.tensor_tensor(o[:, :, k * CD:(k + 1) * CD],
                                      psum[:, k % 4, 0:TT * CD].rearrange("p (t d) -> p t d", t=TT),
                                      sums[:, k, :].unsqueeze(2).to_broadcast([P, TT, CD]), ALU.mult).then_inc(head_taken, 1)

                for k in range(CH):
                    row_max(k)
                    if k >= 2:
                        take_head(k - 2)
                take_head(CH - 2)
                take_head(CH - 1)
                step.wait()
                dve.wait_ge(out_ready, b + 1)
                dve.tensor_tensor(x_b, psum[:, 4, :].rearrange("p (t d) -> p t d", t=TT), x_b, ALU.add).then_inc(out_taken, 1)
                step.end()


HID, NE, NGR = 512, 8, 2
PER_GROUP = NE // NGR


def experts(nc, norm, x_all, xnT_all, ident, psum, a):
    with ExitStack() as stack:
        s = Scope(nc, stack, "f1")
        KH = HID // P
        w_in, w1 = s.sb("w_in", [P, CC, 2 * HID]), s.sb("w1", [P, CC, 2 * HID])
        w_out, w2 = s.sb("w_out", [P, KH, D]), s.sb("w2", [P, KH, NE * D])
        wg = s.sb("wg", [P, CC, NGR + NE])
        bg, rev = s.sb("bg", [P, NGR + NE]), s.sb("rev", [P, NE])
        xnT = s.sb("xnT", [P, CC, T])
        silu = s.sb("silu", [P, 2, T])
        hidden = s.sb("hidden", [P, 2, KH, T])
        logits, top = s.sb("logits", [P, TT, NGR + NE]), s.sb("top", [P, TT, 1 + NGR])
        expd = s.sb("expd", [P, TT, NGR + NE])
        total = s.sb("total", [P, TT, 1 + NGR])
        chosen_group, group_p = s.sb("chosen_group", [P, TT, NGR]), s.sb("group_p", [P, TT])
        p, mask, eq, rest = (s.sb(n, [P, TT, NE]) for n in ("p", "mask", "eq", "rest"))
        red = s.sb("red", [P, TT])
        acc = s.sb("acc", [P, TT, D])
        loaded, x_here, projected, silu_done, hidden_taken = (
            s.sem(n) for n in ("loaded", "x_here", "projected", "silu_done", "hidden_taken"))
        gates_ready, shifted, exp_done, own = s.sem("gates_ready"), s.sem("shifted"), s.sem("exp_done"), s.sem("own")
        routed_ready, routed_taken = s.sem("routed_ready"), s.sem("routed_taken")
        loads = [(wg[:], chunked(a["wg"])), (w_in[:], chunked(a["w_in"])), (w1[:], chunked(a["w1"])),
                 (w_out[:], chunked(a["w_out"])), (w2[:], chunked(a["w2"])), (bg[:], over_partitions(a["bg"], NGR + NE)),
                 (rev[:], over_partitions(a["rev"], NE))]
        normalise(nc, norm, x_all, xnT_all, ident, psum, loads, loaded)
        block = stack.enter_context(nc.Block())
        NHID = 2 * KH
        NR = NE // 2 + 1

        @block.sync
        def _(sp):
            with sp.Fori(0, B) as b:
                sp.wait_ge(projected, b * NHID)
                sp.dma_start(xnT[:], xnT_all[:, bass.ds(b, 1), :, :]).then_inc(x_here, 16)

        @block.tensor
        def _(pe):
            pe.wait_ge(loaded, 16 * len(loads))
            with pe.Fori(0, B) as b:
                pe.wait_ge(x_here, b * 16 + 16)
                pe.wait_ge(shifted, b)
                for t in range(TT):
                    for c in range(CC):
                        ins = pe.matmul(psum[:, 7, t * 16:t * 16 + NGR + NE], xnT[:, c, t * P:(t + 1) * P], wg[:, c, :],
                                        start=(c == 0), stop=(c == CC - 1))
                ins.then_inc(gates_ready, 1)
                for n in range(NHID):
                    w, j = (w_in, w1)[n // KH], n % KH
                    bank = psum[:, 4 + n % 3, :]
                    if n >= 3:
                        pe.wait_ge(hidden_taken, b * NHID + n - 2)
                    else:
                        pe.wait_ge(hidden_taken, b * NHID)
                    for part in range(2):
                        lo = part * HID + j * P
                        for c in range(CC):
                            ins = pe.matmul(bank[:, part * T:(part + 1) * T], w[:, c, lo:lo + P], xnT[:, c, :],
                                            start=(c == 0), stop=(c == CC - 1))
                    ins.then_inc(projected, 1)
                for t in range(TT):
                    for r in range(NR):
                        n = t * NR + r
                        if n >= 4:
                            pe.wait_ge(routed_taken, b * TT * NR + n - 3)
                        else:
                            pe.wait_ge(routed_taken, b * TT * NR)
                        if n == 0:
                            pe.wait_ge(hidden_taken, b * NHID + KH)
                        if n == 1:
                            pe.wait_ge(hidden_taken, b * NHID + NHID)
                        for k in range(KH):
                            if r == 0:
                                ins = pe.matmul(psum[:, n % 4, 0:D], hidden[:, 0, k, t * P:(t + 1) * P], w_out[:, k, :],
                                                start=(k == 0), stop=(k == KH - 1))
                            else:
                                ins = pe.matmul(psum[:, n % 4, :], hidden[:, 1, k, t * P:(t + 1) * P],
                                                w2[:, k, (r - 1) * 512:r * 512], start=(k == 0), stop=(k == KH - 1))
                        ins.then_inc(routed_ready, 1)

        @block.scalar
        def _(act):
            with act.Fori(0, B) as b:
                act.wait_ge(shifted, b + 1)
                act.activation(expd[:], logits[:], ACT.Exp).then_inc(exp_done, 1)
                for n in range(NHID):
                    act.wait_ge(projected, b * NHID + n + 1)
                    if n >= 2:
                        act.wait_ge(hidden_taken, b * NHID + n - 1)
                    act.activation(silu[:, n % 2, :], psum[:, 4 + n % 3, 0:T], ACT.Silu).then_inc(silu_done, 1)

        @block.vector
        def _(dve):
            dve.wait_ge(loaded, 16 * len(loads))
            with dve.Fori(0, B) as b:
                per = 14 + TOP2_STEPS + TT * NE // 2
                step = Steps(dve, own, b * per, per)
                step.wait()
                dve.wait_ge(routed_taken, b * TT * NR)
                dve.wait_ge(gates_ready, b + 1)
                step.link(dve.tensor_tensor(logits[:], psum[:, 7, 0:TT * 16].rearrange("p (t n) -> p t n", t=TT)[:, :, 0:NGR + NE],
                                            bg[:].unsqueeze(1).to_broadcast([P, TT, NGR + NE]), ALU.add))
                by_group = lambda v: v[:, :, NGR:NGR + NE].rearrange("p t (g e) -> p t g e", g=NGR)
                step.did(dve.tensor_reduce(top[:, :, 0], logits[:, :, 0:NGR], AX.X, ALU.max))
                step.link(dve.tensor_reduce(top[:, :, 1:1 + NGR], by_group(logits), AX.X, ALU.max))
                dve.tensor_tensor(logits[:, :, 0:NGR], logits[:, :, 0:NGR], top[:, :, 0:1].to_broadcast([P, TT, NGR]), ALU.subtract)
                dve.tensor_tensor(by_group(logits), by_group(logits),
                                  top[:, :, 1:1 + NGR].unsqueeze(3).to_broadcast([P, TT, NGR, PER_GROUP]),
                                  ALU.subtract).then_inc(shifted, 1)
                for n in range(NHID):
                    dve.wait_ge(silu_done, b * NHID + n + 1)
                    dve.tensor_tensor(hidden[:, n // KH, n % KH, :], silu[:, n % 2, :], psum[:, 4 + n % 3, T:2 * T],
                                      ALU.mult).then_inc(hidden_taken, 1)
                dve.wait_ge(exp_done, b + 1)
                step.did(dve.tensor_reduce(total[:, :, 0], expd[:, :, 0:NGR], AX.X, ALU.add))
                step.link(dve.tensor_reduce(total[:, :, 1:1 + NGR], by_group(expd), AX.X, ALU.add))
                step.link(dve.reciprocal(total[:], total[:]))
                step.link(dve.tensor_tensor(expd[:, :, 0:NGR], expd[:, :, 0:NGR], total[:, :, 0:1].to_broadcast([P, TT, NGR]), ALU.mult))
                step.did(dve.tensor_tensor(chosen_group[:, :, 0], expd[:, :, 0], expd[:, :, 1], ALU.is_ge))
                step.link(dve.tensor_tensor(chosen_group[:, :, 1], expd[:, :, 1], expd[:, :, 0], ALU.is_gt))
                step.link(dve.tensor_reduce(group_p[:], expd[:, :, 0:NGR], AX.X, ALU.max))
                step.link(dve.tensor_tensor(chosen_group[:], chosen_group[:], group_p[:].unsqueeze(2).to_broadcast([P, TT, NGR]),
                                            ALU.mult))
                p4 = p[:].rearrange("p t (g e) -> p t g e", g=NGR)
                step.link(dve.tensor_tensor(p4, by_group(expd), total[:, :, 1:1 + NGR].unsqueeze(3).to_broadcast(
                    [P, TT, NGR, PER_GROUP]), ALU.mult))
                step.link(dve.tensor_tensor(p4, p4, chosen_group[:].unsqueeze(3).to_broadcast([P, TT, NGR, PER_GROUP]),
                                            ALU.mult))
                top2(dve, step, p[:], mask[:], (eq[:], rest[:]), red[:], rev[:], TT)
                step.link(dve.tensor_tensor(p[:], p[:], mask[:], ALU.mult))
                for t in range(TT):
                    R0 = (b * TT + t) * NR
                    x_t = x_all[:, bass.ds(b * TT + t, 1), :].rearrange("p a d -> p (a d)")
                    for r in range(NR):
                        bank = psum[:, (t * NR + r) % 4, :]
                        dve.wait_ge(routed_ready, R0 + r + 1)
                        if r == 0:
                            dve.tensor_tensor(acc[:, t, :], bank[:, 0:D], x_t, ALU.add).then_inc(routed_taken, 1)
                            continue
                        for half in range(2):
                            e = 2 * (r - 1) + half
                            dve.wait_ge(routed_taken, R0 + r) if half == 0 else step.wait()
                            ins = dve.scalar_tensor_tensor(x_t if e == NE - 1 else acc[:, t, :], bank[:, half * D:(half + 1) * D],
                                                           p[:, t, e:e + 1], acc[:, t, :], ALU.mult, ALU.add)
                            if half == 0:
                                step.did(ins)
                        ins.then_inc(routed_taken, 1)
                step.end()


STAGES = (("a0", attention0), ("x0", linear_attention), ("f0", switch_attention),
          ("a1", attention1), ("x1", cross_attention1), ("f1", experts))


def build(nc, inputs, out):
    with ExitStack() as stack:
        Scope.semaphores = stack
        s = Scope(nc, stack, "all")
        x_all = s.sb("x_all", [P, TILES, D])
        xnT_all = s.sb("xnT_all", [P, B, CC, T])
        ident = s.sb("ident", [P, P])
        psum = stack.enter_context(nc.psum_tensor("psum", [P, 8, 512], F32))
        x_loaded, stored = s.sem("x_loaded"), s.sem("stored")
        norm = Norm(Scope(nc, stack, "ln"))
        with nc.Block() as block:
            @block.sync
            def _(sp):
                sp.dma_start(ident[:], inputs["ident"]).then_inc(x_loaded, 16)
                sp.dma_start(x_all[:], inputs["x"].rearrange("b (t p) d -> p (b t) d", p=P)).then_inc(x_loaded, 16)
                sp.wait_ge(x_loaded, 32)
        for prefix, stage in STAGES:
            own = {k[len(prefix) + 1:]: v for k, v in inputs.items() if k.startswith(prefix + "_")}
            stage(nc, norm, x_all, xnT_all, ident, psum, own)
        with nc.Block() as block:
            @block.sync
            def _(sp):
                sp.dma_start(out.rearrange("b (t p) d -> p (b t) d", p=P), x_all[:]).then_inc(stored, 16)
                sp.wait_ge(stored, 16)


def _rope_tables():
    inv_freq = (1.0 / 10000.0 ** (np.arange(0, DH, 2, dtype=np.float32) / DH)).astype(np.float32)
    freqs = np.arange(T, dtype=np.float32)[:, None] * inv_freq[None, :]
    cos, sin = np.cos(freqs).T.astype(np.float32), np.sin(freqs).T.astype(np.float32)
    cos = np.tile(np.concatenate([cos, cos]), (P // DH, 1))
    sin = np.tile(np.concatenate([-sin, sin]), (P // DH, 1))
    return np.ascontiguousarray(np.stack([cos, sin], axis=1))


def _blocks(width):
    i = np.arange(P) // width
    return (i[:, None] == i[None, :]).astype(np.float32)


def _layouts(n):
    half = DH // 2
    plain = np.concatenate([np.arange(0, DH, 2), np.arange(1, DH, 2)])
    swapped = np.roll(plain, half)
    cols = {v: (np.arange(BR * NH)[:, None] * DH + p[None, :]).ravel() for v, p in (("", plain), ("s", swapped))}
    out = {"ident": np.eye(P, dtype=np.float32), "x": n["x"]}
    W, bias = n["L0_attn_W_Q"], n["L0_attn_b_Q"]
    out["a0_wq"], out["a0_wqs"] = W[:, cols[""]], W[:, cols["s"]]
    out["a0_bq"] = np.stack([bias[cols[v]].reshape(8, P).T for v in ("", "s")], axis=1)
    W, bias = n["L0_attn_W_K"], n["L0_attn_b_K"]
    out["a0_wk"], out["a0_wks"] = W[:, cols[""][:D]], W[:, cols["s"][:D]]
    out["a0_bk"] = np.stack([bias[cols[v][:D]].reshape(CC, P).T for v in ("", "s")], axis=1)
    out["a0_wv"], out["a0_bv"] = n["L0_attn_W_V"], n["L0_attn_b_V"]
    out["a0_wo"] = n["L0_attn_W_O"].reshape(BR * D, D)
    out["a0_bo"] = n["L0_attn_W_O_bias"].reshape(-1)
    out["a0_vnull"] = n["L0_attn_v_nulls"].reshape(-1)
    out["a0_sinks"] = n["L0_attn_sink_scalars"]
    out["a0_rope"] = _rope_tables()
    out["a0_same_head"] = _blocks(DH)
    out["a0_head_mask"] = np.ascontiguousarray(_blocks(DH)[:, ::DH])
    for name in ("q", "k", "v"):
        out[f"x0_w{name}"], out[f"x0_b{name}"] = n[f"L0_xattn_W{name}"], n[f"L0_xattn_b{name}"]
    out["x0_scale"] = n["L0_xattn_scale"].reshape(-1)
    out["x0_same_head"], out["x0_head_mask"] = out["a0_same_head"], out["a0_head_mask"]
    out["x0_ctxT"] = n["ctx_1024"].transpose(0, 2, 1).reshape(B * D, T)
    out["f0_wg"] = np.concatenate([n["L0_ffn_Ws"].reshape(-1, D), n["L0_ffn_Wd"].reshape(-1, D)]).T
    out["f0_wv"] = n["L0_ffn_Wv"].reshape(-1, D).T
    out["f0_wq"], out["f0_wk"] = n["L0_ffn_Wq"].reshape(-1, D).T, n["L0_ffn_Wk"].reshape(-1, D).T
    out["f0_wo"] = n["L0_ffn_Wo"].transpose(0, 2, 1).reshape(-1, D)
    out["f0_rev"] = np.arange(8, 0, -1, dtype=np.float32)
    out["a1_ctxT"] = n["L1_attn_context"].reshape(KEYS, CTX).T
    out["a1_wq"], out["a1_wk"], out["a1_wv"] = n["L1_attn_Wq"], n["L1_attn_Wk"], n["L1_attn_Wv"]
    out["a1_wo"], out["a1_bo"] = n["L1_attn_Wout"], n["L1_attn_bout"]
    for name in ("q", "k", "v"):
        out[f"x1_w{name}"] = n[f"L1_xattn_w_{name}"]
    out["x1_wo"], out["x1_bo"] = n["L1_xattn_out_w"].T, n["L1_xattn_out_b"]
    out["x1_mask"], out["x1_ctxT"] = n["mask_SxS2_ik0"], out["x0_ctxT"]
    out["f1_w_in"], out["f1_w1"], out["f1_w_out"] = n["L1_ffn_w_in"].T, n["L1_ffn_w1"].T, n["L1_ffn_w_out"].T
    out["f1_w2"] = n["L1_ffn_w2"].transpose(2, 0, 1).reshape(HID, NE * D)
    out["f1_wg"] = np.concatenate([n["L1_ffn_wg"], n["L1_ffn_we"]]).T
    out["f1_bg"] = np.concatenate([n["L1_ffn_gb"], n["L1_ffn_eb"]])
    out["f1_rev"] = out["f0_rev"]
    return out


def kernel(**inputs):
    import concourse.bacc as bacc
    from concourse.bass_utils import run_bass_kernel_spmd

    nc = bacc.Bacc("TRN2", target_bir_lowering=False, num_devices=1)
    arrays, tensors = {}, {}
    for name, value in _layouts({k: np.asarray(v) for k, v in inputs.items()}).items():
        value = np.ascontiguousarray(value)
        arrays[f"in_{name}"] = value
        tensors[name] = nc.dram_tensor(f"in_{name}", value.shape, mybir.dt.from_np(value.dtype), kind="ExternalInput").ap()
    out = nc.dram_tensor("out", (B, T, D), F32, kind="ExternalOutput").ap()
    build(nc, tensors, out)
    return run_bass_kernel_spmd(nc, [arrays], core_ids=[0]).results[0]["out"]
```

```python
from contextlib import ExitStack
import math

import numpy as np
import concourse.bass as bass
from concourse import mybir

F32 = mybir.dt.float32
I32 = mybir.dt.int32
ALU = mybir.AluOpType
ACT = mybir.ActivationFunctionType
AX = mybir.AxisListType

P = 128
B, T, D = 8, 256, 256
TILES = B * T // P
TT = T // P
CC = D // P
LN_EPS = 1e-5


class Scope:

    semaphores = None

    def __init__(self, nc, stack, prefix):
        self.nc, self.stack, self.prefix = nc, stack, prefix

    def sb(self, name, shape, dtype=F32):
        return self.stack.enter_context(self.nc.sbuf_tensor(f"{self.prefix}_{name}", shape, dtype))

    def sem(self, name):
        return (Scope.semaphores or self.stack).enter_context(self.nc.semaphore(f"{self.prefix}_{name}"))

    def sems(self, name, n):
        return [self.sem(f"{name}{i}") for i in range(n)]


class Steps:

    def __init__(self, eng, sem, base=0, per=None):
        self.eng, self.sem, self.base, self.per, self.n = eng, sem, base, per, 0

    def did(self, instruction):
        instruction.then_inc(self.sem, 1)
        self.n += 1

    def wait(self):
        self.eng.wait_ge(self.sem, self.base + self.n)

    def link(self, instruction):
        self.did(instruction)
        self.wait()

    def end(self):
        assert self.per is None or self.n == self.per, (self.n, self.per)


def alone(eng, sem, value, passed):
    eng.wait_ge(sem, value)
    eng.sem_inc(passed, 1)


def chunked(w):
    return w.rearrange("(k p) n -> p k n", p=P)


def over_partitions(v, n):
    return v.rearrange("(a n) -> a n", a=1).to_broadcast([P, n])


class Norm:

    def __init__(self, s):
        self.runs = 0
        self.own, self.variance_ready, self.std_ready = s.sem("own"), s.sem("variance_ready"), s.sem("std_ready")
        self.normalised, self.transposed, self.copied = (s.sems(n, TT) for n in ("normalised", "transposed", "copied"))


def normalise(nc, norm, x_all, xnT_all, ident, psum, loads, loaded):
    with ExitStack() as stack:
        run = norm.runs
        norm.runs += 1
        b0 = run * B
        s = Scope(nc, stack, f"ln{run}")
        stats = s.sb("stats", [P, TILES, 6])
        mean_var = s.sb("mean_var", [P, TILES, 2])
        std = s.sb("std", [P, TILES])
        rstd = s.sb("rstd", [P, TILES])
        shift = s.sb("shift", [P, TILES])
        eps = s.sb("eps", [P, 1])
        xn = s.sb("xn", [P, TT, D])
        psT = psum[:, 0:TT, :].rearrange("p t (c n) -> p t c n", n=P)
        variance_ready, std_ready = norm.variance_ready, norm.std_ready
        normalised, transposed, copied = norm.normalised, norm.transposed, norm.copied
        block = stack.enter_context(nc.Block())

        @block.sync
        def _(sp):
            for dst, src in loads:
                sp.dma_start(dst, src).then_inc(loaded, 16)

        @block.vector
        def _(dve):
            step = Steps(dve, norm.own, run * (TILES + 3))
            step.did(dve.memset(eps[:], LN_EPS))
            for t in range(TILES):
                step.did(dve.bn_stats(stats[:, t, :], x_all[:, t, :]))
            step.wait()
            for t in range(TILES):
                ins = dve.bn_aggr(mean_var[:, t, :], stats[:, t, :])
            ins.then_inc(variance_ready, 1)
            dve.wait_ge(std_ready, run + 1)
            step.link(dve.reciprocal(rstd[:], std[:]))
            step.link(dve.scalar_tensor_tensor(shift[:], mean_var[:, :, 0], -1.0, rstd[:], ALU.mult, ALU.mult))
            with dve.Fori(0, B) as b:
                for t in range(TT):
                    dve.wait_ge(transposed[t], b0 + b)
                    tile = b * TT + t
                    dve.tensor_scalar(xn[:, t, :], x_all[:, bass.ds(tile, 1), :], rstd[:, bass.ds(tile, 1)],
                                      shift[:, bass.ds(tile, 1)], ALU.mult, ALU.add).then_inc(normalised[t], 1)

        @block.tensor
        def _(pe):
            with pe.Fori(0, B) as b:
                for t in range(TT):
                    pe.wait_ge(normalised[t], b0 + b + 1)
                    pe.wait_ge(copied[t], b0 + b)
                    for c in range(CC):
                        ins = pe.transpose(psT[:, t, c, :], xn[:, t, c * P:(c + 1) * P], ident[:])
                    ins.then_inc(transposed[t], 1)

        @block.scalar
        def _(act):
            act.wait_ge(variance_ready, run + 1)
            act.activation(std[:], mean_var[:, :, 1], ACT.Sqrt, bias=eps[:, 0:1]).then_inc(std_ready, 1)
            with act.Fori(0, B) as b:
                for t in range(TT):
                    act.wait_ge(transposed[t], b0 + b + 1)
                    act.activation(xnT_all[:, bass.ds(b, 1), :, t * P:(t + 1) * P], psT[:, t, 0:CC, :],
                                   ACT.Copy).then_inc(copied[t], 1)


BR, NH, DH = 4, 16, 16
NU = NH
RING = 8
K1 = BR * T
UNIT = BR * T + BR * P
SILU_SCALE = math.pi / math.sqrt(3.0)
CAP = 44.0

THRESHOLD_LAG, SUM_LAG, TAKE_LAG = 6, 8, 8
SILU_EVERY, SILU_FROM, SILU_TO = 4, 5, 2
HERE, AHEAD, OLD = "new", "ahead", "old"
SPARE = {0: [("q", 0, HERE)], 1: [("q", 1, HERE)], 2: [("q", 2, HERE)], 3: [("q", 3, HERE)],
         4: [("k", 0, AHEAD)], 5: [("k", 1, AHEAD)], 6: [("norm", 0, AHEAD)], 7: [("v", 0, HERE)],
         8: [("q", 0, AHEAD)], 9: [("q", 1, AHEAD)], 10: [("turn", 0, OLD), ("turn", 1, OLD)],
         11: [("turn", 2, OLD), ("turn", 3, OLD)], 12: [("q", 2, AHEAD)], 13: [("q", 3, AHEAD)],
         14: [("out", 0, OLD)], 15: []}
ROTATED = 2 + 2 * BR


WARM_UP_SLOTS = (0, 4, 8, 12)


def warm_up(pe, bank, ident, operand):
    for _ in range(4):
        pe.matmul(bank, ident[:], operand[:, 0:2, :], start=True, stop=True)


def rotations(b, kind, i, when):
    place = i if when == HERE else 4 + i if kind == "k" else 6 + i
    return b * ROTATED + 6 + place


def wait(eng, sem, value):
    if not isinstance(value, int) or value > 0:
        eng.wait_ge(sem, value)


def wait_alone(eng, sem, value, passed):
    if not isinstance(value, int) or value > 0:
        alone(eng, sem, value, passed)


def over_batches(eng, body):
    body(-1, False, True, False)
    body(0, True, True, False)
    with eng.Fori(0, B - 2) as i:
        body(i + 1, True, True, True)
    body(B - 1, True, False, True)
    body(B, False, False, True)


def units(b, lag, new, old):
    for j in range(NU):
        v = j - lag
        yield (v % NU, b * NU + v) if (new if v >= 0 else old) else None


def attention0(nc, norm, x_all, xnT_all, ident, psum, a):
    with ExitStack() as stack:
        s = Scope(nc, stack, "a0")
        wq, wqs = s.sb("wq", [P, CC, BR * D]), s.sb("wqs", [P, CC, BR * D])
        wk, wks, wv = s.sb("wk", [P, CC, D]), s.sb("wks", [P, CC, D]), s.sb("wv", [P, CC, D])
        wo = s.sb("wo", [P, BR * CC, D])
        bq = s.sb("bq", [P, 2, 8])
        bk = s.sb("bk", [P, 2, CC])
        bv = s.sb("bv", [P, D])
        rope = s.sb("rope", [P, 2, T])
        same_head = s.sb("same_head", [P, P])
        head_mask = s.sb("head_mask", [P, 8])
        sinks = s.sb("sinks", [P, BR * NH])
        sinks_eps = s.sb("sinks_eps", [P, BR, NH])
        vnull = s.sb("vnull", [P, BR, NH, DH])
        bo = s.sb("bo", [P, BR, D])
        ln_quarter = s.sb("ln_quarter", [P, 1])
        xnT = s.sb("xnT", [P, CC, T])
        rot = [s.sb(f"rot{i}", [P, 2, T]) for i in range(2)]
        qT = s.sb("qT", [P, CC, BR, T])
        kT = s.sb("kT", [P, CC, T])
        ksq = s.sb("ksq", [P, CC, T])
        kT_head = s.sb("kT_head", [P, NH, T])
        v1 = s.sb("v1", [P, TT, NH, DH + 1])
        e = s.sb("e", [P, 2, UNIT])
        w = s.sb("w", [P, RING, UNIT])
        ctx = s.sb("ctx", [P, TT * BR, NH, DH + 1])
        total = s.sb("total", [P, TT * BR, NH])
        ctxn = s.sb("ctxn", [P, TT, BR * NH, DH])
        ctxT = s.sb("ctxT", [P, TT, 8, P])
        psS = [psum[:, 3 * i:3 * i + 3, :].rearrange("p k n -> p (k n)") for i in range(2)]
        psO = psum[:, 6, 0:TT * BR * (DH + 1)]
        spare = psum[:, 7, :]

        loaded, v_x_here = s.sem("loaded"), s.sem("v_x_here")
        projected, v_done, norm_done, turn_done, out_done = (
            s.sem(n) for n in ("projected", "v_done", "norm_done", "turn_done", "out_done"))
        rot_made, v_taken, norm_taken, turn_taken, out_taken = (
            s.sem(n) for n in ("rot_made", "v_taken", "norm_taken", "turn_taken", "out_taken"))
        rotated, ksq_ready, ln_k, knorm_ready, knormed, kheads_ready = (
            s.sem(n) for n in ("rotated", "ksq_ready", "ln_k", "knorm_ready", "knormed", "kheads_ready"))
        scored, exp_done, ln_done, softplus_done, masked, silu_done, weights_done, summed, ctx_taken = (
            s.sem(n) for n in ("scored", "exp_done", "ln_done", "softplus_done", "masked", "silu_done",
                               "weights_done", "summed", "ctx_taken"))
        totalled, inverted, null_added, ctx_ready = (
            s.sem(n) for n in ("totalled", "inverted", "null_added", "ctx_ready"))
        x_biased = s.sem("x_biased")
        consts, passed, own = s.sem("consts"), s.sem("passed"), s.sem("own_setup")

        loads = [(wk[:], chunked(a["wk"])), (wks[:], chunked(a["wks"])), (wv[:], chunked(a["wv"])),
                 (wq[:], chunked(a["wq"])), (wqs[:], chunked(a["wqs"])), (wo[:], chunked(a["wo"])),
                 (bq[:], a["bq"]), (bk[:], a["bk"]), (bv[:], over_partitions(a["bv"], D)),
                 (rope[:], a["rope"]), (same_head[:], a["same_head"]), (head_mask[:], a["head_mask"]),
                 (sinks[:], over_partitions(a["sinks"], BR * NH)),
                 (vnull[:].rearrange("p r h d -> p (r h d)"), over_partitions(a["vnull"], BR * D)),
                 (bo[:].rearrange("p r d -> p (r d)"), over_partitions(a["bo"], BR * D))]
        normalise(nc, norm, x_all, xnT_all, ident, psum, loads, loaded)
        block = stack.enter_context(nc.Block())

        @block.sync
        def _(sp):
            with sp.Fori(0, B) as b:
                sp.wait_ge(v_done, b)
                sp.dma_start(xnT[:], xnT_all[:, bass.ds(b, 1), :, :]).then_inc(v_x_here, 16)

        @block.tensor
        def _(pe):
            pe.wait_ge(loaded, 16 * len(loads))

            class Sums:

                def __init__(self, b, unit):
                    self.left = []
                    if unit:
                        self.b, (self.u, self.n) = b, unit
                        self.left = [(t, r, j) for t in range(TT) for r in range(BR) for j in range(t + 1)]

                def some(self, count):
                    for _ in range(min(count, len(self.left))):
                        t, r, j = self.left.pop(0)
                        u, n = self.u, self.n
                        if (t, r, j) == (0, 0, 0):
                            if u == 0:
                                pe.wait_ge(v_taken, self.b + 1)
                            pe.wait_ge(weights_done, n + 1)
                            wait(pe, ctx_taken, n)
                        lo = (t * BR + r) * (DH + 1)
                        q0 = K1 + r * P if j else r * T + t * P
                        ins = pe.matmul(psO[:, lo:lo + DH + 1], w[:, u % RING, q0:q0 + P], v1[:, j, u, :],
                                        start=(j == 0), stop=(j == t))
                        if not self.left:
                            ins.then_inc(summed, 1)

                def rest(self):
                    self.some(len(self.left))

            def body(b, new, ahead, old):
                exists = {HERE: new, AHEAD: ahead, OLD: old}
                of = {HERE: b, AHEAD: b + 1, OLD: b - 1}
                spare_free = [(out_taken, b - 1), (rot_made, b * ROTATED + (6 if new or ahead else 0))]

                def pass_through_spare(kind, i, when):
                    nonlocal spare_free
                    bb = of[when]
                    for sem, value in spare_free:
                        wait(pe, sem, value)
                    if kind in "qk":
                        g = 0 if when == AHEAD else 1
                        lo = i * P if kind == "k" else (2 * i + g) * P
                        for v, weights in enumerate((wk, wks) if kind == "k" else (wq, wqs)):
                            for c in range(CC):
                                ins = pe.matmul(spare[:, v * T:(v + 1) * T], weights[:, c, lo:lo + P],
                                                xnT_all[:, bass.ds(bb, 1), c, :], start=(c == 0), stop=(c == CC - 1))
                                if (v, c) != (1, CC - 1):
                                    sums.some(4)
                        ins.then_inc(projected, 1)
                        spare_free = [(rot_made, rotations(b, kind, i, when) + 1)]
                    elif kind == "v":
                        pe.wait_ge(v_x_here, bb * 16 + 16)
                        for t in range(TT):
                            for c in range(CC):
                                ins = pe.matmul(spare[:, t * D:(t + 1) * D], xnT[:, c, t * P:(t + 1) * P], wv[:, c, :],
                                                start=(c == 0), stop=(c == CC - 1))
                        ins.then_inc(v_done, 1)
                        spare_free = [(v_taken, bb + 1)]
                    elif kind == "norm":
                        pe.wait_ge(ksq_ready, bb + 1)
                        for g in range(CC):
                            ins = pe.matmul(spare[:, g * T:(g + 1) * T], same_head[:], ksq[:, g, :], start=True, stop=True)
                        ins.then_inc(norm_done, 1)
                        spare_free = [(norm_taken, bb + 1)]
                    elif kind == "turn":
                        if i == 0:
                            pe.wait_ge(ctx_ready, bb * 4 + 4)
                        for k in range(4):
                            lo = 8 * (4 * (i % 2) + k)
                            ins = pe.transpose(spare[:, k * P:(k + 1) * P],
                                               ctxn[:, i // 2, lo:lo + 8, :].rearrange("p h d -> p (h d)"), ident[:])
                        ins.then_inc(turn_done, 1)
                        spare_free = [(turn_taken, bb * 4 + i + 1)]
                    else:
                        for t in range(TT):
                            for k in range(8):
                                ins = pe.matmul(spare[:, t * D:(t + 1) * D], ctxT[:, t, k, :], wo[:, k, :],
                                                start=(k == 0), stop=(k == 7))
                        ins.then_inc(out_done, 1)

                for j, summed_unit in enumerate(units(b, SUM_LAG, new, old)):
                    sums = Sums(b, summed_unit)
                    if new:
                        g, n = j // 8, b * NU + j
                        if j % 8 == 0:
                            pe.wait_ge(kheads_ready, b * 2 + g + 1)
                            pe.wait_ge(rotated, b * ROTATED + 6 + 4 * g)
                        wait(pe, softplus_done, n - 1)
                        for half in range(2):
                            pe.matmul(psS[j % 2][:, half * 512:(half + 1) * 512], kT_head[:, j, 0:P],
                                      qT[:, g, 2 * half:2 * half + 2, :], start=True, stop=True)
                        pe.matmul(psS[j % 2][:, K1:UNIT], kT_head[:, j, P:T], qT[:, g, :, P:T],
                                  start=True, stop=True).then_inc(scored, 1)
                    if j in WARM_UP_SLOTS and new:
                        for sem, value in spare_free:
                            wait(pe, sem, value)
                        warm_up(pe, spare, ident, wo)
                    for kind, i, when in SPARE[j]:
                        if exists[when]:
                            pass_through_spare(kind, i, when)
                            sums.rest()
                    sums.rest()

            over_batches(pe, body)

        @block.scalar
        def _(act):
            act.preload_act_table_set("natural_log_exp_and_others")
            act.wait_ge(consts, 1)

            def body(b, new, ahead, old):
                for j in range(NU):
                    n = b * NU + j
                    if new:
                        act.wait_ge(scored, n + 1)
                        act.activation(e[:, j % 2, :], psS[j % 2], ACT.Exp).then_inc(exp_done, 1)
                        act.wait_ge(exp_done, n + 1)
                        act.activation(e[:, j % 2, :], e[:, j % 2, :], ACT.Ln, bias=1.0).then_inc(ln_done, 1)
                    if ahead and j == 7:
                        act.wait_ge(norm_taken, b + 2)
                        act.activation(ksq[:], ksq[:], ACT.Ln).then_inc(ln_k, 1)
                        act.wait_ge(ln_k, b + 2)
                        act.activation(ksq[:], ksq[:], ACT.Exp, scale=-0.5, bias=ln_quarter[:, 0:1]).then_inc(knorm_ready, 1)
                    for kind, i, when in SPARE[j]:
                        if kind == "turn" and old:
                            act.wait_ge(turn_done, (b - 1) * 4 + i + 1)
                            wait(act, out_done, b - 1)
                            act.activation(ctxT[:, i // 2, 4 * (i % 2):4 * (i % 2) + 4, :],
                                           spare.rearrange("p (k n) -> p k n", k=4), ACT.Copy).then_inc(turn_taken, 1)
                    if j % SILU_EVERY == SILU_EVERY - 1:
                        those = [v for v in range(j - SILU_FROM, j - SILU_TO + 1) if (new if v >= 0 else old)]
                        if those:
                            for v in those:
                                wu = w[:, v % RING, :]
                                act.wait_ge(masked, b * NU + v + 1)
                                act.activation(wu, wu, ACT.Silu, scale=SILU_SCALE).then_inc(silu_done, 1)
                            act.preload_act_table_set("natural_log_exp_and_others")

            over_batches(act, body)

        @block.gpsimd
        def _(pool):
            pool.wait_ge(consts, 1)

            def head_rows(g, first, last):
                for u in range(8 * g + first, 8 * g + last):
                    ins = pool.tensor_scalar(kT_head[:, u, :], kT[:, g, :], head_mask[:, u % 8:u % 8 + 1], 1.0,
                                             ALU.mult, ALU.mult)
                    if u % 8 == 7:
                        ins.then_inc(kheads_ready, 1)

            def body(b, new, ahead, old):
                for j, taken_unit in enumerate(units(b, TAKE_LAG, new, old)):
                    if new:
                        alone(pool, softplus_done, b * NU + j + 1, passed)
                        for part in (w[:, j % RING, 0:K1].rearrange("p (r t) -> p r t", r=BR)[:, :, 0:P],
                                     w[:, j % RING, K1:UNIT].rearrange("p (r t) -> p r t", r=BR)):
                            ins = pool.affine_select(out=part, in_=part, compare_op=ALU.is_ge, fill=0.0, base=0,
                                                     pattern=[[0, BR], [1, P]], channel_multiplier=-1)
                        ins.then_inc(masked, 1)
                    for kind, i, when in SPARE[j]:
                        if kind in "qk" and (new if when == HERE else ahead):
                            g = 0 if when == AHEAD else 1
                            r = rotations(b, kind, i, when)
                            out = kT[:, i, :] if kind == "k" else qT[:, g, i, :]
                            alone(pool, rot_made, r + 1, passed)
                            if kind == "k":
                                wait_alone(pool, kheads_ready, b * 2 + 2, passed)
                            else:
                                wait_alone(pool, scored, b * NU + (8 if when == AHEAD else 0), passed)
                            pool.tensor_tensor(out, rot[i % 2][:, 0, :], rot[i % 2][:, 1, :], ALU.add).then_inc(rotated, 1)
                            if kind == "k":
                                alone(pool, rotated, r + 1, passed)
                                wait_alone(pool, knormed, b + 1, passed)
                                ins = pool.tensor_tensor(ksq[:, i, :], out, out, ALU.mult)
                                if i == 1:
                                    ins.then_inc(ksq_ready, 1)
                    if new and j < 4:
                        if j == 0:
                            wait_alone(pool, scored, b * NU, passed)
                            alone(pool, knormed, b + 1, passed)
                        head_rows(1, 2 * j, 2 * j + 2)
                    if ahead and j == 8:
                        alone(pool, knorm_ready, b + 2, passed)
                        pool.tensor_tensor(kT[:], kT[:], ksq[:], ALU.mult).then_inc(knormed, 1)
                    if ahead and 9 <= j < 13:
                        if j == 9:
                            wait_alone(pool, scored, b * NU + 8, passed)
                            alone(pool, knormed, b + 2, passed)
                        head_rows(0, 2 * (j - 9), 2 * (j - 9) + 2)
                    if taken_unit and taken_unit[0] % 4 == 3:
                        u, n = taken_unit
                        bb = b if j >= TAKE_LAG else b - 1
                        n4 = bb * 4 + u // 4
                        heads = slice(u - 3, u + 1)
                        alone(pool, ctx_taken, n + 1, passed)
                        wait_alone(pool, turn_done, bb * 4, passed)
                        c4 = ctxn[:].rearrange("p t (r h) d -> p t r h d", r=BR)
                        for t in range(TT):
                            ins = pool.tensor_tensor(c4[:, t, :, heads, :], ctx[:, BR * t:BR * t + BR, heads, 0:DH],
                                                     vnull[:, :, heads, :], ALU.add)
                        ins.then_inc(null_added, 1)
                        alone(pool, null_added, n4 + 1, passed)
                        alone(pool, inverted, n4 + 1, passed)
                        c3 = ctxn[:].rearrange("p t (r h) d -> p (t r) h d", r=BR)[:, :, heads, :]
                        pool.tensor_tensor(c3, c3, total[:, :, heads].unsqueeze(3).to_broadcast([P, TT * BR, 4, DH]),
                                           ALU.mult).then_inc(ctx_ready, 1)
                    if old and j == 12:
                        x_b = x_all[:, bass.ds((b - 1) * TT, TT), :]
                        pool.tensor_tensor(x_b, x_b, bo[:, 0:1, :].to_broadcast([P, TT, D]), ALU.add).then_inc(x_biased, 1)

            over_batches(pool, body)

        @block.vector
        def _(dve):
            dve.wait_ge(loaded, 16 * len(loads))
            step = Steps(dve, own)
            step.did(dve.memset(ln_quarter[:], math.log(0.25)))
            step.did(dve.memset(v1[:, :, :, DH:DH + 1], 1.0))
            step.link(dve.tensor_scalar(sinks[:], sinks[:], SILU_SCALE, None, ALU.mult))
            by_head = sinks[:].rearrange("p (r h) -> p r h", r=BR)
            step.did(dve.tensor_scalar(sinks_eps[:], by_head, 1e-6 * SILU_SCALE, None, ALU.add))
            step.did(dve.tensor_tensor(vnull[:], vnull[:], by_head.unsqueeze(3).to_broadcast([P, BR, NH, DH]), ALU.mult))
            step.link(dve.tensor_tensor(bo[:, 0:2, :], bo[:, 0:2, :], bo[:, 2:4, :], ALU.add))
            step.link(dve.tensor_tensor(bo[:, 0, :], bo[:, 0, :], bo[:, 1, :], ALU.add))
            dve.tensor_scalar(bo[:, 0, :], bo[:, 0, :], 1.0 / BR, None, ALU.mult).then_inc(consts, 1)
            dve.wait_ge(consts, 1)

            def take_from_spare(b, kind, i, when):
                bb = b + 1 if when == AHEAD else b
                if kind in "qk":
                    r = rotations(b, kind, i, when)
                    bias, col = (bk, i) if kind == "k" else (bq, 2 * i + (0 if when == AHEAD else 1))
                    ps = spare.rearrange("p (v t) -> p v t", v=2)
                    dve.wait_ge(projected, r + 1)
                    wait(dve, rotated, r - 1)
                    for v in range(2):
                        ins = dve.scalar_tensor_tensor(rot[i % 2][:, v, :], ps[:, v, :], bias[:, v, col:col + 1],
                                                       rope[:, v, :], ALU.add, ALU.mult)
                    ins.then_inc(rot_made, 1)
                elif kind == "v":
                    dve.wait_ge(v_done, bb + 1)
                    wait(dve, summed, b * NU)
                    for t in range(TT):
                        ins = dve.tensor_tensor(v1[:, t, :, 0:DH], spare[:, t * D:(t + 1) * D].rearrange("p (h d) -> p h d", d=DH),
                                                bv[:].rearrange("p (h d) -> p h d", d=DH), ALU.add)
                    ins.then_inc(v_taken, 1)
                elif kind == "norm":
                    dve.wait_ge(norm_done, bb + 1)
                    dve.tensor_scalar(ksq[:].rearrange("p g t -> p (g t)"), spare, 1e-6, None, ALU.max).then_inc(norm_taken, 1)
                elif kind == "out":
                    dve.wait_ge(out_done, b)
                    dve.wait_ge(x_biased, b)
                    x_b = x_all[:, bass.ds((b - 1) * TT, TT), :]
                    dve.scalar_tensor_tensor(x_b, spare.rearrange("p (t d) -> p t d", t=TT), 1.0 / BR, x_b,
                                             ALU.mult, ALU.add).then_inc(out_taken, 1)

            def body(b, new, ahead, old):
                exists = {HERE: new, AHEAD: ahead, OLD: old}
                below_sink, taken = list(units(b, THRESHOLD_LAG, new, old)), list(units(b, TAKE_LAG, new, old))
                for j in range(NU):
                    if new:
                        dve.wait_ge(ln_done, b * NU + j + 1)
                        wait(dve, summed, b * NU + j - RING + 1)
                        dve.scalar_tensor_tensor(w[:, j % RING, :], e[:, j % 2, :], CAP, psS[j % 2],
                                                 ALU.min, ALU.max).then_inc(softplus_done, 1)
                    for kind, i, when in SPARE[j]:
                        if exists[when]:
                            take_from_spare(b, kind, i, when)
                    if taken[j]:
                        u, n = taken[j]
                        dve.wait_ge(summed, n + 1)
                        bb = b if j >= TAKE_LAG else b - 1
                        if u % 4 == 0:
                            wait(dve, null_added, bb * 4)
                        dve.tensor_copy(ctx[:, :, u, :], psO.rearrange("p (r d) -> p r d", d=DH + 1))\
                           .then_inc(ctx_taken, 1)
                        if u % 4 == 3:
                            n4 = bb * 4 + u // 4
                            heads = slice(u - 3, u + 1)
                            dve.wait_ge(ctx_taken, n + 1)
                            wait(dve, ctx_ready, bb * 4)
                            for t in range(TT):
                                ins = dve.tensor_tensor(total[:, BR * t:BR * t + BR, heads],
                                                        ctx[:, BR * t:BR * t + BR, heads, DH], sinks_eps[:, :, heads], ALU.add)
                            ins.then_inc(totalled, 1)
                            dve.wait_ge(totalled, n4 + 1)
                            dve.reciprocal(total[:, :, heads], total[:, :, heads]).then_inc(inverted, 1)
                    if below_sink[j]:
                        u, n = below_sink[j]
                        dve.wait_ge(silu_done, n + 1)
                        for r in range(BR):
                            for part in (w[:, u % RING, r * T:(r + 1) * T], w[:, u % RING, K1 + r * P:K1 + (r + 1) * P]):
                                ins = dve.scalar_tensor_tensor(part, part, sinks[:, r * NH + u:r * NH + u + 1], part,
                                                               ALU.is_ge, ALU.mult)
                        ins.then_inc(weights_done, 1)

            over_batches(dve, body)


FOCUS_EPS = 1e-6
XH = 16
HEADS_IN_CHUNK = P // (D // XH)


def linear_attention(nc, norm, x_all, xnT_all, ident, psum, a):
    with ExitStack() as stack:
        s = Scope(nc, stack, "x0")
        wq, wk, wv = (s.sb(n, [P, CC, D]) for n in ("wq", "wk", "wv"))
        bq, bk, bv = (s.sb(n, [P, D]) for n in ("bq", "bk", "bv"))
        inv_scale = s.sb("inv_scale", [P, D])
        scale_e = s.sb("scale_e", [P, D])
        same_head = s.sb("same_head", [P, P])
        head_mask = s.sb("head_mask", [P, HEADS_IN_CHUNK])
        xnT, ctxT = s.sb("xnT", [P, CC, T]), s.sb("ctxT", [P, CC, T])
        f, f2, f3 = (s.sb(n, [P, 2 * TT, D]) for n in ("f", "f2", "f3"))
        norm2, norm6, factor = (s.sb(n, [P, 2 * TT]) for n in ("norm2", "norm6", "factor"))
        v1 = s.sb("v1", [P, TT, CC, P + 1])
        KVW = P + HEADS_IN_CHUNK
        kv = s.sb("kv", [P, CC, KVW])
        qT = s.sb("qT", [P, CC, T])
        z = s.sb("z", [P, TT, CC, HEADS_IN_CHUNK])
        o = s.sb("o", [P, TT, D])
        loaded, x_here, ctx_here = s.sem("loaded"), s.sem("x_here"), s.sem("ctx_here")
        consts, own_dve, own_setup = s.sem("consts"), s.sem("own_dve"), s.sem("own_setup")
        projected, taken, features_raw = s.sem("projected"), s.sem("taken"), s.sem("features_raw")
        squared, cubed, sixth, ratio_ready, factor_ready = (
            s.sem(n) for n in ("squared", "cubed", "sixth", "ratio_ready", "factor_ready"))
        features, kv_summed, kv_ready = s.sem("features"), s.sem("kv_summed"), s.sem("kv_ready")
        q_turned, qT_ready, out_ready, out_taken = (s.sem(n) for n in ("q_turned", "qT_ready", "out_ready", "out_taken"))
        own_act = s.sem("own_act")
        loads = [(wq[:], chunked(a["wq"])), (wk[:], chunked(a["wk"])), (wv[:], chunked(a["wv"])),
                 (bq[:], over_partitions(a["bq"], D)), (bk[:], over_partitions(a["bk"], D)),
                 (bv[:], over_partitions(a["bv"], D)), (inv_scale[:], over_partitions(a["scale"], D)),
                 (same_head[:], a["same_head"]), (head_mask[:], a["head_mask"])]
        normalise(nc, norm, x_all, xnT_all, ident, psum, loads, loaded)
        block = stack.enter_context(nc.Block())

        @block.sync
        def _(sp):
            with sp.Fori(0, B) as b:
                sp.wait_ge(projected, b * 3)
                sp.dma_start(xnT[:], xnT_all[:, bass.ds(b, 1), :, :]).then_inc(x_here, 16)
                sp.dma_start(ctxT[:], a["ctxT"][bass.ds(b * D, D), :].rearrange("(k p) n -> p k n", p=P))\
                  .then_inc(ctx_here, 16)

        @block.tensor
        def _(pe):
            pe.wait_ge(loaded, 16 * len(loads))
            with pe.Fori(0, B) as b:
                pe.wait_ge(x_here, b * 16 + 16)
                pe.wait_ge(ctx_here, b * 16 + 16)
                pe.wait_ge(out_taken, b)
                for n, (src, weights) in enumerate(((ctxT, wk), (xnT, wq), (ctxT, wv))):
                    for t in range(TT):
                        for c in range(CC):
                            ins = pe.matmul(psum[:, n, t * D:(t + 1) * D], src[:, c, t * P:(t + 1) * P], weights[:, c, :],
                                            start=(c == 0), stop=(c == CC - 1))
                    ins.then_inc(projected, 1)
                pe.wait_ge(features, b + 1)
                for c in range(CC):
                    for t in range(TT):
                        ins = pe.matmul(psum[:, 3, c * (P + 1):(c + 1) * (P + 1)], f3[:, TT + t, c * P:(c + 1) * P],
                                        v1[:, t, c, :], start=(t == 0), stop=(t == TT - 1))
                ins.then_inc(kv_summed, 1)
                for c in range(CC):
                    for t in range(TT):
                        ins = pe.transpose(psum[:, 4, c * T + t * P:c * T + (t + 1) * P], f3[:, t, c * P:(c + 1) * P],
                                           ident[:])
                ins.then_inc(q_turned, 1)
                pe.wait_ge(kv_ready, b + 1)
                pe.wait_ge(qT_ready, b + 1)
                for t in range(TT):
                    for c in range(CC):
                        ins = pe.matmul(psum[:, 5 + t, c * KVW:(c + 1) * KVW], qT[:, c, t * P:(t + 1) * P], kv[:, c, :],
                                        start=True, stop=True)
                ins.then_inc(out_ready, 1)

        @block.scalar
        def _(act):
            act.wait_ge(consts, 1)
            step = Steps(act, own_act)
            act.preload_act_table_set("natural_log_exp_and_others")
            step.link(act.activation(scale_e[:], scale_e[:], ACT.Exp))
            step.link(act.activation(scale_e[:], scale_e[:], ACT.Ln, bias=1.0))
            act.preload_act_table_set("sqrt_and_others")
            with act.Fori(0, B) as b:
                act.wait_ge(features_raw, b + 1)
                for i in range(2 * TT):
                    ins = act.activation(f2[:, i, :], f[:, i, :], ACT.Square, accum_out=norm2[:, i:i + 1])
                ins.then_inc(squared, 1)
                act.wait_ge(cubed, b + 1)
                act.wait_ge(squared, b + 1)
                for i in range(2 * TT):
                    ins = act.activation(f2[:, i, :], f3[:, i, :], ACT.Square, accum_out=norm6[:, i:i + 1])
                ins.then_inc(sixth, 1)
                act.wait_ge(ratio_ready, b + 1)
                act.activation(factor[:], factor[:], ACT.Sqrt).then_inc(factor_ready, 1)
                act.wait_ge(q_turned, b + 1)
                act.activation(qT[:], psum[:, 4, :].rearrange("p (c t) -> p c t", c=CC), ACT.Copy).then_inc(qT_ready, 1)

        @block.vector
        def _(dve):
            dve.wait_ge(loaded, 16 * len(loads))
            step = Steps(dve, own_setup)
            step.did(dve.memset(v1[:, :, :, P:P + 1], 1.0))
            dve.tensor_scalar(scale_e[:], inv_scale[:], CAP, None, ALU.min).then_inc(consts, 1)
            dve.wait_ge(own_act, 2)
            step.link(dve.tensor_tensor(inv_scale[:], inv_scale[:], scale_e[:], ALU.max))
            step.link(dve.reciprocal(inv_scale[:], inv_scale[:]))
            with dve.Fori(0, B) as b:
                step = Steps(dve, own_dve, b * 9, 9)
                step.wait()
                dve.wait_ge(out_taken, b)
                dve.wait_ge(projected, b * 3 + 1)
                bias = lambda v: v[:].unsqueeze(1).to_broadcast([P, TT, D])
                tile = lambda n: psum[:, n, :].rearrange("p (t d) -> p t d", t=TT)
                step.did(dve.tensor_tensor(f[:, TT:2 * TT, :], tile(0), bias(bk), ALU.add))
                dve.wait_ge(projected, b * 3 + 2)
                step.link(dve.tensor_tensor(f[:, 0:TT, :], tile(1), bias(bq), ALU.add))
                step.link(dve.tensor_scalar(f[:], f[:], 0.0, FOCUS_EPS, ALU.max, ALU.add))
                dve.tensor_tensor(f[:], f[:], inv_scale[:].unsqueeze(1).to_broadcast([P, 2 * TT, D]), ALU.mult)\
                   .then_inc(features_raw, 1)
                dve.wait_ge(projected, b * 3 + 3)
                for t in range(TT):
                    step.did(dve.tensor_tensor(v1[:, t, :, 0:P], psum[:, 2, t * D:(t + 1) * D].rearrange("p (c d) -> p c d", c=CC),
                                               bv[:].rearrange("p (c d) -> p c d", c=CC), ALU.add))
                dve.wait_ge(squared, b + 1)
                dve.wait_ge(features_raw, b + 1)
                dve.tensor_tensor(f3[:], f2[:], f[:], ALU.mult).then_inc(cubed, 1)
                dve.wait_ge(sixth, b + 1)
                step.link(dve.reciprocal(factor[:], norm6[:]))
                dve.tensor_tensor(factor[:], factor[:], norm2[:], ALU.mult).then_inc(ratio_ready, 1)
                dve.wait_ge(factor_ready, b + 1)
                dve.wait_ge(cubed, b + 1)
                for i in range(2 * TT):
                    ins = dve.tensor_scalar(f3[:, i, :], f3[:, i, :], factor[:, i:i + 1], None, ALU.mult)
                ins.then_inc(features, 1)
                dve.wait_ge(kv_summed, b + 1)
                for c in range(CC):
                    lo = c * (P + 1)
                    dve.tensor_tensor(kv[:, c, 0:P], psum[:, 3, lo:lo + P], same_head[:], ALU.mult)
                    ins = dve.tensor_tensor(kv[:, c, P:KVW], psum[:, 3, lo + P:lo + P + 1].to_broadcast([P, HEADS_IN_CHUNK]),
                                            head_mask[:], ALU.mult)
                ins.then_inc(kv_ready, 1)
                dve.wait_ge(out_ready, b + 1)
                outs = psum[:, 5:5 + TT, 0:CC * KVW].rearrange("p t (c n) -> p t c n", c=CC)
                step.link(dve.tensor_scalar(z[:], outs[:, :, :, P:KVW], FOCUS_EPS, None, ALU.add))
                step.link(dve.reciprocal(z[:], z[:]))
                for t in range(TT):
                    ins = dve.tensor_tensor(o[:, t, :].rearrange("p (c h d) -> p c h d", c=CC, h=HEADS_IN_CHUNK),
                                            outs[:, t, :, 0:P].rearrange("p c (h d) -> p c h d", h=HEADS_IN_CHUNK),
                                            z[:, t].unsqueeze(3).to_broadcast([P, CC, HEADS_IN_CHUNK, P // HEADS_IN_CHUNK]),
                                            ALU.mult)
                step.link(ins)
                x_b = x_all[:, bass.ds(b * TT, TT), :]
                dve.tensor_tensor(x_b, x_b, o[:], ALU.add).then_inc(out_taken, 1)
                step.end()


def scores_softmax_value_order(units):
    for u in range(units + 2):
        if u < units:
            yield "scores", u
        if 1 <= u <= units:
            yield "turn", u - 1
        if u >= 2:
            yield "values", u - 2


def top2(dve, step, v, mask, work, red, rev, groups):
    wide = lambda r: r.unsqueeze(2).to_broadcast([P, groups, 8])
    eq, rest = work
    for rank in range(2):
        src = v if rank == 0 else rest
        step.link(dve.tensor_reduce(red, src, AX.X, ALU.max))
        step.link(dve.tensor_tensor(eq, src, wide(red), ALU.is_equal))
        step.link(dve.tensor_tensor(eq, eq, rev.unsqueeze(1).to_broadcast([P, groups, 8]), ALU.mult))
        step.link(dve.tensor_reduce(red, eq, AX.X, ALU.max))
        step.link(dve.tensor_tensor(eq, eq, wide(red), ALU.is_equal))
        if rank == 0:
            step.did(dve.tensor_copy(mask, eq))
            step.link(dve.scalar_tensor_tensor(rest, eq, -3e38, v, ALU.mult, ALU.add))
        else:
            step.link(dve.tensor_tensor(mask, mask, eq, ALU.add))


TOP2_STEPS = 13


SH, SDH, SE = 16, 64, 8
QK_GROUPS = SH * SDH // P // 2
SG = SH * SE


def switch_attention(nc, norm, x_all, xnT_all, ident, psum, a):
    with ExitStack() as stack:
        s = Scope(nc, stack, "f0")
        loaded = s.sem("loaded")
        pv_all = s.sb("pv_all", [P, TILES, SE * SDH])
        mix_all = s.sb("mix_all", [P, TILES, SG])
        pick_all = s.sb("pick_all", [P, TILES, SG])
        u_all = s.sb("u_all", [P, TILES, SE * SDH])
        wo = s.sb("wo", [P, SE * SDH // P, D])
        xnT = s.sb("xnT", [P, CC, T])

        with ExitStack() as stage:
            g = Scope(nc, stage, "f0g")
            wg, wv = g.sb("wg", [P, CC, 2 * SG]), g.sb("wv", [P, CC, SE * SDH])
            rev = g.sb("rev", [P, 8])
            NG = TT * 2 * SH
            gate, mask, eq, rest = (g.sb(n, [P, NG, 8]) for n in ("gate", "mask", "eq", "rest"))
            sig = g.sb("sig", [P, TT, SG])
            red = g.sb("red", [P, NG])
            x_here, projected, gates_taken, values_taken, sig_ready, own = (
                g.sem(n) for n in ("x_here", "projected", "gates_taken", "values_taken", "sig_ready", "own"))
            chosen = g.sem("chosen")
            loads = [(wg[:], chunked(a["wg"])), (wv[:], chunked(a["wv"])), (rev[:], over_partitions(a["rev"], 8)),
                     (wo[:], chunked(a["wo"]))]
            normalise(nc, norm, x_all, xnT_all, ident, psum, loads, loaded)
            block = stage.enter_context(nc.Block())

            @block.sync
            def _(sp):
                with sp.Fori(0, B) as b:
                    sp.wait_ge(projected, b * 3)
                    sp.dma_start(xnT[:], xnT_all[:, bass.ds(b, 1), :, :]).then_inc(x_here, 16)

            @block.tensor
            def _(pe):
                pe.wait_ge(loaded, 16 * len(loads))
                with pe.Fori(0, B) as b:
                    pe.wait_ge(x_here, b * 16 + 16)
                    pe.wait_ge(gates_taken, b)
                    for t in range(TT):
                        for c in range(CC):
                            ins = pe.matmul(psum[:, 0, t * D:(t + 1) * D], xnT[:, c, t * P:(t + 1) * P], wg[:, c, :],
                                            start=(c == 0), stop=(c == CC - 1))
                    ins.then_inc(projected, 1)
                    pe.wait_ge(values_taken, b)
                    for t in range(TT):
                        for c in range(CC):
                            ins = pe.matmul(psum[:, 1 + t, :], xnT[:, c, t * P:(t + 1) * P], wv[:, c, :],
                                            start=(c == 0), stop=(c == CC - 1))
                        ins.then_inc(projected, 1)

            @block.scalar
            def _(act):
                with act.Fori(0, B) as b:
                    act.wait_ge(projected, b * 3 + 1)
                    act.wait_ge(chosen, b)
                    act.activation(sig[:], psum[:, 0, :].rearrange("p (t n) -> p t n", t=TT)[:, :, 0:SG], ACT.Sigmoid)\
                       .then_inc(sig_ready, 1)
                    act.wait_ge(projected, b * 3 + 3)
                    act.activation(pv_all[:, bass.ds(b * TT, TT), :], psum[:, 1:1 + TT, :], ACT.Copy)\
                       .then_inc(values_taken, 1)

            @block.vector
            def _(dve):
                dve.wait_ge(loaded, 16 * len(loads))
                with dve.Fori(0, B) as b:
                    step = Steps(dve, own, b * TOP2_STEPS, TOP2_STEPS)
                    dve.wait_ge(chosen, b)
                    step.wait()
                    dve.wait_ge(projected, b * 3 + 1)
                    dve.wait_ge(sig_ready, b + 1)
                    dve.tensor_copy(gate[:].rearrange("p g e -> p (g e)"), psum[:, 0, :]).then_inc(gates_taken, 1)
                    dve.wait_ge(gates_taken, b + 1)
                    top2(dve, step, gate[:], mask[:], (eq[:], rest[:]), red[:], rev[:], NG)
                    m = mask[:].rearrange("p (t n) e -> p t (n e)", t=TT)
                    dve.tensor_tensor(mix_all[:, bass.ds(b * TT, TT), :], sig[:], m[:, :, 0:SG], ALU.mult)
                    dve.tensor_copy(pick_all[:, bass.ds(b * TT, TT), :], m[:, :, SG:2 * SG]).then_inc(chosen, 1)
                    step.end()

        with ExitStack() as stage:
            h = Scope(nc, stage, "f0h")
            wq, wk = h.sb("wq", [P, CC, SH * SDH]), h.sb("wk", [P, CC, SH * SDH])
            qT, kT = h.sb("qT", [P, 2 * QK_GROUPS, T]), h.sb("kT", [P, 2 * QK_GROUPS, T])
            pv = h.sb("pv", [P, TT, SE, SDH])
            mix, pick = h.sb("mix", [P, TT, SH, SE]), h.sb("pick", [P, TT, SH, SE])
            HALF = 4
            prod = h.sb("prod", [P, HALF, SE, SDH])
            v = [h.sb(f"v{i}", [P, TT, SH, SDH]) for i in range(2)]
            weights = [h.sb(f"weights{i}", [P, TT, T]) for i in range(2)]
            turned_w = [h.sb(f"turned_w{i}", [P, TT, T]) for i in range(2)]
            negmax, sums = h.sb("negmax", [P, SH, TT]), h.sb("sums", [P, SH, TT])
            pick_s = h.sb("pick_s", [P, 2, TT, SE])
            picked = h.sb("picked", [P, 2, TT, SE, SDH])
            u = h.sb("u", [P, TT, SE, SDH])
            w_loaded, x_here, qk_ready, qk_taken = (h.sem(n) for n in ("w_loaded", "x_here", "qk_ready", "qk_taken"))
            mix_here = h.sem("mix_here")
            v_ready, summed = h.sems("v_ready", 2), h.sems("summed", 2)
            scored, max_ready, exp_done, turned, turned_taken, out_taken = (
                h.sem(n) for n in ("scored", "max_ready", "exp_done", "turned", "turned_taken", "out_taken"))
            own_pool, own_dve, passed, u_ready = (h.sem(n) for n in ("own_pool", "own_dve", "passed", "u_ready"))
            block = stage.enter_context(nc.Block())
            PAIRS = B // 2
            QK_BANKS = (0, 1, 2, 3, 4)
            NQK = 2 * QK_GROUPS

            @block.sync
            def _(sp):
                sp.dma_start(wq[:], chunked(a["wq"])).then_inc(w_loaded, 16)
                sp.dma_start(wk[:], chunked(a["wk"])).then_inc(w_loaded, 16)
                with sp.Fori(0, PAIRS) as pair:
                    for i in range(2):
                        b = pair * 2 + i
                        sp.wait_ge(v_ready[1 - i], pair + i)
                        sp.dma_start(pv[:].rearrange("p t e d -> p t (e d)"), pv_all[:, bass.ds(b * TT, TT), :])\
                          .then_inc(mix_here, 16)
                        sp.dma_start(mix[:].rearrange("p t h e -> p t (h e)"), mix_all[:, bass.ds(b * TT, TT), :])\
                          .then_inc(mix_here, 16)
                        sp.wait_ge(qk_ready, b * NQK)
                        sp.dma_start(xnT[:], xnT_all[:, bass.ds(b, 1), :, :]).then_inc(x_here, 16)

            @block.gpsimd
            def _(pool):
                per = TT * (SH // HALF) * 4 - 1
                with pool.Fori(0, PAIRS) as pair:
                    step = Steps(pool, own_pool, pair * 2 * per, 2 * per)
                    for i in range(2):
                        alone(pool, mix_here, pair * 64 + 32 * i + 32, passed)
                        alone(pool, summed[i], pair * SH, passed)
                        alone(pool, v_ready[1 - i], pair + i, passed)
                        for t in range(TT):
                            for h0 in range(0, SH, HALF):
                                alone(pool, own_pool, step.base + step.n, passed)
                                step.did(pool.tensor_tensor(
                                    prod[:], pv[:, t].unsqueeze(1).to_broadcast([P, HALF, SE, SDH]),
                                    mix[:, t, h0:h0 + HALF, :].unsqueeze(3).to_broadcast([P, HALF, SE, SDH]), ALU.mult))
                                for half in (4, 2, 1):
                                    alone(pool, own_pool, step.base + step.n, passed)
                                    out = (prod[:, :, 0:half, :] if half > 1
                                           else v[i][:, t, h0:h0 + HALF, :].unsqueeze(2))
                                    ins = pool.tensor_tensor(out, prod[:, :, 0:half, :], prod[:, :, half:2 * half, :],
                                                             ALU.add)
                                    if half > 1 or t < TT - 1 or h0 + HALF < SH:
                                        step.did(ins)
                        ins.then_inc(v_ready[i], 1)
                    step.end()

            @block.tensor
            def _(pe):
                pe.wait_ge(w_loaded, 32)
                with pe.Fori(0, PAIRS) as pair:
                    for i in range(2):
                        S0 = pair * 2 * SH + i * SH
                        Q0 = pair * 2 * NQK + i * NQK
                        pe.wait_ge(x_here, pair * 32 + 16 * i + 16)
                        pe.wait_ge(out_taken, S0)
                        for n in range(NQK):
                            w, m = (wq, wk)[n % 2], n // 2
                            bank = psum[:, QK_BANKS[n % 5], :]
                            if n >= 5:
                                pe.wait_ge(qk_taken, Q0 + n - 4)
                            for j in range(2):
                                lo = (2 * m + j) * P
                                for c in range(CC):
                                    ins = pe.matmul(bank[:, j * T:(j + 1) * T], w[:, c, lo:lo + P], xnT[:, c, :],
                                                    start=(c == 0), stop=(c == CC - 1))
                            ins.then_inc(qk_ready, 1)
                        for what, k in scores_softmax_value_order(SH):
                            r0 = SDH * (k % 2)
                            if what == "scores":
                                if k == 0:
                                    pe.wait_ge(qk_taken, Q0 + NQK)
                                if k >= 2:
                                    pe.wait_ge(exp_done, S0 + k - 1)
                                for t in range(TT):
                                    ins = pe.matmul(psum[:, 6 + k % 2, t * T:(t + 1) * T],
                                                    qT[r0:r0 + SDH, k // 2, t * P:(t + 1) * P], kT[r0:r0 + SDH, k // 2, :],
                                                    start=True, stop=True)
                                ins.then_inc(scored, 1)
                            elif what == "turn":
                                pe.wait_ge(exp_done, S0 + k + 1)
                                if k >= 2:
                                    pe.wait_ge(turned_taken, S0 + k - 1)
                                for j in range(TT):
                                    for t in range(TT):
                                        lo = j * T + t * P
                                        ins = pe.transpose(psum[:, 4 + k % 2, lo:lo + P],
                                                           weights[k % 2][:, t, j * P:(j + 1) * P], ident[:])
                                ins.then_inc(turned, 1)
                            else:
                                if k == 0:
                                    pe.wait_ge(v_ready[i], pair + 1)
                                pe.wait_ge(turned_taken, S0 + k + 1)
                                if k >= 4:
                                    pe.wait_ge(out_taken, S0 + k - 3)
                                for t in range(TT):
                                    for j in range(TT):
                                        ins = pe.matmul(psum[:, k % 4, t * SDH:(t + 1) * SDH],
                                                        turned_w[k % 2][:, j, t * P:(t + 1) * P], v[i][:, j, k, :],
                                                        start=(j == 0), stop=(j == TT - 1))
                                ins.then_inc(summed[i], 1)

            @block.scalar
            def _(act):
                with act.Fori(0, PAIRS) as pair:
                  for i in range(2):
                    b = pair * 2 + i
                    for n in range(NQK):
                        act.wait_ge(qk_ready, b * NQK + n + 1)
                        dst, m = (qT, kT)[n % 2], n // 2
                        act.activation(dst[:, 2 * m:2 * m + 2, :], psum[:, QK_BANKS[n % 5], :].rearrange("p (j t) -> p j t", j=2),
                                       ACT.Copy, scale=(SDH ** -0.5 if n % 2 == 0 else 1.0)).then_inc(qk_taken, 1)

                    def exps(k):
                        act.wait_ge(max_ready, b * SH + k + 1)
                        if k >= 2:
                            act.wait_ge(turned, b * SH + k - 1)
                        for t in range(TT):
                            ins = act.activation(weights[k % 2][:, t, :], psum[:, 6 + k % 2, t * T:(t + 1) * T], ACT.Exp,
                                                 bias=negmax[:, k, t:t + 1], accum_out=sums[:, k, t:t + 1])
                        ins.then_inc(exp_done, 1)

                    def take_turned(k):
                        act.wait_ge(turned, b * SH + k + 1)
                        if k >= 2:
                            act.wait_ge(summed[i], pair * SH + k - 1)
                        act.activation(turned_w[k % 2][:], psum[:, 4 + k % 2, :].rearrange("p (j t) -> p j t", j=TT),
                                       ACT.Copy).then_inc(turned_taken, 1)

                    for k in range(SH):
                        exps(k)
                        if k >= 1:
                            take_turned(k - 1)
                    take_turned(SH - 1)

            @block.vector
            def _(dve):
                per = 3 * SH
                with dve.Fori(0, PAIRS) as pair:
                    step = Steps(dve, own_dve, pair * 2 * per, 2 * per)
                    for i in range(2):
                        b = pair * 2 + i
                        S0 = b * SH
                        step.wait()
                        dve.wait_ge(u_ready, b)
                        step.link(dve.tensor_copy(pick[:].rearrange("p t h e -> p t (h e)"),
                                                  pick_all[:, bass.ds(b * TT, TT), :]))

                        def row_max(k):
                            dve.wait_ge(scored, S0 + k + 1)
                            dve.tensor_reduce(negmax[:, k, :], psum[:, 6 + k % 2, :].rearrange("p (t j) -> p t j", t=TT),
                                              AX.X, ALU.max, negate=True).then_inc(max_ready, 1)

                        def to_experts(k):
                            dve.wait_ge(exp_done, S0 + k + 1)
                            step.link(dve.reciprocal(sums[:, k, :], sums[:, k, :]))
                            step.link(dve.tensor_tensor(pick_s[:, k % 2], pick[:, :, k, :],
                                                        sums[:, k, :].unsqueeze(2).to_broadcast([P, TT, SE]), ALU.mult))
                            dve.wait_ge(summed[i], pair * SH + k + 1)
                            for t in range(TT):
                                ins = dve.tensor_tensor(
                                    u[:, t] if k == 0 else picked[:, k % 2, t],
                                    psum[:, k % 4, t * SDH:(t + 1) * SDH].unsqueeze(1).to_broadcast([P, SE, SDH]),
                                    pick_s[:, k % 2, t].unsqueeze(2).to_broadcast([P, SE, SDH]), ALU.mult)
                            ins.then_inc(out_taken, 1)
                            dve.wait_ge(out_taken, S0 + k + 1)
                            if k:
                                step.did(dve.tensor_tensor(u[:], u[:], picked[:, k % 2], ALU.add))

                        for k in range(SH):
                            row_max(k)
                            if k >= 2:
                                to_experts(k - 2)
                        to_experts(SH - 2)
                        to_experts(SH - 1)
                        step.wait()
                        dve.tensor_copy(u_all[:, bass.ds(b * TT, TT), :], u[:].rearrange("p t e d -> p t (e d)"))\
                           .then_inc(u_ready, 1)
                    step.end()

        with ExitStack() as stage:
            o = Scope(nc, stage, "f0o")
            KO = SE * SDH // P
            u_b = o.sb("u", [P, TT, SE * SDH])
            uT = o.sb("uT", [P, TT, KO, P])
            u_here, turned, taken, out_ready, out_taken = (
                o.sem(n) for n in ("u_here", "turned", "taken", "out_ready", "out_taken"))
            block = stage.enter_context(nc.Block())

            @block.sync
            def _(sp):
                with sp.Fori(0, B) as b:
                    sp.wait_ge(turned, b * TT)
                    sp.dma_start(u_b[:], u_all[:, bass.ds(b * TT, TT), :]).then_inc(u_here, 16)

            @block.tensor
            def _(pe):
                with pe.Fori(0, B) as b:
                    pe.wait_ge(u_here, b * 16 + 16)
                    pe.wait_ge(taken, b * TT)
                    for t in range(TT):
                        for k in range(KO):
                            ins = pe.transpose(psum[:, t, k * P:(k + 1) * P], u_b[:, t, k * P:(k + 1) * P], ident[:])
                        ins.then_inc(turned, 1)
                    pe.wait_ge(taken, b * TT + TT)
                    pe.wait_ge(out_taken, b)
                    for t in range(TT):
                        for k in range(KO):
                            ins = pe.matmul(psum[:, 2, t * D:(t + 1) * D], uT[:, t, k, :], wo[:, k, :],
                                            start=(k == 0), stop=(k == KO - 1))
                    ins.then_inc(out_ready, 1)

            @block.scalar
            def _(act):
                with act.Fori(0, B) as b:
                    act.wait_ge(out_ready, b)
                    for t in range(TT):
                        act.wait_ge(turned, b * TT + t + 1)
                        act.activation(uT[:, t], psum[:, t, :].rearrange("p (k n) -> p k n", k=KO), ACT.Copy)\
                           .then_inc(taken, 1)

            @block.vector
            def _(dve):
                with dve.Fori(0, B) as b:
                    dve.wait_ge(out_ready, b + 1)
                    x_b = x_all[:, bass.ds(b * TT, TT), :]
                    dve.tensor_tensor(x_b, psum[:, 2, :].rearrange("p (t d) -> p t d", t=TT), x_b, ALU.add)\
                       .then_inc(out_taken, 1)


def turn_and_project(pe, psum, ident, o, oT, w, turned, turned_taken, out_ready, b, chunks):
    for t in range(TT):
        for g in range(chunks // 4):
            for i in range(4):
                lo = (4 * g + i) * P
                ins = pe.transpose(psum[:, 2 * t + g, i * P:(i + 1) * P], o[:, t, lo:lo + P], ident[:])
            ins.then_inc(turned, 1)
    pe.wait_ge(turned_taken, b * 4 + 4)
    for t in range(TT):
        for k in range(chunks):
            ins = pe.matmul(psum[:, 4, t * D:(t + 1) * D], oT[:, t, k, :], w[:, k, :], start=(k == 0),
                            stop=(k == chunks - 1))
    ins.then_inc(out_ready, 1)


def take_turned_output(act, psum, oT, turned, turned_taken, b):
    for n in range(4):
        act.wait_ge(turned, b * 4 + n + 1)
        act.activation(oT[:, n // 2, 4 * (n % 2):4 * (n % 2) + 4, :], psum[:, n, :].rearrange("p (k n) -> p k n", n=P),
                       ACT.Copy).then_inc(turned_taken, 1)


AH, AD = 8, 128
KEYS, CTX = 1024, 192
KB = KEYS // P
SHARPEN = 1.5


def attention1(nc, norm, x_all, xnT_all, ident, psum, a):
    with ExitStack() as stack:
        s = Scope(nc, stack, "a1")
        wq, wo = s.sb("wq", [P, CC, AH * AD]), s.sb("wo", [P, AH, D])
        wk, wv = s.sb("wk", [P, 2, AH * AD]), s.sb("wv", [P, 2, AH * AD])
        bo = s.sb("bo", [P, D])
        ctxT = s.sb("ctxT", [P, 2, KEYS])
        kT, v = s.sb("kT", [P, AH, KEYS]), s.sb("v", [P, KB, AH * AD])
        xnT, qT = s.sb("xnT", [P, CC, T]), s.sb("qT", [P, AH, T])
        weights = [s.sb(f"weights{i}", [P, KEYS]) for i in range(2)]
        turned_w = [s.sb(f"turned_w{i}", [P, KEYS]) for i in range(2)]
        U = AH * TT
        negmax, sums = s.sb("negmax", [P, U]), s.sb("sums", [P, U])
        o, oT = s.sb("o", [P, TT, AH * AD]), s.sb("oT", [P, TT, AH, P])
        loaded, x_here = s.sem("loaded"), s.sem("x_here")
        kv_ready, kv_act, kv_dve = s.sem("kv_ready"), s.sem("kv_act"), s.sem("kv_dve")
        q_ready, q_taken, scored, max_ready, exp_done, turned = (
            s.sem(n) for n in ("q_ready", "q_taken", "scored", "max_ready", "exp_done", "turned"))
        half_taken = s.sems("half_taken", 2)
        summed, head_taken, own = s.sem("summed"), s.sem("head_taken"), s.sem("own")
        o_turned, o_turned_taken, out_ready, out_taken = (
            s.sem(n) for n in ("o_turned", "o_turned_taken", "out_ready", "out_taken"))
        loads = []
        for dst, src in ((ctxT, a["ctxT"]), (wk, a["wk"]), (wv, a["wv"])):
            loads += [(dst[:, 0, :], src[0:P, :]), (dst[0:CTX - P, 1, :], src[P:CTX, :])]
        loads += [(wq[:], chunked(a["wq"])), (wo[:], chunked(a["wo"])), (bo[:], over_partitions(a["bo"], D))]
        normalise(nc, norm, x_all, xnT_all, ident, psum, loads, loaded)
        block = stack.enter_context(nc.Block())
        HALF = KEYS // 2
        parts = [("k", h, half) for h in range(AH) for half in range(2)] + \
                [("v", st, half) for st in range(KB) for half in range(2)]

        @block.sync
        def _(sp):
            with sp.Fori(0, B) as b:
                sp.wait_ge(q_ready, b * 4)
                sp.dma_start(xnT[:], xnT_all[:, bass.ds(b, 1), :, :]).then_inc(x_here, 16)

        @block.tensor
        def _(pe):
            pe.wait_ge(loaded, 16 * len(loads))
            for n, (kind, i, half) in enumerate(parts):
                if n >= 8:
                    pe.wait_ge((kv_act, kv_dve)[n % 2], (n - 8) // 2 + 1)
                for c, rows in enumerate((P, CTX - P)):
                    if kind == "k":
                        ins = pe.matmul(psum[:, n % 8, :], wk[0:rows, c, i * AD:(i + 1) * AD],
                                        ctxT[0:rows, c, half * HALF:(half + 1) * HALF], start=(c == 0), stop=(c == 1))
                    else:
                        ins = pe.matmul(psum[:, n % 8, :], ctxT[0:rows, c, i * P:(i + 1) * P],
                                        wv[0:rows, c, half * HALF:(half + 1) * HALF], start=(c == 0), stop=(c == 1))
                ins.then_inc(kv_ready, 1)
            pe.wait_ge(kv_act, len(parts) // 2)
            pe.wait_ge(kv_dve, len(parts) // 2)
            with pe.Fori(0, B) as b:
                S0 = b * U
                pe.wait_ge(x_here, b * 16 + 16)
                pe.wait_ge(out_taken, b)
                for m in range(AH // 2):
                    if m >= 2:
                        pe.wait_ge(q_taken, b * 4 + m - 1)
                    for j in range(2):
                        for c in range(CC):
                            lo = (2 * m + j) * AD
                            ins = pe.matmul(psum[:, 6 + m % 2, j * T:(j + 1) * T], wq[:, c, lo:lo + AD], xnT[:, c, :],
                                            start=(c == 0), stop=(c == CC - 1))
                    ins.then_inc(q_ready, 1)
                for what, k in scores_softmax_value_order(U):
                    h, t = k // TT, k % TT
                    if what == "scores":
                        if k == 0:
                            pe.wait_ge(q_taken, b * 4 + 4)
                        if k >= 2:
                            pe.wait_ge(exp_done, S0 + k - 1)
                        for half in range(2):
                            ins = pe.matmul(psum[:, 2 * (k % 2) + half, :], qT[:, h, t * P:(t + 1) * P],
                                            kT[:, h, half * HALF:(half + 1) * HALF], start=True, stop=True)
                        ins.then_inc(scored, 1)
                    elif what == "turn":
                        pe.wait_ge(exp_done, S0 + k + 1)
                        for half in range(2):
                            pe.wait_ge(half_taken[half], S0 + k)
                            for j in range(4):
                                lo = half * HALF + j * P
                                ins = pe.transpose(psum[:, 4 + half, j * P:(j + 1) * P], weights[k % 2][:, lo:lo + P],
                                                   ident[:])
                            ins.then_inc(turned, 1)
                    else:
                        for half in range(2):
                            pe.wait_ge(half_taken[half], S0 + k + 1)
                        if k >= 2:
                            pe.wait_ge(head_taken, S0 + k - 1)
                        for j in range(KB):
                            ins = pe.matmul(psum[:, 6 + k % 2, 0:AD], turned_w[k % 2][:, j * P:(j + 1) * P],
                                            v[:, j, h * AD:(h + 1) * AD], start=(j == 0), stop=(j == KB - 1))
                        ins.then_inc(summed, 1)
                pe.wait_ge(head_taken, S0 + U)
                turn_and_project(pe, psum, ident, o, oT, wo, o_turned, o_turned_taken, out_ready, b, AH)

        def take_context(eng, n, copy, done):
            kind, i, half = parts[n]
            dst = kT[:, i, half * HALF:(half + 1) * HALF] if kind == "k" else v[:, i, half * HALF:(half + 1) * HALF]
            eng.wait_ge(kv_ready, n + 1)
            copy(dst, psum[:, n % 8, :]).then_inc(done, 1)

        @block.scalar
        def _(act):
            for n in range(0, len(parts), 2):
                take_context(act, n, lambda out, in_: act.activation(out, in_, ACT.Copy), kv_act)
            with act.Fori(0, B) as b:
                S0 = b * U
                for m in range(AH // 2):
                    act.wait_ge(q_ready, b * 4 + m + 1)
                    act.activation(qT[:, 2 * m:2 * m + 2, :], psum[:, 6 + m % 2, :].rearrange("p (j t) -> p j t", j=2),
                                   ACT.Copy, scale=SHARPEN * AD ** -0.5).then_inc(q_taken, 1)

                def exps(k):
                    act.wait_ge(max_ready, S0 + k + 1)
                    if k >= 2:
                        act.wait_ge(turned, 2 * (S0 + k - 1))
                    act.activation(weights[k % 2][:], psum[:, 2 * (k % 2):2 * (k % 2) + 2, :].rearrange("p a n -> p (a n)"),
                                   ACT.Exp, bias=negmax[:, k:k + 1], accum_out=sums[:, k:k + 1]).then_inc(exp_done, 1)

                def take_half(k):
                    act.wait_ge(turned, 2 * (S0 + k) + 2)
                    if k >= 2:
                        act.wait_ge(summed, S0 + k - 1)
                    act.activation(turned_w[k % 2][:, HALF:KEYS], psum[:, 5, :], ACT.Copy).then_inc(half_taken[1], 1)

                for k in range(U):
                    exps(k)
                    if k >= 1:
                        take_half(k - 1)
                take_half(U - 1)
                take_turned_output(act, psum, oT, o_turned, o_turned_taken, b)

        @block.vector
        def _(dve):
            for n in range(1, len(parts), 2):
                take_context(dve, n, dve.tensor_copy, kv_dve)
            with dve.Fori(0, B) as b:
                step = Steps(dve, own, b * (U + 1), U + 1)
                S0 = b * U
                dve.wait_ge(out_taken, b)
                x_b = x_all[:, bass.ds(b * TT, TT), :]
                step.did(dve.tensor_tensor(x_b, x_b, bo[:].unsqueeze(1).to_broadcast([P, TT, D]), ALU.add))

                def row_max(k):
                    dve.wait_ge(scored, S0 + k + 1)
                    dve.tensor_reduce(negmax[:, k:k + 1], psum[:, 2 * (k % 2):2 * (k % 2) + 2, :].rearrange("p a n -> p (a n)"),
                                      AX.X, ALU.max, negate=True).then_inc(max_ready, 1)

                def take_half(k):
                    dve.wait_ge(turned, 2 * (S0 + k) + 1)
                    if k >= 2:
                        dve.wait_ge(summed, S0 + k - 1)
                    dve.tensor_copy(turned_w[k % 2][:, 0:HALF], psum[:, 4, :]).then_inc(half_taken[0], 1)

                def take_head(k):
                    h, t = k // TT, k % TT
                    dve.wait_ge(exp_done, S0 + k + 1)
                    step.link(dve.reciprocal(sums[:, k:k + 1], sums[:, k:k + 1]))
                    dve.wait_ge(summed, S0 + k + 1)
                    dve.tensor_scalar(o[:, t, h * AD:(h + 1) * AD], psum[:, 6 + k % 2, 0:AD], sums[:, k:k + 1], None,
                                      ALU.mult).then_inc(head_taken, 1)

                for k in range(U):
                    row_max(k)
                    if k >= 1:
                        take_half(k - 1)
                    if k >= 2:
                        take_head(k - 2)
                take_half(U - 1)
                take_head(U - 2)
                take_head(U - 1)
                step.wait()
                dve.wait_ge(out_ready, b + 1)
                dve.tensor_tensor(x_b, psum[:, 4, :].rearrange("p (t d) -> p t d", t=TT), x_b, ALU.add).then_inc(out_taken, 1)
                step.end()


CH, CD = 16, 64
MASKED = -1e9


def cross_attention1(nc, norm, x_all, xnT_all, ident, psum, a):
    with ExitStack() as stack:
        s = Scope(nc, stack, "x1")
        HD = CH * CD
        TILES_QK = HD // P
        wq, wk, wv = (s.sb(n, [P, CC, HD]) for n in ("wq", "wk", "wv"))
        wo, bo = s.sb("wo", [P, HD // P, D]), s.sb("bo", [P, D])
        mask_i, mask = s.sb("mask_i", [P, TT, T], I32), s.sb("mask", [P, TT, T])
        xnT, ctxT = s.sb("xnT", [P, CC, T]), s.sb("ctxT", [P, CC, T])
        qT, kT = s.sb("qT", [P, TILES_QK, T]), s.sb("kT", [P, TILES_QK, T])
        v = s.sb("v", [P, TT, HD])
        masked_s = [s.sb(f"masked_s{i}", [P, TT, T]) for i in range(2)]
        weights = [s.sb(f"weights{i}", [P, TT, T]) for i in range(2)]
        turned_w = [s.sb(f"turned_w{i}", [P, TT, T]) for i in range(2)]
        rowmax, negmax, sums = (s.sb(n, [P, CH, TT]) for n in ("rowmax", "negmax", "sums"))
        o, oT = s.sb("o", [P, TT, HD]), s.sb("oT", [P, TT, HD // P, P])
        loaded, x_here, ctx_here = s.sem("loaded"), s.sem("x_here"), s.sem("ctx_here")
        projected, v_taken, qk_taken = s.sem("projected"), s.sem("v_taken"), s.sem("qk_taken")
        scored, maxed, max_ready, exp_done, turned, turned_taken, summed, head_taken = (
            s.sem(n) for n in ("scored", "maxed", "max_ready", "exp_done", "turned", "turned_taken", "summed",
                               "head_taken"))
        own, own_setup, passed = s.sem("own"), s.sem("own_setup"), s.sem("passed")
        o_turned, o_turned_taken, out_ready, out_taken = (
            s.sem(n) for n in ("o_turned", "o_turned_taken", "out_ready", "out_taken"))
        loads = [(wv[:], chunked(a["wv"])), (wq[:], chunked(a["wq"])), (wk[:], chunked(a["wk"])),
                 (wo[:], chunked(a["wo"])), (bo[:], over_partitions(a["bo"], D)), (mask_i[:], chunked(a["mask"]))]
        normalise(nc, norm, x_all, xnT_all, ident, psum, loads, loaded)
        block = stack.enter_context(nc.Block())
        order = [("v", 0, 0), ("v", 0, 1), ("v", 1, 0), ("v", 1, 1)] + \
                [(kind, m, 0) for m in range(TILES_QK // 2) for kind in ("q", "k")]
        NP, NV = len(order), 4

        @block.sync
        def _(sp):
            with sp.Fori(0, B) as b:
                sp.wait_ge(projected, b * NP)
                sp.dma_start(ctxT[:], a["ctxT"][bass.ds(b * D, D), :].rearrange("(k p) n -> p k n", p=P))\
                  .then_inc(ctx_here, 16)
                sp.dma_start(xnT[:], xnT_all[:, bass.ds(b, 1), :, :]).then_inc(x_here, 16)

        @block.tensor
        def _(pe):
            pe.wait_ge(loaded, 16 * len(loads))
            with pe.Fori(0, B) as b:
                S0 = b * CH
                pe.wait_ge(ctx_here, b * 16 + 16)
                pe.wait_ge(x_here, b * 16 + 16)
                pe.wait_ge(out_taken, b)
                for n, (kind, m, half) in enumerate(order):
                    if 6 <= n < 6 + NV:
                        pe.wait_ge(v_taken, b * NV + n - 5)
                    elif n >= 6 + NV:
                        pe.wait_ge(qk_taken, b * (NP - NV) + n - 5 - NV)
                    for c in range(CC):
                        if kind == "v":
                            ins = pe.matmul(psum[:, n % 6, :], ctxT[:, c, m * P:(m + 1) * P],
                                            wv[:, c, half * 512:(half + 1) * 512], start=(c == 0), stop=(c == CC - 1))
                    if kind != "v":
                        w, src = (wq, xnT) if kind == "q" else (wk, ctxT)
                        for j in range(2):
                            lo = (2 * m + j) * P
                            for c in range(CC):
                                ins = pe.matmul(psum[:, n % 6, j * T:(j + 1) * T], w[:, c, lo:lo + P], src[:, c, :],
                                                start=(c == 0), stop=(c == CC - 1))
                    ins.then_inc(projected, 1)
                for what, k in scores_softmax_value_order(CH):
                    r0 = CD * (k % 2)
                    if what == "scores":
                        if k == 0:
                            pe.wait_ge(qk_taken, b * (NP - NV) + NP - NV)
                            pe.wait_ge(v_taken, b * NV + NV)
                        if k >= 2:
                            pe.wait_ge(max_ready, S0 + k - 1)
                        for t in range(TT):
                            ins = pe.matmul(psum[:, 6 + k % 2, t * T:(t + 1) * T],
                                            qT[r0:r0 + CD, k // 2, t * P:(t + 1) * P], kT[r0:r0 + CD, k // 2, :],
                                            start=True, stop=True)
                        ins.then_inc(scored, 1)
                    elif what == "turn":
                        pe.wait_ge(exp_done, S0 + k + 1)
                        if k >= 2:
                            pe.wait_ge(turned_taken, S0 + k - 1)
                        for j in range(TT):
                            for t in range(TT):
                                lo = j * T + t * P
                                ins = pe.transpose(psum[:, 4 + k % 2, lo:lo + P], weights[k % 2][:, t, j * P:(j + 1) * P],
                                                   ident[:])
                        ins.then_inc(turned, 1)
                    else:
                        pe.wait_ge(turned_taken, S0 + k + 1)
                        if k >= 4:
                            pe.wait_ge(head_taken, S0 + k - 3)
                        for t in range(TT):
                            for j in range(TT):
                                ins = pe.matmul(psum[:, k % 4, t * CD:(t + 1) * CD],
                                                turned_w[k % 2][:, j, t * P:(t + 1) * P], v[:, j, k * CD:(k + 1) * CD],
                                                start=(j == 0), stop=(j == TT - 1))
                        ins.then_inc(summed, 1)
                pe.wait_ge(head_taken, S0 + CH)
                turn_and_project(pe, psum, ident, o, oT, wo, o_turned, o_turned_taken, out_ready, b, HD // P)

        @block.scalar
        def _(act):
            with act.Fori(0, B) as b:
                S0 = b * CH
                for n in range(NV, NP):
                    kind, m, _ = order[n]
                    act.wait_ge(projected, b * NP + n + 1)
                    act.activation((qT if kind == "q" else kT)[:, 2 * m:2 * m + 2, :],
                                   psum[:, n % 6, :].rearrange("p (j t) -> p j t", j=2), ACT.Copy,
                                   scale=(CD ** -0.5 if kind == "q" else 1.0)).then_inc(qk_taken, 1)

                def exps(k):
                    act.wait_ge(max_ready, S0 + k + 1)
                    if k >= 2:
                        act.wait_ge(turned, S0 + k - 1)
                    for t in range(TT):
                        ins = act.activation(weights[k % 2][:, t, :], masked_s[k % 2][:, t, :], ACT.Exp,
                                             bias=negmax[:, k, t:t + 1], accum_out=sums[:, k, t:t + 1])
                    ins.then_inc(exp_done, 1)

                def take_turned(k):
                    act.wait_ge(turned, S0 + k + 1)
                    if k >= 2:
                        act.wait_ge(summed, S0 + k - 1)
                    act.activation(turned_w[k % 2][:], psum[:, 4 + k % 2, :].rearrange("p (j t) -> p j t", j=TT),
                                   ACT.Copy).then_inc(turned_taken, 1)

                for k in range(CH):
                    exps(k)
                    if k >= 1:
                        take_turned(k - 1)
                take_turned(CH - 1)
                take_turned_output(act, psum, oT, o_turned, o_turned_taken, b)

        @block.vector
        def _(dve):
            dve.wait_ge(loaded, 16 * len(loads))
            step = Steps(dve, own_setup)
            step.link(dve.tensor_copy(mask[:], mask_i[:]))
            step.link(dve.tensor_scalar(mask[:], mask[:], 0.0, MASKED, ALU.is_equal, ALU.mult))
            with dve.Fori(0, B) as b:
                per = CH + 1
                step = Steps(dve, own, b * per, per)
                S0 = b * CH
                dve.wait_ge(out_taken, b)
                x_b = x_all[:, bass.ds(b * TT, TT), :]
                step.did(dve.tensor_tensor(x_b, x_b, bo[:].unsqueeze(1).to_broadcast([P, TT, D]), ALU.add))
                for n in range(NV):
                    _, m, half = order[n]
                    dve.wait_ge(projected, b * NP + n + 1)
                    dve.tensor_copy(v[:, m, half * 512:(half + 1) * 512], psum[:, n, :]).then_inc(v_taken, 1)

                def row_max(k):
                    if k >= 2:
                        dve.wait_ge(exp_done, S0 + k - 1)
                    alone(dve, scored, S0 + k + 1, passed)
                    for t in range(TT):
                        ins = dve.tensor_tensor_reduce(masked_s[k % 2][:, t, :], psum[:, 6 + k % 2, t * T:(t + 1) * T],
                                                       mask[:, t, :], 1.0, -3e38, ALU.add, ALU.max, rowmax[:, k, t:t + 1])
                    ins.then_inc(maxed, 1)
                    dve.wait_ge(maxed, S0 + k + 1)
                    dve.tensor_scalar(negmax[:, k, :], rowmax[:, k, :], -1.0, None, ALU.mult).then_inc(max_ready, 1)

                def take_head(k):
                    dve.wait_ge(exp_done, S0 + k + 1)
                    step.link(dve.reciprocal(sums[:, k, :], sums[:, k, :]))
                    dve.wait_ge(summed, S0 + k + 1)
                    dve.tensor_tensor(o[:, :, k * CD:(k + 1) * CD],
                                      psum[:, k % 4, 0:TT * CD].rearrange("p (t d) -> p t d", t=TT),
                                      sums[:, k, :].unsqueeze(2).to_broadcast([P, TT, CD]), ALU.mult).then_inc(head_taken, 1)

                for k in range(CH):
                    row_max(k)
                    if k >= 2:
                        take_head(k - 2)
                take_head(CH - 2)
                take_head(CH - 1)
                step.wait()
                dve.wait_ge(out_ready, b + 1)
                dve.tensor_tensor(x_b, psum[:, 4, :].rearrange("p (t d) -> p t d", t=TT), x_b, ALU.add).then_inc(out_taken, 1)
                step.end()


HID, NE, NGR = 512, 8, 2
PER_GROUP = NE // NGR


def experts(nc, norm, x_all, xnT_all, ident, psum, a):
    with ExitStack() as stack:
        s = Scope(nc, stack, "f1")
        KH = HID // P
        w_in, w1 = s.sb("w_in", [P, CC, 2 * HID]), s.sb("w1", [P, CC, 2 * HID])
        w_out, w2 = s.sb("w_out", [P, KH, D]), s.sb("w2", [P, KH, NE * D])
        wg = s.sb("wg", [P, CC, NGR + NE])
        bg, rev = s.sb("bg", [P, NGR + NE]), s.sb("rev", [P, NE])
        xnT = s.sb("xnT", [P, CC, T])
        silu = s.sb("silu", [P, 2, T])
        hidden = s.sb("hidden", [P, 2, KH, T])
        logits, top = s.sb("logits", [P, TT, NGR + NE]), s.sb("top", [P, TT, 1 + NGR])
        expd = s.sb("expd", [P, TT, NGR + NE])
        total = s.sb("total", [P, TT, 1 + NGR])
        chosen_group, group_p = s.sb("chosen_group", [P, TT, NGR]), s.sb("group_p", [P, TT])
        p, mask, eq, rest = (s.sb(n, [P, TT, NE]) for n in ("p", "mask", "eq", "rest"))
        red = s.sb("red", [P, TT])
        acc = s.sb("acc", [P, TT, D])
        loaded, x_here, projected, silu_done, hidden_taken = (
            s.sem(n) for n in ("loaded", "x_here", "projected", "silu_done", "hidden_taken"))
        gates_ready, shifted, exp_done, own = s.sem("gates_ready"), s.sem("shifted"), s.sem("exp_done"), s.sem("own")
        routed_ready, routed_taken = s.sem("routed_ready"), s.sem("routed_taken")
        loads = [(wg[:], chunked(a["wg"])), (w_in[:], chunked(a["w_in"])), (w1[:], chunked(a["w1"])),
                 (w_out[:], chunked(a["w_out"])), (w2[:], chunked(a["w2"])), (bg[:], over_partitions(a["bg"], NGR + NE)),
                 (rev[:], over_partitions(a["rev"], NE))]
        normalise(nc, norm, x_all, xnT_all, ident, psum, loads, loaded)
        block = stack.enter_context(nc.Block())
        NHID = 2 * KH
        NR = NE // 2 + 1

        @block.sync
        def _(sp):
            with sp.Fori(0, B) as b:
                sp.wait_ge(projected, b * NHID)
                sp.dma_start(xnT[:], xnT_all[:, bass.ds(b, 1), :, :]).then_inc(x_here, 16)

        @block.tensor
        def _(pe):
            pe.wait_ge(loaded, 16 * len(loads))
            with pe.Fori(0, B) as b:
                pe.wait_ge(x_here, b * 16 + 16)
                pe.wait_ge(shifted, b)
                for t in range(TT):
                    for c in range(CC):
                        ins = pe.matmul(psum[:, 7, t * 16:t * 16 + NGR + NE], xnT[:, c, t * P:(t + 1) * P], wg[:, c, :],
                                        start=(c == 0), stop=(c == CC - 1))
                ins.then_inc(gates_ready, 1)
                for n in range(NHID):
                    w, j = (w_in, w1)[n // KH], n % KH
                    bank = psum[:, 4 + n % 3, :]
                    if n >= 3:
                        pe.wait_ge(hidden_taken, b * NHID + n - 2)
                    else:
                        pe.wait_ge(hidden_taken, b * NHID)
                    for part in range(2):
                        lo = part * HID + j * P
                        for c in range(CC):
                            ins = pe.matmul(bank[:, part * T:(part + 1) * T], w[:, c, lo:lo + P], xnT[:, c, :],
                                            start=(c == 0), stop=(c == CC - 1))
                    ins.then_inc(projected, 1)
                for t in range(TT):
                    for r in range(NR):
                        n = t * NR + r
                        if n >= 4:
                            pe.wait_ge(routed_taken, b * TT * NR + n - 3)
                        else:
                            pe.wait_ge(routed_taken, b * TT * NR)
                        if n == 0:
                            pe.wait_ge(hidden_taken, b * NHID + KH)
                        if n == 1:
                            pe.wait_ge(hidden_taken, b * NHID + NHID)
                        for k in range(KH):
                            if r == 0:
                                ins = pe.matmul(psum[:, n % 4, 0:D], hidden[:, 0, k, t * P:(t + 1) * P], w_out[:, k, :],
                                                start=(k == 0), stop=(k == KH - 1))
                            else:
                                ins = pe.matmul(psum[:, n % 4, :], hidden[:, 1, k, t * P:(t + 1) * P],
                                                w2[:, k, (r - 1) * 512:r * 512], start=(k == 0), stop=(k == KH - 1))
                        ins.then_inc(routed_ready, 1)

        @block.scalar
        def _(act):
            with act.Fori(0, B) as b:
                act.wait_ge(shifted, b + 1)
                act.activation(expd[:], logits[:], ACT.Exp).then_inc(exp_done, 1)
                for n in range(NHID):
                    act.wait_ge(projected, b * NHID + n + 1)
                    if n >= 2:
                        act.wait_ge(hidden_taken, b * NHID + n - 1)
                    act.activation(silu[:, n % 2, :], psum[:, 4 + n % 3, 0:T], ACT.Silu).then_inc(silu_done, 1)

        @block.vector
        def _(dve):
            dve.wait_ge(loaded, 16 * len(loads))
            with dve.Fori(0, B) as b:
                per = 14 + TOP2_STEPS + TT * NE // 2
                step = Steps(dve, own, b * per, per)
                step.wait()
                dve.wait_ge(routed_taken, b * TT * NR)
                dve.wait_ge(gates_ready, b + 1)
                step.link(dve.tensor_tensor(logits[:], psum[:, 7, 0:TT * 16].rearrange("p (t n) -> p t n", t=TT)[:, :, 0:NGR + NE],
                                            bg[:].unsqueeze(1).to_broadcast([P, TT, NGR + NE]), ALU.add))
                by_group = lambda v: v[:, :, NGR:NGR + NE].rearrange("p t (g e) -> p t g e", g=NGR)
                step.did(dve.tensor_reduce(top[:, :, 0], logits[:, :, 0:NGR], AX.X, ALU.max))
                step.link(dve.tensor_reduce(top[:, :, 1:1 + NGR], by_group(logits), AX.X, ALU.max))
                dve.tensor_tensor(logits[:, :, 0:NGR], logits[:, :, 0:NGR], top[:, :, 0:1].to_broadcast([P, TT, NGR]), ALU.subtract)
                dve.tensor_tensor(by_group(logits), by_group(logits),
                                  top[:, :, 1:1 + NGR].unsqueeze(3).to_broadcast([P, TT, NGR, PER_GROUP]),
                                  ALU.subtract).then_inc(shifted, 1)
                for n in range(NHID):
                    dve.wait_ge(silu_done, b * NHID + n + 1)
                    dve.tensor_tensor(hidden[:, n // KH, n % KH, :], silu[:, n % 2, :], psum[:, 4 + n % 3, T:2 * T],
                                      ALU.mult).then_inc(hidden_taken, 1)
                dve.wait_ge(exp_done, b + 1)
                step.did(dve.tensor_reduce(total[:, :, 0], expd[:, :, 0:NGR], AX.X, ALU.add))
                step.link(dve.tensor_reduce(total[:, :, 1:1 + NGR], by_group(expd), AX.X, ALU.add))
                step.link(dve.reciprocal(total[:], total[:]))
                step.link(dve.tensor_tensor(expd[:, :, 0:NGR], expd[:, :, 0:NGR], total[:, :, 0:1].to_broadcast([P, TT, NGR]), ALU.mult))
                step.did(dve.tensor_tensor(chosen_group[:, :, 0], expd[:, :, 0], expd[:, :, 1], ALU.is_ge))
                step.link(dve.tensor_tensor(chosen_group[:, :, 1], expd[:, :, 1], expd[:, :, 0], ALU.is_gt))
                step.link(dve.tensor_reduce(group_p[:], expd[:, :, 0:NGR], AX.X, ALU.max))
                step.link(dve.tensor_tensor(chosen_group[:], chosen_group[:], group_p[:].unsqueeze(2).to_broadcast([P, TT, NGR]),
                                            ALU.mult))
                p4 = p[:].rearrange("p t (g e) -> p t g e", g=NGR)
                step.link(dve.tensor_tensor(p4, by_group(expd), total[:, :, 1:1 + NGR].unsqueeze(3).to_broadcast(
                    [P, TT, NGR, PER_GROUP]), ALU.mult))
                step.link(dve.tensor_tensor(p4, p4, chosen_group[:].unsqueeze(3).to_broadcast([P, TT, NGR, PER_GROUP]),
                                            ALU.mult))
                top2(dve, step, p[:], mask[:], (eq[:], rest[:]), red[:], rev[:], TT)
                step.link(dve.tensor_tensor(p[:], p[:], mask[:], ALU.mult))
                for t in range(TT):
                    R0 = (b * TT + t) * NR
                    x_t = x_all[:, bass.ds(b * TT + t, 1), :].rearrange("p a d -> p (a d)")
                    for r in range(NR):
                        bank = psum[:, (t * NR + r) % 4, :]
                        dve.wait_ge(routed_ready, R0 + r + 1)
                        if r == 0:
                            dve.tensor_tensor(acc[:, t, :], bank[:, 0:D], x_t, ALU.add).then_inc(routed_taken, 1)
                            continue
                        for half in range(2):
                            e = 2 * (r - 1) + half
                            dve.wait_ge(routed_taken, R0 + r) if half == 0 else step.wait()
                            ins = dve.scalar_tensor_tensor(x_t if e == NE - 1 else acc[:, t, :], bank[:, half * D:(half + 1) * D],
                                                           p[:, t, e:e + 1], acc[:, t, :], ALU.mult, ALU.add)
                            if half == 0:
                                step.did(ins)
                        ins.then_inc(routed_taken, 1)
                step.end()


STAGES = (("a0", attention0), ("x0", linear_attention), ("f0", switch_attention),
          ("a1", attention1), ("x1", cross_attention1), ("f1", experts))


def build(nc, inputs, out):
    with ExitStack() as stack:
        Scope.semaphores = stack
        s = Scope(nc, stack, "all")
        x_all = s.sb("x_all", [P, TILES, D])
        xnT_all = s.sb("xnT_all", [P, B, CC, T])
        ident = s.sb("ident", [P, P])
        psum = stack.enter_context(nc.psum_tensor("psum", [P, 8, 512], F32))
        x_loaded, stored = s.sem("x_loaded"), s.sem("stored")
        norm = Norm(Scope(nc, stack, "ln"))
        with nc.Block() as block:
            @block.sync
            def _(sp):
                sp.dma_start(ident[:], inputs["ident"]).then_inc(x_loaded, 16)
                sp.dma_start(x_all[:], inputs["x"].rearrange("b (t p) d -> p (b t) d", p=P)).then_inc(x_loaded, 16)
                sp.wait_ge(x_loaded, 32)
        for prefix, stage in STAGES:
            own = {k[len(prefix) + 1:]: v for k, v in inputs.items() if k.startswith(prefix + "_")}
            stage(nc, norm, x_all, xnT_all, ident, psum, own)
        with nc.Block() as block:
            @block.sync
            def _(sp):
                sp.dma_start(out.rearrange("b (t p) d -> p (b t) d", p=P), x_all[:]).then_inc(stored, 16)
                sp.wait_ge(stored, 16)


def _rope_tables():
    inv_freq = (1.0 / 10000.0 ** (np.arange(0, DH, 2, dtype=np.float32) / DH)).astype(np.float32)
    freqs = np.arange(T, dtype=np.float32)[:, None] * inv_freq[None, :]
    cos, sin = np.cos(freqs).T.astype(np.float32), np.sin(freqs).T.astype(np.float32)
    cos = np.tile(np.concatenate([cos, cos]), (P // DH, 1))
    sin = np.tile(np.concatenate([-sin, sin]), (P // DH, 1))
    return np.ascontiguousarray(np.stack([cos, sin], axis=1))


def _blocks(width):
    i = np.arange(P) // width
    return (i[:, None] == i[None, :]).astype(np.float32)


def _layouts(n):
    half = DH // 2
    plain = np.concatenate([np.arange(0, DH, 2), np.arange(1, DH, 2)])
    swapped = np.roll(plain, half)
    cols = {v: (np.arange(BR * NH)[:, None] * DH + p[None, :]).ravel() for v, p in (("", plain), ("s", swapped))}
    out = {"ident": np.eye(P, dtype=np.float32), "x": n["x"]}
    W, bias = n["L0_attn_W_Q"], n["L0_attn_b_Q"]
    out["a0_wq"], out["a0_wqs"] = W[:, cols[""]], W[:, cols["s"]]
    out["a0_bq"] = np.stack([bias[cols[v]].reshape(8, P).T for v in ("", "s")], axis=1)
    W, bias = n["L0_attn_W_K"], n["L0_attn_b_K"]
    out["a0_wk"], out["a0_wks"] = W[:, cols[""][:D]], W[:, cols["s"][:D]]
    out["a0_bk"] = np.stack([bias[cols[v][:D]].reshape(CC, P).T for v in ("", "s")], axis=1)
    out["a0_wv"], out["a0_bv"] = n["L0_attn_W_V"], n["L0_attn_b_V"]
    out["a0_wo"] = n["L0_attn_W_O"].reshape(BR * D, D)
    out["a0_bo"] = n["L0_attn_W_O_bias"].reshape(-1)
    out["a0_vnull"] = n["L0_attn_v_nulls"].reshape(-1)
    out["a0_sinks"] = n["L0_attn_sink_scalars"]
    out["a0_rope"] = _rope_tables()
    out["a0_same_head"] = _blocks(DH)
    out["a0_head_mask"] = np.ascontiguousarray(_blocks(DH)[:, ::DH])
    for name in ("q", "k", "v"):
        out[f"x0_w{name}"], out[f"x0_b{name}"] = n[f"L0_xattn_W{name}"], n[f"L0_xattn_b{name}"]
    out["x0_scale"] = n["L0_xattn_scale"].reshape(-1)
    out["x0_same_head"], out["x0_head_mask"] = out["a0_same_head"], out["a0_head_mask"]
    out["x0_ctxT"] = n["ctx_1024"].transpose(0, 2, 1).reshape(B * D, T)
    out["f0_wg"] = np.concatenate([n["L0_ffn_Ws"].reshape(-1, D), n["L0_ffn_Wd"].reshape(-1, D)]).T
    out["f0_wv"] = n["L0_ffn_Wv"].reshape(-1, D).T
    out["f0_wq"], out["f0_wk"] = n["L0_ffn_Wq"].reshape(-1, D).T, n["L0_ffn_Wk"].reshape(-1, D).T
    out["f0_wo"] = n["L0_ffn_Wo"].transpose(0, 2, 1).reshape(-1, D)
    out["f0_rev"] = np.arange(8, 0, -1, dtype=np.float32)
    out["a1_ctxT"] = n["L1_attn_context"].reshape(KEYS, CTX).T
    out["a1_wq"], out["a1_wk"], out["a1_wv"] = n["L1_attn_Wq"], n["L1_attn_Wk"], n["L1_attn_Wv"]
    out["a1_wo"], out["a1_bo"] = n["L1_attn_Wout"], n["L1_attn_bout"]
    for name in ("q", "k", "v"):
        out[f"x1_w{name}"] = n[f"L1_xattn_w_{name}"]
    out["x1_wo"], out["x1_bo"] = n["L1_xattn_out_w"].T, n["L1_xattn_out_b"]
    out["x1_mask"], out["x1_ctxT"] = n["mask_SxS2_ik0"], out["x0_ctxT"]
    out["f1_w_in"], out["f1_w1"], out["f1_w_out"] = n["L1_ffn_w_in"].T, n["L1_ffn_w1"].T, n["L1_ffn_w_out"].T
    out["f1_w2"] = n["L1_ffn_w2"].transpose(2, 0, 1).reshape(HID, NE * D)
    out["f1_wg"] = np.concatenate([n["L1_ffn_wg"], n["L1_ffn_we"]]).T
    out["f1_bg"] = np.concatenate([n["L1_ffn_gb"], n["L1_ffn_eb"]])
    out["f1_rev"] = out["f0_rev"]
    return out


def kernel(**inputs):
    import concourse.bacc as bacc
    from concourse.bass_utils import run_bass_kernel_spmd

    nc = bacc.Bacc("TRN2", target_bir_lowering=False, num_devices=1)
    arrays, tensors = {}, {}
    for name, value in _layouts({k: np.asarray(v) for k, v in inputs.items()}).items():
        value = np.ascontiguousarray(value)
        arrays[f"in_{name}"] = value
        tensors[name] = nc.dram_tensor(f"in_{name}", value.shape, mybir.dt.from_np(value.dtype), kind="ExternalInput").ap()
    out = nc.dram_tensor("out", (B, T, D), F32, kind="ExternalOutput").ap()
    build(nc, tensors, out)
    return run_bass_kernel_spmd(nc, [arrays], core_ids=[0]).results[0]["out"]
```

```python
from contextlib import ExitStack
import math

import numpy as np
import concourse.bass as bass
from concourse import mybir

F32 = mybir.dt.float32
I32 = mybir.dt.int32
F32R = mybir.dt.float32r
ALU = mybir.AluOpType
ACT = mybir.ActivationFunctionType
AX = mybir.AxisListType

P = 128
B, T, D = 8, 256, 256
TILES = B * T // P
TT = T // P
CC = D // P
LN_EPS = 1e-5


class Scope:

    semaphores = None

    def __init__(self, nc, stack, prefix):
        self.nc, self.stack, self.prefix = nc, stack, prefix

    def sb(self, name, shape, dtype=F32):
        return self.stack.enter_context(self.nc.sbuf_tensor(f"{self.prefix}_{name}", shape, dtype))

    def sem(self, name):
        return (Scope.semaphores or self.stack).enter_context(self.nc.semaphore(f"{self.prefix}_{name}"))

    def sems(self, name, n):
        return [self.sem(f"{name}{i}") for i in range(n)]


class Steps:

    def __init__(self, eng, sem, base=0, per=None):
        self.eng, self.sem, self.base, self.per, self.n = eng, sem, base, per, 0

    def did(self, instruction):
        instruction.then_inc(self.sem, 1)
        self.n += 1

    def wait(self):
        self.eng.wait_ge(self.sem, self.base + self.n)

    def link(self, instruction):
        self.did(instruction)
        self.wait()

    def end(self):
        assert self.per is None or self.n == self.per, (self.n, self.per)


def alone(eng, sem, value, passed):
    eng.wait_ge(sem, value)
    eng.sem_inc(passed, 1)


def chunked(w):
    return w.rearrange("(k p) n -> p k n", p=P)


def over_partitions(v, n):
    return v.rearrange("(a n) -> a n", a=1).to_broadcast([P, n])


HERE, AHEAD, OLD = "new", "ahead", "old"


def wait(eng, sem, value):
    if not isinstance(value, int) or value > 0:
        eng.wait_ge(sem, value)


def wait_alone(eng, sem, value, passed):
    if not isinstance(value, int) or value > 0:
        alone(eng, sem, value, passed)


def over_batches(eng, body):
    body(-1, False, True, False)
    body(0, True, True, False)
    with eng.Fori(0, B - 2) as i:
        body(i + 1, True, True, True)
    body(B - 1, True, False, True)
    body(B, False, False, True)


def units(b, lag, new, old, count=16):
    for j in range(count):
        v = j - lag
        yield (v % count, b * count + v) if (new if v >= 0 else old) else None


def split_product(pe, out, lhsT, rhs, start, stop):
    pe.matmul(out, lhsT[0], rhs[0], start=start, stop=False)
    pe.matmul(out, lhsT[0], rhs[1], start=False, stop=False)
    return pe.matmul(out, lhsT[1], rhs[0], start=False, stop=stop)


class Norm:

    def __init__(self, s):
        self.runs = 0
        self.own, self.variance_ready, self.std_ready = s.sem("own"), s.sem("variance_ready"), s.sem("std_ready")
        self.normalised, self.transposed, self.copied = (s.sems(n, TT) for n in ("normalised", "transposed", "copied"))


def normalise(nc, norm, x_all, xnT_all, ident, psum, loads, loaded):
    with ExitStack() as stack:
        run = norm.runs
        norm.runs += 1
        b0 = run * B
        s = Scope(nc, stack, f"ln{run}")
        stats = s.sb("stats", [P, TILES, 6])
        mean_var = s.sb("mean_var", [P, TILES, 2])
        std = s.sb("std", [P, TILES])
        rstd = s.sb("rstd", [P, TILES])
        shift = s.sb("shift", [P, TILES])
        eps = s.sb("eps", [P, 1])
        xn = s.sb("xn", [P, TT, D])
        psT = psum[:, 0:TT, :].rearrange("p t (c n) -> p t c n", n=P)
        variance_ready, std_ready = norm.variance_ready, norm.std_ready
        normalised, transposed, copied = norm.normalised, norm.transposed, norm.copied
        block = stack.enter_context(nc.Block())

        @block.sync
        def _(sp):
            for dst, src in loads:
                sp.dma_start(dst, src).then_inc(loaded, 16)

        @block.vector
        def _(dve):
            step = Steps(dve, norm.own, run * (TILES + 3))
            step.did(dve.memset(eps[:], LN_EPS))
            for t in range(TILES):
                step.did(dve.bn_stats(stats[:, t, :], x_all[:, t, :]))
            step.wait()
            for t in range(TILES):
                ins = dve.bn_aggr(mean_var[:, t, :], stats[:, t, :])
            ins.then_inc(variance_ready, 1)
            dve.wait_ge(std_ready, run + 1)
            step.link(dve.reciprocal(rstd[:], std[:]))
            step.link(dve.scalar_tensor_tensor(shift[:], mean_var[:, :, 0], -1.0, rstd[:], ALU.mult, ALU.mult))
            with dve.Fori(0, B) as b:
                for t in range(TT):
                    dve.wait_ge(transposed[t], b0 + b)
                    tile = b * TT + t
                    dve.tensor_scalar(xn[:, t, :], x_all[:, bass.ds(tile, 1), :], rstd[:, bass.ds(tile, 1)],
                                      shift[:, bass.ds(tile, 1)], ALU.mult, ALU.add).then_inc(normalised[t], 1)

        @block.tensor
        def _(pe):
            with pe.Fori(0, B) as b:
                for t in range(TT):
                    pe.wait_ge(normalised[t], b0 + b + 1)
                    pe.wait_ge(copied[t], b0 + b)
                    for c in range(CC):
                        ins = pe.transpose(psT[:, t, c, :], xn[:, t, c * P:(c + 1) * P], ident[:])
                    ins.then_inc(transposed[t], 1)

        @block.scalar
        def _(act):
            act.wait_ge(variance_ready, run + 1)
            act.activation(std[:], mean_var[:, :, 1], ACT.Sqrt, bias=eps[:, 0:1]).then_inc(std_ready, 1)
            with act.Fori(0, B) as b:
                for t in range(TT):
                    act.wait_ge(transposed[t], b0 + b + 1)
                    act.activation(xnT_all[:, bass.ds(b, 1), :, t * P:(t + 1) * P], psT[:, t, 0:CC, :],
                                   ACT.Copy).then_inc(copied[t], 1)


BR, NH, DH = 4, 16, 16
NU = NH
RING = 8
K1 = BR * T
UNIT = BR * T + BR * P
SILU_SCALE = math.pi / math.sqrt(3.0)
CAP = 44.0

SOFTPLUS_LAG, THRESHOLD_LAG, SUM_LAG = 1, 6, 8
SILU_EVERY, SILU_FROM, SILU_TO = 4, 5, 2

SPARE = {0: [("regroup", 2, OLD), ("regroup", 3, OLD)], 1: [("q", 0, HERE)], 2: [("q", 1, HERE)],
         3: [("q", 2, HERE), ("q", 3, HERE)], 4: [("regroup", 4, OLD), ("regroup", 5, OLD)], 5: [("k", 0, AHEAD)],
         6: [("k", 1, AHEAD)], 7: [("v", 0, HERE)], 8: [("regroup", 6, OLD), ("regroup", 7, OLD)],
         9: [("norm", 0, AHEAD), ("q", 0, AHEAD)], 10: [("turn", 0, OLD), ("turn", 1, OLD)],
         11: [("turn", 2, OLD), ("turn", 3, OLD)], 12: [("regroup", 0, HERE), ("regroup", 1, HERE)],
         13: [("q", 1, AHEAD), ("q", 2, AHEAD)], 14: [("q", 3, AHEAD)], 15: [("out", 0, OLD)]}
REGROUPS = 8
ROTATED = 2 + 2 * BR


def rotations(b, kind, i, when):
    place = i if when == HERE else 4 + i if kind == "k" else 6 + i
    return b * ROTATED + 6 + place


def attention0(nc, norm, x_all, xnT_all, ident, psum, a):
    with ExitStack() as stack:
        s = Scope(nc, stack, "a0")
        wq, wqs = s.sb("wq", [P, CC, BR * D]), s.sb("wqs", [P, CC, BR * D])
        wk, wks, wv = s.sb("wk", [P, CC, D]), s.sb("wks", [P, CC, D]), s.sb("wv", [P, CC, D])
        wo = s.sb("wo", [P, BR * CC, D])
        bq = s.sb("bq", [P, 2, 8])
        bk = s.sb("bk", [P, 2, CC])
        bv = s.sb("bv", [P, D])
        rope = s.sb("rope", [P, 2, T])
        same_head = s.sb("same_head", [P, P])
        head_mask = s.sb("head_mask", [P, 8])
        sinks = s.sb("sinks", [P, BR * NH])
        sinks_eps = s.sb("sinks_eps", [P, BR, NH])
        vnull = s.sb("vnull", [P, BR, NH, DH])
        bo = s.sb("bo", [P, BR, D])
        ln_quarter = s.sb("ln_quarter", [P, 1])
        xnT = s.sb("xnT", [P, CC, T])
        rot = [s.sb(f"rot{i}", [P, 2, T]) for i in range(2)]
        qT = s.sb("qT", [P, CC, BR, T])
        kT = s.sb("kT", [P, CC, T])
        ksq = s.sb("ksq", [P, CC, T])
        kT_head = s.sb("kT_head", [P, NH, T])
        v1 = s.sb("v1", [P, TT, NH, DH + 1])
        e = s.sb("e", [P, 2, UNIT])
        w = s.sb("w", [P, RING, UNIT])
        sumT = s.sb("sumT", [P, 2, BR * T])
        ctx = s.sb("ctx", [P, BR * TT, NH, DH + 1])
        total = s.sb("total", [P, BR * TT, NH])
        ctxn = s.sb("ctxn", [P, TT, BR * NH, DH])
        ctxT = s.sb("ctxT", [P, TT, 8, P])
        psS = [psum[:, 3 * i:3 * i + 3, :].rearrange("p k n -> p (k n)") for i in range(2)]
        psO = psum[:, 6, :]
        spare = psum[:, 7, :]

        loaded, v_x_here = s.sem("loaded"), s.sem("v_x_here")
        projected, v_done, norm_done, turn_done, out_done = (
            s.sem(n) for n in ("projected", "v_done", "norm_done", "turn_done", "out_done"))
        rot_made, v_taken, norm_taken, turn_taken, out_taken = (
            s.sem(n) for n in ("rot_made", "v_taken", "norm_taken", "turn_taken", "out_taken"))
        rotated, ksq_ready, ln_k, knorm_ready, knormed, kheads_ready = (
            s.sem(n) for n in ("rotated", "ksq_ready", "ln_k", "knorm_ready", "knormed", "kheads_ready"))
        scored, exp_done, ln_done, softplus_done, masked, silu_done, weights_done, summed, sums_taken = (
            s.sem(n) for n in ("scored", "exp_done", "ln_done", "softplus_done", "masked", "silu_done",
                               "weights_done", "summed", "sums_taken"))
        regrouped, regroup_taken = s.sem("regrouped"), s.sem("regroup_taken")
        totalled, inverted, null_added, ctx_ready = (
            s.sem(n) for n in ("totalled", "inverted", "null_added", "ctx_ready"))
        x_biased = s.sem("x_biased")
        consts, passed, own = s.sem("consts"), s.sem("passed"), s.sem("own_setup")

        loads = [(wk[:], chunked(a["wk"])), (wks[:], chunked(a["wks"])), (wv[:], chunked(a["wv"])),
                 (wq[:], chunked(a["wq"])), (wqs[:], chunked(a["wqs"])), (wo[:], chunked(a["wo"])),
                 (bq[:], a["bq"]), (bk[:], a["bk"]), (bv[:], over_partitions(a["bv"], D)),
                 (rope[:], a["rope"]), (same_head[:], a["same_head"]), (head_mask[:], a["head_mask"]),
                 (sinks[:], over_partitions(a["sinks"], BR * NH)),
                 (vnull[:].rearrange("p r h d -> p (r h d)"), over_partitions(a["vnull"], BR * D)),
                 (bo[:].rearrange("p r d -> p (r d)"), over_partitions(a["bo"], BR * D))]
        normalise(nc, norm, x_all, xnT_all, ident, psum, loads, loaded)
        block = stack.enter_context(nc.Block())

        @block.sync
        def _(sp):
            with sp.Fori(0, B) as b:
                sp.wait_ge(v_done, b)
                sp.dma_start(xnT[:], xnT_all[:, bass.ds(b, 1), :, :]).then_inc(v_x_here, 16)

        @block.tensor
        def _(pe):
            pe.wait_ge(loaded, 16 * len(loads))

            def sum_half(b, unit, half):
                u, n = unit
                if u == 0 and half == 0:
                    pe.wait_ge(v_taken, b + 1)
                pe.wait_ge(weights_done, n + 1)
                wait(pe, sums_taken, 2 * n + half)
                pe.matmul(psO[0:DH + 1, :], v1[:, 0, u, :], w[:, u % RING, half * 512:(half + 1) * 512],
                          start=True, stop=False)
                lo = K1 + half * 256
                pe.matmul(psO[0:DH + 1, :].rearrange("p (r t) -> p r t", r=2)[:, :, P:T], v1[:, 1, u, :],
                          w[:, u % RING, lo:lo + 256].rearrange("p (r t) -> p r t", r=2), start=False, stop=True)\
                  .then_inc(summed, 1)

            def body(b, new, ahead, old):
                exists = {HERE: new, AHEAD: ahead, OLD: old}
                of = {HERE: b, AHEAD: b + 1, OLD: b - 1}
                spare_free = [(out_taken, b - 1), (rot_made, b * ROTATED + (6 if new or ahead else 0))]
                if old:
                    spare_free.append((regroup_taken, (b - 1) * REGROUPS + 2))

                def pass_through_spare(kind, i, when):
                    nonlocal spare_free
                    bb = of[when]
                    for sem, value in spare_free:
                        wait(pe, sem, value)
                    if kind in "qk":
                        g = 0 if when == AHEAD else 1
                        lo = i * P if kind == "k" else (2 * i + g) * P
                        for v, weights in enumerate((wk, wks) if kind == "k" else (wq, wqs)):
                            for c in range(CC):
                                ins = pe.matmul(spare[:, v * T:(v + 1) * T], weights[:, c, lo:lo + P],
                                                xnT_all[:, bass.ds(bb, 1), c, :], start=(c == 0), stop=(c == CC - 1))
                        ins.then_inc(projected, 1)
                        spare_free = [(rot_made, rotations(b, kind, i, when) + 1)]
                    elif kind == "v":
                        pe.wait_ge(v_x_here, bb * 16 + 16)
                        for t in range(TT):
                            for c in range(CC):
                                ins = pe.matmul(spare[:, t * D:(t + 1) * D], xnT[:, c, t * P:(t + 1) * P], wv[:, c, :],
                                                start=(c == 0), stop=(c == CC - 1))
                        ins.then_inc(v_done, 1)
                        spare_free = [(v_taken, bb + 1)]
                    elif kind == "norm":
                        pe.wait_ge(ksq_ready, bb + 1)
                        for g in range(CC):
                            ins = pe.matmul(spare[:, g * T:(g + 1) * T], same_head[:], ksq[:, g, :], start=True, stop=True)
                        ins.then_inc(norm_done, 1)
                        spare_free = [(norm_taken, bb + 1)]
                    elif kind == "regroup":
                        pe.wait_ge(sums_taken, (bb * NU + i // 2 * 4 + 4) * 2)
                        for k in range(4):
                            lo = i % 2 * 512 + k * P
                            ins = pe.transpose(spare[:, k * P:(k + 1) * P], sumT[:, i // 2 % 2, lo:lo + P], ident[:])
                        ins.then_inc(regrouped, 1)
                        spare_free = [(regroup_taken, bb * REGROUPS + i + 1)]
                    elif kind == "turn":
                        if i == 0:
                            pe.wait_ge(ctx_ready, bb * 4 + 4)
                        for k in range(4):
                            lo = 8 * (4 * (i % 2) + k)
                            ins = pe.transpose(spare[:, k * P:(k + 1) * P],
                                               ctxn[:, i // 2, lo:lo + 8, :].rearrange("p h d -> p (h d)"), ident[:])
                        ins.then_inc(turn_done, 1)
                        spare_free = [(turn_taken, bb * 4 + i + 1)]
                    else:
                        for t in range(TT):
                            for k in range(8):
                                ins = pe.matmul(spare[:, t * D:(t + 1) * D], ctxT[:, t, k, :], wo[:, k, :],
                                                start=(k == 0), stop=(k == 7))
                        ins.then_inc(out_done, 1)

                for j, summed_unit in enumerate(units(b, SUM_LAG, new, old)):
                    beside = [item for item in SPARE[j] if exists[item[2]]]
                    if summed_unit:
                        sum_half(b, summed_unit, 0)
                    for kind, i, when in beside[:-1][0:1]:
                        pass_through_spare(kind, i, when)
                    if new:
                        g, n = j // 8, b * NU + j
                        if j % 8 == 0:
                            pe.wait_ge(kheads_ready, b * 2 + g + 1)
                            pe.wait_ge(rotated, b * ROTATED + 6 + 4 * g)
                        wait(pe, softplus_done, n - 1)
                        for half in range(2):
                            pe.matmul(psS[j % 2][:, half * 512:(half + 1) * 512], kT_head[:, j, 0:P],
                                      qT[:, g, 2 * half:2 * half + 2, :], start=True, stop=True)
                        pe.matmul(psS[j % 2][:, K1:UNIT], kT_head[:, j, P:T], qT[:, g, :, P:T],
                                  start=True, stop=True).then_inc(scored, 1)
                    if summed_unit:
                        sum_half(b, summed_unit, 1)
                    for kind, i, when in beside[1:] or beside:
                        pass_through_spare(kind, i, when)

            over_batches(pe, body)

        @block.scalar
        def _(act):
            act.preload_act_table_set("natural_log_exp_and_others")
            act.wait_ge(consts, 1)

            def body(b, new, ahead, old):
                exists = {HERE: new, AHEAD: ahead, OLD: old}

                def take_turned(kind, i, when):
                    if kind == "turn":
                        act.wait_ge(turn_done, (b - 1) * 4 + i + 1)
                        wait(act, out_done, b - 1)
                        act.activation(ctxT[:, i // 2, 4 * (i % 2):4 * (i % 2) + 4, :],
                                       spare.rearrange("p (k n) -> p k n", k=4), ACT.Copy).then_inc(turn_taken, 1)

                for j in range(NU):
                    n = b * NU + j
                    beside = [item for item in SPARE[j] if exists[item[2]]]
                    for kind, i, when in beside[:-1][0:1]:
                        take_turned(kind, i, when)
                    if new:
                        act.wait_ge(scored, n + 1)
                        act.activation(e[:, j % 2, :], psS[j % 2], ACT.Exp).then_inc(exp_done, 1)
                        act.wait_ge(exp_done, n + 1)
                        act.activation(e[:, j % 2, :], e[:, j % 2, :], ACT.Ln, bias=1.0).then_inc(ln_done, 1)
                    for kind, i, when in beside[1:] or beside:
                        take_turned(kind, i, when)
                    if ahead and j == 9:
                        act.wait_ge(norm_taken, b + 2)
                        act.activation(ksq[:], ksq[:], ACT.Ln).then_inc(ln_k, 1)
                        act.wait_ge(ln_k, b + 2)
                        act.activation(ksq[:], ksq[:], ACT.Exp, scale=-0.5, bias=ln_quarter[:, 0:1]).then_inc(knorm_ready, 1)
                    if j % SILU_EVERY == SILU_EVERY - 1:
                        those = [v for v in range(j - SILU_FROM, j - SILU_TO + 1) if (new if v >= 0 else old)]
                        if those:
                            for v in those:
                                wu = w[:, v % RING, :]
                                act.wait_ge(masked, b * NU + v + 1)
                                act.activation(wu, wu, ACT.Silu, scale=SILU_SCALE).then_inc(silu_done, 1)
                            act.preload_act_table_set("natural_log_exp_and_others")

            over_batches(act, body)

        @block.gpsimd
        def _(pool):
            pool.wait_ge(consts, 1)

            def head_rows(g, first, last):
                for u in range(8 * g + first, 8 * g + last):
                    ins = pool.tensor_scalar(kT_head[:, u, :], kT[:, g, :], head_mask[:, u % 8:u % 8 + 1], 1.0,
                                             ALU.mult, ALU.mult)
                    if u % 8 == 7:
                        ins.then_inc(kheads_ready, 1)

            def body(b, new, ahead, old):
                softplus_units = list(units(b, SOFTPLUS_LAG, new, old))
                for j in range(NU):
                    if softplus_units[j]:
                        u, n = softplus_units[j]
                        alone(pool, softplus_done, n + 1, passed)
                        for part in (w[:, u % RING, 0:K1].rearrange("p (r t) -> p r t", r=BR)[:, :, 0:P],
                                     w[:, u % RING, K1:UNIT].rearrange("p (r t) -> p r t", r=BR)):
                            ins = pool.affine_select(out=part, in_=part, compare_op=ALU.is_ge, fill=0.0, base=0,
                                                     pattern=[[0, BR], [1, P]], channel_multiplier=-1)
                        ins.then_inc(masked, 1)
                    for kind, i, when in SPARE[j]:
                        if kind in "qk" and (new if when == HERE else ahead):
                            g = 0 if when == AHEAD else 1
                            r = rotations(b, kind, i, when)
                            out = kT[:, i, :] if kind == "k" else qT[:, g, i, :]
                            alone(pool, rot_made, r + 1, passed)
                            if kind == "k":
                                wait_alone(pool, kheads_ready, b * 2 + 2, passed)
                            else:
                                wait_alone(pool, scored, b * NU + (8 if when == AHEAD else 0), passed)
                            pool.tensor_tensor(out, rot[i % 2][:, 0, :], rot[i % 2][:, 1, :], ALU.add).then_inc(rotated, 1)
                            if kind == "k":
                                alone(pool, rotated, r + 1, passed)
                                wait_alone(pool, knormed, b + 1, passed)
                                ins = pool.tensor_tensor(ksq[:, i, :], out, out, ALU.mult)
                                if i == 1:
                                    ins.then_inc(ksq_ready, 1)
                    if new and j < 4:
                        if j == 0:
                            wait_alone(pool, scored, b * NU, passed)
                            alone(pool, knormed, b + 1, passed)
                        head_rows(1, 2 * j, 2 * j + 2)
                    if ahead and j == 10:
                        alone(pool, knorm_ready, b + 2, passed)
                        pool.tensor_tensor(kT[:], kT[:], ksq[:], ALU.mult).then_inc(knormed, 1)
                    if ahead and 11 <= j < 15:
                        if j == 11:
                            wait_alone(pool, scored, b * NU + 8, passed)
                            alone(pool, knormed, b + 2, passed)
                        head_rows(0, 2 * (j - 11), 2 * (j - 11) + 2)
                    for kind, i, when in SPARE[j]:
                        if kind == "regroup" and i % 2 and (new if when == HERE else old):
                            bb = b if when == HERE else b - 1
                            q4 = i // 2
                            n4 = bb * 4 + q4
                            heads = slice(4 * q4, 4 * q4 + 4)
                            alone(pool, regroup_taken, bb * REGROUPS + i + 1, passed)
                            wait_alone(pool, turn_done, bb * 4, passed)
                            by_t = ctx[:].rearrange("p (r t) h d -> p r t h d", t=TT)
                            c4 = ctxn[:].rearrange("p t (r h) d -> p t r h d", r=BR)
                            for t in range(TT):
                                ins = pool.tensor_tensor(c4[:, t, :, heads, :], by_t[:, :, t, heads, 0:DH],
                                                         vnull[:, :, heads, :], ALU.add)
                            ins.then_inc(null_added, 1)
                            alone(pool, null_added, n4 + 1, passed)
                            alone(pool, inverted, n4 + 1, passed)
                            for t in range(TT):
                                inv = total[:].rearrange("p (r t) h -> p r t h", t=TT)[:, :, t, heads]
                                ins = pool.tensor_tensor(c4[:, t, :, heads, :], c4[:, t, :, heads, :],
                                                         inv.unsqueeze(3).to_broadcast([P, BR, 4, DH]), ALU.mult)
                            ins.then_inc(ctx_ready, 1)
                    if old and j == 12:
                        x_b = x_all[:, bass.ds((b - 1) * TT, TT), :]
                        pool.tensor_tensor(x_b, x_b, bo[:, 0:1, :].to_broadcast([P, TT, D]), ALU.add).then_inc(x_biased, 1)

            over_batches(pool, body)

        @block.vector
        def _(dve):
            dve.wait_ge(loaded, 16 * len(loads))
            step = Steps(dve, own)
            step.did(dve.memset(ln_quarter[:], math.log(0.25)))
            step.did(dve.memset(v1[:, :, :, DH:DH + 1], 1.0))
            step.did(dve.memset(sumT[:], 0.0))
            step.link(dve.tensor_scalar(sinks[:], sinks[:], SILU_SCALE, None, ALU.mult))
            by_head = sinks[:].rearrange("p (r h) -> p r h", r=BR)
            step.did(dve.tensor_scalar(sinks_eps[:], by_head, 1e-6 * SILU_SCALE, None, ALU.add))
            step.did(dve.tensor_tensor(vnull[:], vnull[:], by_head.unsqueeze(3).to_broadcast([P, BR, NH, DH]), ALU.mult))
            step.link(dve.tensor_tensor(bo[:, 0:2, :], bo[:, 0:2, :], bo[:, 2:4, :], ALU.add))
            step.link(dve.tensor_tensor(bo[:, 0, :], bo[:, 0, :], bo[:, 1, :], ALU.add))
            dve.tensor_scalar(bo[:, 0, :], bo[:, 0, :], 1.0 / BR, None, ALU.mult).then_inc(consts, 1)
            dve.wait_ge(consts, 1)

            def take_from_spare(b, kind, i, when):
                bb = b + 1 if when == AHEAD else b
                if kind in "qk":
                    r = rotations(b, kind, i, when)
                    bias, col = (bk, i) if kind == "k" else (bq, 2 * i + (0 if when == AHEAD else 1))
                    ps = spare.rearrange("p (v t) -> p v t", v=2)
                    dve.wait_ge(projected, r + 1)
                    wait(dve, rotated, r - 1)
                    for v in range(2):
                        ins = dve.scalar_tensor_tensor(rot[i % 2][:, v, :], ps[:, v, :], bias[:, v, col:col + 1],
                                                       rope[:, v, :], ALU.add, ALU.mult)
                    ins.then_inc(rot_made, 1)
                elif kind == "v":
                    dve.wait_ge(v_done, bb + 1)
                    wait(dve, summed, b * NU * 2)
                    for t in range(TT):
                        ins = dve.tensor_tensor(v1[:, t, :, 0:DH], spare[:, t * D:(t + 1) * D].rearrange("p (h d) -> p h d", d=DH),
                                                bv[:].rearrange("p (h d) -> p h d", d=DH), ALU.add)
                    ins.then_inc(v_taken, 1)
                elif kind == "norm":
                    dve.wait_ge(norm_done, bb + 1)
                    dve.tensor_scalar(ksq[:].rearrange("p g t -> p (g t)"), spare, 1e-6, None, ALU.max).then_inc(norm_taken, 1)
                elif kind == "regroup":
                    bb = b if when == HERE else b - 1
                    q4 = i // 2
                    heads = slice(4 * q4, 4 * q4 + 4)
                    dve.wait_ge(regrouped, bb * REGROUPS + i + 1)
                    wait(dve, null_added, bb * 4)
                    dve.tensor_copy(ctx[:, 4 * (i % 2):4 * (i % 2) + 4, heads, :],
                                    spare.rearrange("p (a h d) -> p a h d", a=4, h=4)[:, :, :, 0:DH + 1])\
                       .then_inc(regroup_taken, 1)
                    if i % 2:
                        n4 = bb * 4 + q4
                        dve.wait_ge(regroup_taken, bb * REGROUPS + i + 1)
                        wait(dve, ctx_ready, bb * 4)
                        tot = total[:].rearrange("p (r t) h -> p r t h", t=TT)
                        by_t = ctx[:].rearrange("p (r t) h d -> p r t h d", t=TT)
                        for t in range(TT):
                            ins = dve.tensor_tensor(tot[:, :, t, heads], by_t[:, :, t, heads, DH], sinks_eps[:, :, heads],
                                                    ALU.add)
                        ins.then_inc(totalled, 1)
                        dve.wait_ge(totalled, n4 + 1)
                        dve.reciprocal(total[:, :, heads], total[:, :, heads]).then_inc(inverted, 1)
                elif kind == "out":
                    dve.wait_ge(out_done, b)
                    dve.wait_ge(x_biased, b)
                    x_b = x_all[:, bass.ds((b - 1) * TT, TT), :]
                    dve.scalar_tensor_tensor(x_b, spare.rearrange("p (t d) -> p t d", t=TT), 1.0 / BR, x_b,
                                             ALU.mult, ALU.add).then_inc(out_taken, 1)

            def body(b, new, ahead, old):
                exists = {HERE: new, AHEAD: ahead, OLD: old}
                below_sink, summed_units = list(units(b, THRESHOLD_LAG, new, old)), list(units(b, SUM_LAG, new, old))

                def take_sums(unit, half):
                    u, n = unit
                    dve.wait_ge(summed, 2 * n + half + 1)
                    if u % 4 == 0 and half == 0:
                        bb = b if u < NU - SUM_LAG else b - 1
                        wait(dve, regrouped, bb * REGROUPS + 2 * (u // 4) - 2)
                    lo = 32 * (u % 4)
                    dve.tensor_copy(sumT[lo:lo + DH + 1, u // 4 % 2, half * 512:(half + 1) * 512], psO[0:DH + 1, :])\
                       .then_inc(sums_taken, 1)

                def threshold(unit, branches):
                    u, n = unit
                    dve.wait_ge(silu_done, n + 1)
                    for r in branches:
                        for part in (w[:, u % RING, r * T:(r + 1) * T], w[:, u % RING, K1 + r * P:K1 + (r + 1) * P]):
                            ins = dve.scalar_tensor_tensor(part, part, sinks[:, r * NH + u:r * NH + u + 1], part,
                                                           ALU.is_ge, ALU.mult)
                    if BR - 1 in branches:
                        ins.then_inc(weights_done, 1)

                softplus_units = list(units(b, SOFTPLUS_LAG, new, old))
                for j in range(NU):
                    beside = [item for item in SPARE[j] if exists[item[2]]]
                    if summed_units[j]:
                        take_sums(summed_units[j], 0)
                    for kind, i, when in beside[:-1][0:1]:
                        take_from_spare(b, kind, i, when)
                    if softplus_units[j]:
                        u, n = softplus_units[j]
                        dve.wait_ge(ln_done, n + 1)
                        wait(dve, summed, (n - RING + 1) * 2)
                        dve.scalar_tensor_tensor(w[:, u % RING, :], e[:, u % 2, :], CAP, psS[u % 2],
                                                 ALU.min, ALU.max).then_inc(softplus_done, 1)
                    if below_sink[j]:
                        threshold(below_sink[j], (0, 1))
                    if summed_units[j]:
                        take_sums(summed_units[j], 1)
                    if below_sink[j]:
                        threshold(below_sink[j], (2, 3))
                    for kind, i, when in beside[1:] or beside:
                        take_from_spare(b, kind, i, when)

            over_batches(dve, body)


FOCUS_EPS = 1e-6
XH = 16
HEADS_IN_CHUNK = P // (D // XH)


def linear_attention(nc, norm, x_all, xnT_all, ident, psum, a):
    with ExitStack() as stack:
        s = Scope(nc, stack, "x0")
        wq, wk, wv = (s.sb(n, [P, CC, D]) for n in ("wq", "wk", "wv"))
        bq, bk, bv = (s.sb(n, [P, D]) for n in ("bq", "bk", "bv"))
        inv_scale = s.sb("inv_scale", [P, D])
        scale_e = s.sb("scale_e", [P, D])
        same_head = s.sb("same_head", [P, P])
        head_mask = s.sb("head_mask", [P, HEADS_IN_CHUNK])
        xnT, ctxT = s.sb("xnT", [P, CC, T]), s.sb("ctxT", [P, CC, T])
        f, f2, f3 = (s.sb(n, [P, 2 * TT, D]) for n in ("f", "f2", "f3"))
        norm2, norm6, factor = (s.sb(n, [P, 2 * TT]) for n in ("norm2", "norm6", "factor"))
        v1 = s.sb("v1", [P, TT, CC, P + 1])
        KVW = P + HEADS_IN_CHUNK
        kv = s.sb("kv", [P, CC, KVW])
        qT = s.sb("qT", [P, CC, T])
        z = s.sb("z", [P, TT, CC, HEADS_IN_CHUNK])
        o = s.sb("o", [P, TT, D])
        loaded, x_here, ctx_here = s.sem("loaded"), s.sem("x_here"), s.sem("ctx_here")
        consts, own_dve, own_setup = s.sem("consts"), s.sem("own_dve"), s.sem("own_setup")
        projected, taken, features_raw = s.sem("projected"), s.sem("taken"), s.sem("features_raw")
        squared, cubed, sixth, ratio_ready, factor_ready = (
            s.sem(n) for n in ("squared", "cubed", "sixth", "ratio_ready", "factor_ready"))
        features, kv_summed, kv_ready = s.sem("features"), s.sem("kv_summed"), s.sem("kv_ready")
        q_turned, qT_ready, out_ready, out_taken = (s.sem(n) for n in ("q_turned", "qT_ready", "out_ready", "out_taken"))
        own_act = s.sem("own_act")
        loads = [(wq[:], chunked(a["wq"])), (wk[:], chunked(a["wk"])), (wv[:], chunked(a["wv"])),
                 (bq[:], over_partitions(a["bq"], D)), (bk[:], over_partitions(a["bk"], D)),
                 (bv[:], over_partitions(a["bv"], D)), (inv_scale[:], over_partitions(a["scale"], D)),
                 (same_head[:], a["same_head"]), (head_mask[:], a["head_mask"])]
        normalise(nc, norm, x_all, xnT_all, ident, psum, loads, loaded)
        block = stack.enter_context(nc.Block())

        @block.sync
        def _(sp):
            with sp.Fori(0, B) as b:
                sp.wait_ge(projected, b * 3)
                sp.dma_start(xnT[:], xnT_all[:, bass.ds(b, 1), :, :]).then_inc(x_here, 16)
                sp.dma_start(ctxT[:], a["ctxT"][bass.ds(b * D, D), :].rearrange("(k p) n -> p k n", p=P))\
                  .then_inc(ctx_here, 16)

        @block.tensor
        def _(pe):
            pe.wait_ge(loaded, 16 * len(loads))
            with pe.Fori(0, B) as b:
                pe.wait_ge(x_here, b * 16 + 16)
                pe.wait_ge(ctx_here, b * 16 + 16)
                pe.wait_ge(out_taken, b)
                for n, (src, weights) in enumerate(((ctxT, wk), (xnT, wq), (ctxT, wv))):
                    for t in range(TT):
                        for c in range(CC):
                            ins = pe.matmul(psum[:, n, t * D:(t + 1) * D], src[:, c, t * P:(t + 1) * P], weights[:, c, :],
                                            start=(c == 0), stop=(c == CC - 1))
                    ins.then_inc(projected, 1)
                pe.wait_ge(features, b + 1)
                for c in range(CC):
                    for t in range(TT):
                        ins = pe.matmul(psum[:, 3, c * (P + 1):(c + 1) * (P + 1)], f3[:, TT + t, c * P:(c + 1) * P],
                                        v1[:, t, c, :], start=(t == 0), stop=(t == TT - 1))
                ins.then_inc(kv_summed, 1)
                for c in range(CC):
                    for t in range(TT):
                        ins = pe.transpose(psum[:, 4, c * T + t * P:c * T + (t + 1) * P], f3[:, t, c * P:(c + 1) * P],
                                           ident[:])
                ins.then_inc(q_turned, 1)
                pe.wait_ge(kv_ready, b + 1)
                pe.wait_ge(qT_ready, b + 1)
                for t in range(TT):
                    for c in range(CC):
                        ins = pe.matmul(psum[:, 5 + t, c * KVW:(c + 1) * KVW], qT[:, c, t * P:(t + 1) * P], kv[:, c, :],
                                        start=True, stop=True)
                ins.then_inc(out_ready, 1)

        @block.scalar
        def _(act):
            act.wait_ge(consts, 1)
            step = Steps(act, own_act)
            act.preload_act_table_set("natural_log_exp_and_others")
            step.link(act.activation(scale_e[:], scale_e[:], ACT.Exp))
            step.link(act.activation(scale_e[:], scale_e[:], ACT.Ln, bias=1.0))
            act.preload_act_table_set("sqrt_and_others")
            with act.Fori(0, B) as b:
                act.wait_ge(features_raw, b + 1)
                for i in range(2 * TT):
                    ins = act.activation(f2[:, i, :], f[:, i, :], ACT.Square, accum_out=norm2[:, i:i + 1])
                ins.then_inc(squared, 1)
                act.wait_ge(cubed, b + 1)
                act.wait_ge(squared, b + 1)
                for i in range(2 * TT):
                    ins = act.activation(f2[:, i, :], f3[:, i, :], ACT.Square, accum_out=norm6[:, i:i + 1])
                ins.then_inc(sixth, 1)
                act.wait_ge(ratio_ready, b + 1)
                act.activation(factor[:], factor[:], ACT.Sqrt).then_inc(factor_ready, 1)
                act.wait_ge(q_turned, b + 1)
                act.activation(qT[:], psum[:, 4, :].rearrange("p (c t) -> p c t", c=CC), ACT.Copy).then_inc(qT_ready, 1)

        @block.vector
        def _(dve):
            dve.wait_ge(loaded, 16 * len(loads))
            step = Steps(dve, own_setup)
            step.did(dve.memset(v1[:, :, :, P:P + 1], 1.0))
            dve.tensor_scalar(scale_e[:], inv_scale[:], CAP, None, ALU.min).then_inc(consts, 1)
            dve.wait_ge(own_act, 2)
            step.link(dve.tensor_tensor(inv_scale[:], inv_scale[:], scale_e[:], ALU.max))
            step.link(dve.reciprocal(inv_scale[:], inv_scale[:]))
            with dve.Fori(0, B) as b:
                step = Steps(dve, own_dve, b * 9, 9)
                step.wait()
                dve.wait_ge(out_taken, b)
                dve.wait_ge(projected, b * 3 + 1)
                bias = lambda v: v[:].unsqueeze(1).to_broadcast([P, TT, D])
                tile = lambda n: psum[:, n, :].rearrange("p (t d) -> p t d", t=TT)
                step.did(dve.tensor_tensor(f[:, TT:2 * TT, :], tile(0), bias(bk), ALU.add))
                dve.wait_ge(projected, b * 3 + 2)
                step.link(dve.tensor_tensor(f[:, 0:TT, :], tile(1), bias(bq), ALU.add))
                step.link(dve.tensor_scalar(f[:], f[:], 0.0, FOCUS_EPS, ALU.max, ALU.add))
                dve.tensor_tensor(f[:], f[:], inv_scale[:].unsqueeze(1).to_broadcast([P, 2 * TT, D]), ALU.mult)\
                   .then_inc(features_raw, 1)
                dve.wait_ge(projected, b * 3 + 3)
                for t in range(TT):
                    step.did(dve.tensor_tensor(v1[:, t, :, 0:P], psum[:, 2, t * D:(t + 1) * D].rearrange("p (c d) -> p c d", c=CC),
                                               bv[:].rearrange("p (c d) -> p c d", c=CC), ALU.add))
                dve.wait_ge(squared, b + 1)
                dve.wait_ge(features_raw, b + 1)
                dve.tensor_tensor(f3[:], f2[:], f[:], ALU.mult).then_inc(cubed, 1)
                dve.wait_ge(sixth, b + 1)
                step.link(dve.reciprocal(factor[:], norm6[:]))
                dve.tensor_tensor(factor[:], factor[:], norm2[:], ALU.mult).then_inc(ratio_ready, 1)
                dve.wait_ge(factor_ready, b + 1)
                dve.wait_ge(cubed, b + 1)
                for i in range(2 * TT):
                    ins = dve.tensor_scalar(f3[:, i, :], f3[:, i, :], factor[:, i:i + 1], None, ALU.mult)
                ins.then_inc(features, 1)
                dve.wait_ge(kv_summed, b + 1)
                for c in range(CC):
                    lo = c * (P + 1)
                    dve.tensor_tensor(kv[:, c, 0:P], psum[:, 3, lo:lo + P], same_head[:], ALU.mult)
                    ins = dve.tensor_tensor(kv[:, c, P:KVW], psum[:, 3, lo + P:lo + P + 1].to_broadcast([P, HEADS_IN_CHUNK]),
                                            head_mask[:], ALU.mult)
                ins.then_inc(kv_ready, 1)
                dve.wait_ge(out_ready, b + 1)
                outs = psum[:, 5:5 + TT, 0:CC * KVW].rearrange("p t (c n) -> p t c n", c=CC)
                step.link(dve.tensor_scalar(z[:], outs[:, :, :, P:KVW], FOCUS_EPS, None, ALU.add))
                step.link(dve.reciprocal(z[:], z[:]))
                for t in range(TT):
                    ins = dve.tensor_tensor(o[:, t, :].rearrange("p (c h d) -> p c h d", c=CC, h=HEADS_IN_CHUNK),
                                            outs[:, t, :, 0:P].rearrange("p c (h d) -> p c h d", h=HEADS_IN_CHUNK),
                                            z[:, t].unsqueeze(3).to_broadcast([P, CC, HEADS_IN_CHUNK, P // HEADS_IN_CHUNK]),
                                            ALU.mult)
                step.link(ins)
                x_b = x_all[:, bass.ds(b * TT, TT), :]
                dve.tensor_tensor(x_b, x_b, o[:], ALU.add).then_inc(out_taken, 1)
                step.end()


def scores_softmax_value_order(units):
    for u in range(units + 2):
        if u < units:
            yield "scores", u
        if 1 <= u <= units:
            yield "turn", u - 1
        if u >= 2:
            yield "values", u - 2


def top2(dve, step, v, mask, work, red, rev, groups):
    wide = lambda r: r.unsqueeze(2).to_broadcast([P, groups, 8])
    eq, rest = work
    for rank in range(2):
        src = v if rank == 0 else rest
        step.link(dve.tensor_reduce(red, src, AX.X, ALU.max))
        step.link(dve.tensor_tensor(eq, src, wide(red), ALU.is_equal))
        step.link(dve.tensor_tensor(eq, eq, rev.unsqueeze(1).to_broadcast([P, groups, 8]), ALU.mult))
        step.link(dve.tensor_reduce(red, eq, AX.X, ALU.max))
        step.link(dve.tensor_tensor(eq, eq, wide(red), ALU.is_equal))
        if rank == 0:
            step.did(dve.tensor_copy(mask, eq))
            step.link(dve.scalar_tensor_tensor(rest, eq, -3e38, v, ALU.mult, ALU.add))
        else:
            step.link(dve.tensor_tensor(mask, mask, eq, ALU.add))


TOP2_STEPS = 13


SH, SDH, SE = 16, 64, 8
SG = SH * SE
QK_ITEMS = 8
MIX_HEADS = 4
KO = SE * SDH // P

SW_BESIDE = {1: [("qk", 6, HERE)], 2: [("qk", 7, HERE)], 4: [("turn", 0, OLD)], 5: [("turn", 1, OLD), ("qk", 0, AHEAD)],
             6: [("qk", 1, AHEAD)], 7: [("out", 0, OLD)], 9: [("qk", 2, AHEAD)], 10: [("qk", 3, AHEAD)],
             13: [("qk", 4, AHEAD)], 14: [("qk", 5, AHEAD)]}


def switch_attention(nc, norm, x_all, xnT_all, ident, psum, a):
    with ExitStack() as stack:
        s = Scope(nc, stack, "f0")
        pv_all = s.sb("pv_all", [P, TILES, SE * SDH])
        mix_all = s.sb("mix_all", [P, TILES, SG])
        pick_all = s.sb("pick_all", [P, TILES, SG])
        wg, wv = s.sb("wg", [P, CC, 2 * SG]), s.sb("wv", [P, CC, SE * SDH])
        wq, wk = s.sb("wq", [P, CC, SH * SDH]), s.sb("wk", [P, CC, SH * SDH])
        wo = s.sb("wo", [P, KO, D])
        rev = s.sb("rev", [P, 8])
        loaded = s.sem("loaded")
        loads = [(wg[:], chunked(a["wg"])), (wv[:], chunked(a["wv"])), (rev[:], over_partitions(a["rev"], 8)),
                 (wq[:], chunked(a["wq"])), (wk[:], chunked(a["wk"])), (wo[:], chunked(a["wo"]))]
        normalise(nc, norm, x_all, xnT_all, ident, psum, loads, loaded)

        xnT = s.sb("xnT", [P, CC, T])
        NG = TT * 2 * SH
        gate, mask, eq, rest = (s.sb(n, [P, NG, 8]) for n in ("gate", "mask", "eq", "rest"))
        sig = s.sb("sig", [P, TT, SG])
        red = s.sb("red", [P, NG])
        gates_x_here, projected, gates_taken, values_taken, sig_ready, own_gates, chosen = (
            s.sem(n) for n in ("gates_x_here", "projected", "gates_taken", "values_taken", "sig_ready", "own_gates",
                               "chosen"))
        qT, kT = s.sb("qT", [P, QK_ITEMS, T]), s.sb("kT", [P, QK_ITEMS, T])
        pv = s.sb("pv", [P, TT, SE, SDH])
        mix = s.sb("mix", [P, TT, SH, SE])
        pick = s.sb("pick", [P, TT, SH, SE])
        prod = s.sb("prod", [P, MIX_HEADS, SE, SDH])
        v = s.sb("v", [P, TT, SH, SDH])
        weights, turned_w = s.sb("weights", [P, 2, TT, T]), s.sb("turned_w", [P, 2, TT, T])
        negmax, sums = s.sb("negmax", [P, SH, TT]), s.sb("sums", [P, SH, TT])
        pick_s = s.sb("pick_s", [P, 2, TT, SE])
        picked = s.sb("picked", [P, TT, SE, SDH])
        u, u_b = s.sb("u", [P, TT, SE, SDH]), s.sb("u_b", [P, TT, SE * SDH])
        uT = s.sb("uT", [P, TT, KO, P])
        qk_ready, qk_taken, mix_here, v_ready = (s.sem(n) for n in ("qk_ready", "qk_taken", "mix_here", "v_ready"))
        scored, max_ready, exp_done, turned, turned_taken, summed, head_taken = (
            s.sem(n) for n in ("scored", "max_ready", "exp_done", "turned", "turned_taken", "summed", "head_taken"))
        inverted, pick_ready, pick_here, added, u_copied, u_turned, uT_ready, out_ready, out_taken = (
            s.sem(n) for n in ("inverted", "pick_ready", "pick_here", "added", "u_copied", "u_turned", "uT_ready",
                               "out_ready", "out_taken"))
        own_pool, passed = s.sem("own_pool"), s.sem("passed")
        block = stack.enter_context(nc.Block())
        beside, ending = psum[:, 2, :], psum[:, 3, :]

        @block.sync
        def _(sp):
            with sp.Fori(0, B) as b:
                sp.wait_ge(projected, b * 3)
                sp.dma_start(xnT[:], xnT_all[:, bass.ds(b, 1), :, :]).then_inc(gates_x_here, 16)
            with sp.Fori(0, B) as b:
                sp.wait_ge(chosen, b + 1)
                sp.wait_ge(values_taken, b + 1)
                sp.wait_ge(v_ready, b * SH // MIX_HEADS)
                sp.dma_start(pv[:].rearrange("p t e d -> p t (e d)"), pv_all[:, bass.ds(b * TT, TT), :])\
                  .then_inc(mix_here, 16)
                sp.dma_start(mix[:].rearrange("p t h e -> p t (h e)"), mix_all[:, bass.ds(b * TT, TT), :])\
                  .then_inc(mix_here, 16)

        @block.gpsimd
        def _(pool):
            GROUPS = SH // MIX_HEADS
            per = GROUPS * (TT * 4 - 1)

            def mix_values(b, first):
                step = Steps(pool, own_pool, b * per, per)
                alone(pool, mix_here, b * 32 + 32, passed)
                for h0 in range(0, SH, MIX_HEADS):
                    if not first:
                        alone(pool, summed, b * SH + h0 + MIX_HEADS - SH, passed)
                    for t in range(TT):
                        if t:
                            alone(pool, own_pool, step.base + step.n, passed)
                        else:
                            wait_alone(pool, v_ready, b * GROUPS + h0 // MIX_HEADS, passed)
                        step.did(pool.tensor_tensor(
                            prod[:], pv[:, t].unsqueeze(1).to_broadcast([P, MIX_HEADS, SE, SDH]),
                            mix[:, t, h0:h0 + MIX_HEADS, :].unsqueeze(3).to_broadcast([P, MIX_HEADS, SE, SDH]), ALU.mult))
                        for half in (4, 2, 1):
                            alone(pool, own_pool, step.base + step.n, passed)
                            out = prod[:, :, 0:half, :] if half > 1 else v[:, t, h0:h0 + MIX_HEADS, :].unsqueeze(2)
                            ins = pool.tensor_tensor(out, prod[:, :, 0:half, :], prod[:, :, half:2 * half, :], ALU.add)
                            if (t, half) == (TT - 1, 1):
                                ins.then_inc(v_ready, 1)
                            else:
                                step.did(ins)
                step.end()

            mix_values(0, True)
            with pool.Fori(0, B - 1) as i:
                mix_values(i + 1, False)

        @block.tensor
        def _(pe):
            pe.wait_ge(loaded, 16 * len(loads))
            with pe.Fori(0, B) as b:
                pe.wait_ge(gates_x_here, b * 16 + 16)
                pe.wait_ge(gates_taken, b)
                for t in range(TT):
                    for c in range(CC):
                        ins = pe.matmul(psum[:, 0, t * D:(t + 1) * D], xnT[:, c, t * P:(t + 1) * P], wg[:, c, :],
                                        start=(c == 0), stop=(c == CC - 1))
                ins.then_inc(projected, 1)
                pe.wait_ge(values_taken, b)
                for t in range(TT):
                    for c in range(CC):
                        ins = pe.matmul(psum[:, 1 + t, :], xnT[:, c, t * P:(t + 1) * P], wv[:, c, :],
                                        start=(c == 0), stop=(c == CC - 1))
                    ins.then_inc(projected, 1)
            pe.wait_ge(gates_taken, B)
            pe.wait_ge(values_taken, B)

            def beside_head(b, kind, i, when):
                bb = b + {HERE: 0, AHEAD: 1, OLD: -1}[when]
                if kind == "qk":
                    w = (wq, wk)[i % 2]
                    wait(pe, qk_taken, bb * QK_ITEMS + i)
                    for j in range(2):
                        lo = (i // 2 * 2 + j) * P
                        for c in range(CC):
                            ins = pe.matmul(beside[:, j * T:(j + 1) * T], w[:, c, lo:lo + P],
                                            xnT_all[:, bass.ds(bb, 1), c, :], start=(c == 0), stop=(c == CC - 1))
                    ins.then_inc(qk_ready, 1)
                elif kind == "turn":
                    pe.wait_ge(u_copied, bb + 1)
                    if i:
                        pe.wait_ge(uT_ready, bb * TT + i)
                    else:
                        wait(pe, out_taken, bb)
                    for k in range(KO):
                        ins = pe.transpose(ending[:, k * P:(k + 1) * P], u_b[:, i, k * P:(k + 1) * P], ident[:])
                    ins.then_inc(u_turned, 1)
                else:
                    pe.wait_ge(uT_ready, bb * TT + TT)
                    for t in range(TT):
                        for k in range(KO):
                            ins = pe.matmul(ending[:, t * D:(t + 1) * D], uT[:, t, k, :], wo[:, k, :],
                                            start=(k == 0), stop=(k == KO - 1))
                    ins.then_inc(out_ready, 1)

            def body(b, new, ahead, old):
                exists = {HERE: new, AHEAD: ahead, OLD: old}
                turning, valuing = list(units(b, 1, new, old)), list(units(b, 2, new, old))
                for j in range(SH):
                    n = b * SH + j
                    if new:
                        if j % 4 == 0:
                            pe.wait_ge(qk_taken, b * QK_ITEMS + j // 2 + 2)
                        wait(pe, exp_done, n - 1)
                        r0 = SDH * (j % 2)
                        for t in range(TT):
                            ins = pe.matmul(psum[:, 6 + j % 2, t * T:(t + 1) * T], qT[r0:r0 + SDH, j // 2, t * P:(t + 1) * P],
                                            kT[r0:r0 + SDH, j // 2, :], start=True, stop=True)
                        ins.then_inc(scored, 1)
                    for kind, i, when in SW_BESIDE.get(j, []):
                        if exists[when]:
                            beside_head(b, kind, i, when)
                    if valuing[j]:
                        k, n = valuing[j]
                        if k % MIX_HEADS == 0:
                            pe.wait_ge(v_ready, (b if j >= 2 else b - 1) * (SH // MIX_HEADS) + k // MIX_HEADS + 1)
                        pe.wait_ge(turned_taken, n + 1)
                        wait(pe, head_taken, n - 1)
                        for t in range(TT):
                            for half in range(TT):
                                ins = pe.matmul(psum[:, k % 2, t * SDH:(t + 1) * SDH],
                                                turned_w[:, k % 2, half, t * P:(t + 1) * P], v[:, half, k, :],
                                                start=(half == 0), stop=(half == TT - 1))
                        ins.then_inc(summed, 1)
                    if turning[j]:
                        k, n = turning[j]
                        pe.wait_ge(exp_done, n + 1)
                        wait(pe, turned_taken, n - 1)
                        for half in range(TT):
                            for t in range(TT):
                                lo = half * T + t * P
                                ins = pe.transpose(psum[:, 4 + k % 2, lo:lo + P],
                                                   weights[:, k % 2, t, half * P:(half + 1) * P], ident[:])
                        ins.then_inc(turned, 1)

            over_batches(pe, body)

        @block.scalar
        def _(act):
            with act.Fori(0, B) as b:
                act.wait_ge(projected, b * 3 + 1)
                act.wait_ge(chosen, b)
                act.activation(sig[:], psum[:, 0, :].rearrange("p (t n) -> p t n", t=TT)[:, :, 0:SG], ACT.Sigmoid)\
                   .then_inc(sig_ready, 1)
                act.wait_ge(projected, b * 3 + 3)
                act.activation(pv_all[:, bass.ds(b * TT, TT), :], psum[:, 1:1 + TT, :], ACT.Copy)\
                   .then_inc(values_taken, 1)

            def body(b, new, ahead, old):
                exists = {HERE: new, AHEAD: ahead, OLD: old}
                turning = list(units(b, 1, new, old))
                for j in range(SH):
                    n = b * SH + j
                    if new:
                        act.wait_ge(max_ready, n + 1)
                        wait(act, turned, n - 1)
                        for t in range(TT):
                            ins = act.activation(weights[:, j % 2, t, :], psum[:, 6 + j % 2, t * T:(t + 1) * T], ACT.Exp,
                                                 bias=negmax[:, j, t:t + 1], accum_out=sums[:, j, t:t + 1])
                        ins.then_inc(exp_done, 1)
                    for kind, i, when in SW_BESIDE.get(j, []):
                        if not exists[when]:
                            continue
                        bb = b + {HERE: 0, AHEAD: 1, OLD: -1}[when]
                        if kind == "qk":
                            act.wait_ge(qk_ready, bb * QK_ITEMS + i + 1)
                            m = i // 2
                            act.activation((qT, kT)[i % 2][:, 2 * m:2 * m + 2, :], beside.rearrange("p (j t) -> p j t", j=2),
                                           ACT.Copy, scale=(SDH ** -0.5 if i % 2 == 0 else 1.0)).then_inc(qk_taken, 1)
                        elif kind == "turn":
                            act.wait_ge(u_turned, bb * TT + i + 1)
                            act.activation(uT[:, i], ending.rearrange("p (k n) -> p k n", k=KO), ACT.Copy).then_inc(uT_ready, 1)
                    if turning[j]:
                        k, n = turning[j]
                        act.wait_ge(turned, n + 1)
                        wait(act, summed, n - 1)
                        act.activation(turned_w[:, k % 2], psum[:, 4 + k % 2, :].rearrange("p (j t) -> p j t", j=TT),
                                       ACT.Copy).then_inc(turned_taken, 1)
                    if old and j == 2:
                        act.wait_ge(added, b * (SH - 1))
                        wait(act, u_turned, (b - 1) * TT)
                        act.activation(u_b[:], u[:].rearrange("p t e d -> p t (e d)"), ACT.Copy).then_inc(u_copied, 1)

            over_batches(act, body)

        @block.vector
        def _(dve):
            dve.wait_ge(loaded, 16 * len(loads))
            with dve.Fori(0, B) as b:
                step = Steps(dve, own_gates, b * TOP2_STEPS, TOP2_STEPS)
                dve.wait_ge(chosen, b)
                step.wait()
                dve.wait_ge(projected, b * 3 + 1)
                dve.wait_ge(sig_ready, b + 1)
                dve.tensor_copy(gate[:].rearrange("p g e -> p (g e)"), psum[:, 0, :]).then_inc(gates_taken, 1)
                dve.wait_ge(gates_taken, b + 1)
                top2(dve, step, gate[:], mask[:], (eq[:], rest[:]), red[:], rev[:], NG)
                m = mask[:].rearrange("p (t n) e -> p t (n e)", t=TT)
                dve.tensor_tensor(mix_all[:, bass.ds(b * TT, TT), :], sig[:], m[:, :, 0:SG], ALU.mult)
                dve.tensor_copy(pick_all[:, bass.ds(b * TT, TT), :], m[:, :, SG:2 * SG]).then_inc(chosen, 1)
                step.end()
            dve.wait_ge(chosen, B)

            def body(b, new, ahead, old):
                finishing = list(units(b, 3, new, old))
                for j in range(SH):
                    n = b * SH + j
                    if new:
                        dve.wait_ge(scored, n + 1)
                        dve.tensor_reduce(negmax[:, j, :], psum[:, 6 + j % 2, :].rearrange("p (t j) -> p t j", t=TT),
                                          AX.X, ALU.max, negate=True).then_inc(max_ready, 1)
                    if finishing[j]:
                        k, n = finishing[j]
                        bb = b if j >= 3 else b - 1
                        dve.wait_ge(exp_done, n + 1)
                        dve.reciprocal(sums[:, k, :], sums[:, k, :]).then_inc(inverted, 1)
                        if k == 0:
                            wait(dve, pick_ready, bb * SH)
                            dve.tensor_copy(pick[:].rearrange("p t h e -> p t (h e)"),
                                            pick_all[:, bass.ds(bb * TT, TT), :]).then_inc(pick_here, 1)
                            dve.wait_ge(pick_here, bb + 1)
                        dve.wait_ge(inverted, n + 1)
                        wait(dve, head_taken, n - 1)
                        dve.tensor_tensor(pick_s[:, k % 2], pick[:, :, k, :],
                                          sums[:, k, :].unsqueeze(2).to_broadcast([P, TT, SE]), ALU.mult).then_inc(pick_ready, 1)
                        dve.wait_ge(summed, n + 1)
                        dve.wait_ge(pick_ready, n + 1)
                        if k == 0:
                            wait(dve, u_copied, bb)
                        else:
                            wait(dve, added, bb * (SH - 1) + k - 1)
                        for t in range(TT):
                            ins = dve.tensor_tensor(
                                (u if k == 0 else picked)[:, t],
                                psum[:, k % 2, t * SDH:(t + 1) * SDH].unsqueeze(1).to_broadcast([P, SE, SDH]),
                                pick_s[:, k % 2, t].unsqueeze(2).to_broadcast([P, SE, SDH]), ALU.mult)
                        ins.then_inc(head_taken, 1)
                        if k:
                            dve.wait_ge(head_taken, n + 1)
                            dve.tensor_tensor(u[:], u[:], picked[:], ALU.add).then_inc(added, 1)
                    if old and j == 8:
                        x_b = x_all[:, bass.ds((b - 1) * TT, TT), :]
                        dve.wait_ge(out_ready, b)
                        dve.tensor_tensor(x_b, ending.rearrange("p (t d) -> p t d", t=TT), x_b, ALU.add).then_inc(out_taken, 1)

            over_batches(dve, body)


def turn_and_project(pe, psum, ident, o, oT, w, turned, turned_taken, out_ready, b, chunks):
    for t in range(TT):
        for g in range(chunks // 4):
            for i in range(4):
                lo = (4 * g + i) * P
                ins = pe.transpose(psum[:, 2 * t + g, i * P:(i + 1) * P], o[:, t, lo:lo + P], ident[:])
            ins.then_inc(turned, 1)
    pe.wait_ge(turned_taken, b * 4 + 4)
    for t in range(TT):
        for k in range(chunks):
            ins = pe.matmul(psum[:, 4, t * D:(t + 1) * D], oT[:, t, k, :], w[:, k, :], start=(k == 0),
                            stop=(k == chunks - 1))
    ins.then_inc(out_ready, 1)


def take_turned_output(act, psum, oT, turned, turned_taken, b):
    for n in range(4):
        act.wait_ge(turned, b * 4 + n + 1)
        act.activation(oT[:, n // 2, 4 * (n % 2):4 * (n % 2) + 4, :], psum[:, n, :].rearrange("p (k n) -> p k n", n=P),
                       ACT.Copy).then_inc(turned_taken, 1)


AH, AD = 8, 128
KEYS, CTX = 1024, 192
KB = KEYS // P
SHARPEN = 1.5


def attention1(nc, norm, x_all, xnT_all, ident, psum, a):
    with ExitStack() as stack:
        s = Scope(nc, stack, "a1")
        wq, wo = s.sb("wq", [P, CC, AH * AD]), s.sb("wo", [P, AH, D])
        wk, wv = s.sb("wk", [P, 2, AH * AD]), s.sb("wv", [P, 2, AH * AD])
        bo = s.sb("bo", [P, D])
        ctxT = s.sb("ctxT", [P, 2, KEYS])
        kT = [s.sb(f"kT_{part}", [P, AH, KEYS], F32R) for part in ("hi", "lo")]
        qT = [s.sb(f"qT_{part}", [P, AH, T], F32R) for part in ("hi", "lo")]
        v = s.sb("v", [P, KB, AH * AD])
        xnT = s.sb("xnT", [P, CC, T])
        weights = [s.sb(f"weights{i}", [P, KEYS]) for i in range(2)]
        turned_w = s.sb("turned_w", [P, 2, KEYS])
        U = AH * TT
        negmax, sums = s.sb("negmax", [P, U]), s.sb("sums", [P, U])
        o, oT = wk, turned_w[:].rearrange("p t (h d) -> p t h d", h=AH)
        loaded, x_here = s.sem("loaded"), s.sem("x_here")
        kv_ready, kv_act, kv_dve = s.sem("kv_ready"), s.sem("kv_act"), s.sem("kv_dve")
        q_ready, q_high, q_taken, scored, max_ready, exp_done, turned = (
            s.sem(n) for n in ("q_ready", "q_high", "q_taken", "scored", "max_ready", "exp_done", "turned"))
        half_taken = s.sems("half_taken", 2)
        summed, head_taken, own = s.sem("summed"), s.sem("head_taken"), s.sem("own")
        o_turned, o_turned_taken, out_ready, out_taken = (
            s.sem(n) for n in ("o_turned", "o_turned_taken", "out_ready", "out_taken"))
        loads = []
        for dst, src in ((ctxT, a["ctxT"]), (wk, a["wk"]), (wv, a["wv"])):
            loads += [(dst[:, 0, :], src[0:P, :]), (dst[0:CTX - P, 1, :], src[P:CTX, :])]
        loads += [(wq[:], chunked(a["wq"])), (wo[:], chunked(a["wo"])), (bo[:], over_partitions(a["bo"], D))]
        normalise(nc, norm, x_all, xnT_all, ident, psum, loads, loaded)
        block = stack.enter_context(nc.Block())
        HALF = KEYS // 2
        parts = [("k", h, half) for h in range(AH) for half in range(2)] + \
                [("v", st, half) for st in range(KB) for half in range(2)]

        KP = 2 * AH
        act_did = lambda n: n + 1 if n < KP else KP + (n - KP) // 2 + 1
        dve_did = lambda n: n + 1 if n < KP else KP + (n - KP + 1) // 2

        @block.sync
        def _(sp):
            with sp.Fori(0, B) as b:
                sp.wait_ge(q_ready, b * 4)
                sp.dma_start(xnT[:], xnT_all[:, bass.ds(b, 1), :, :]).then_inc(x_here, 16)

        @block.tensor
        def _(pe):
            pe.wait_ge(loaded, 16 * len(loads))
            for n, (kind, i, half) in enumerate(parts):
                if n >= 8:
                    if n - 8 < KP or n % 2 == 1:
                        pe.wait_ge(kv_dve, dve_did(n - 8))
                    else:
                        pe.wait_ge(kv_act, act_did(n - 8))
                for c, rows in enumerate((P, CTX - P)):
                    if kind == "k":
                        ins = pe.matmul(psum[:, n % 8, :], wk[0:rows, c, i * AD:(i + 1) * AD],
                                        ctxT[0:rows, c, half * HALF:(half + 1) * HALF], start=(c == 0), stop=(c == 1))
                    else:
                        ins = pe.matmul(psum[:, n % 8, :], ctxT[0:rows, c, i * P:(i + 1) * P],
                                        wv[0:rows, c, half * HALF:(half + 1) * HALF], start=(c == 0), stop=(c == 1))
                ins.then_inc(kv_ready, 1)
            pe.wait_ge(kv_act, act_did(len(parts) - 1))
            pe.wait_ge(kv_dve, dve_did(len(parts) - 1))
            with pe.Fori(0, B) as b:
                S0 = b * U
                pe.wait_ge(x_here, b * 16 + 16)
                pe.wait_ge(out_taken, b)
                for m in range(AH // 2):
                    if m >= 2:
                        pe.wait_ge(q_taken, b * 4 + m - 1)
                    for j in range(2):
                        for c in range(CC):
                            lo = (2 * m + j) * AD
                            ins = pe.matmul(psum[:, 6 + m % 2, j * T:(j + 1) * T], wq[:, c, lo:lo + AD], xnT[:, c, :],
                                            start=(c == 0), stop=(c == CC - 1))
                    ins.then_inc(q_ready, 1)
                for what, k in scores_softmax_value_order(U):
                    h, t = k // TT, k % TT
                    if what == "scores":
                        if k == 0:
                            pe.wait_ge(q_taken, b * 4 + 4)
                        if k >= 2:
                            pe.wait_ge(exp_done, S0 + k - 1)
                        for half in range(2):
                            ins = split_product(pe, psum[:, 2 * (k % 2) + half, :],
                                                [q[:, h, t * P:(t + 1) * P] for q in qT],
                                                [keys[:, h, half * HALF:(half + 1) * HALF] for keys in kT], True, True)
                        ins.then_inc(scored, 1)
                    elif what == "turn":
                        pe.wait_ge(exp_done, S0 + k + 1)
                        for half in range(2):
                            pe.wait_ge(half_taken[half], S0 + k)
                            for j in range(4):
                                lo = half * HALF + j * P
                                ins = pe.transpose(psum[:, 4 + half, j * P:(j + 1) * P], weights[k % 2][:, lo:lo + P],
                                                   ident[:])
                            ins.then_inc(turned, 1)
                    else:
                        for half in range(2):
                            pe.wait_ge(half_taken[half], S0 + k + 1)
                        if k >= 2:
                            pe.wait_ge(head_taken, S0 + k - 1)
                        for j in range(KB):
                            ins = pe.matmul(psum[:, 6 + k % 2, 0:AD], turned_w[:, k % 2, j * P:(j + 1) * P],
                                            v[:, j, h * AD:(h + 1) * AD], start=(j == 0), stop=(j == KB - 1))
                        ins.then_inc(summed, 1)
                pe.wait_ge(head_taken, S0 + U)
                turn_and_project(pe, psum, ident, o, oT, wo, o_turned, o_turned_taken, out_ready, b, AH)

        def part_of(to, n):
            kind, i, half = parts[n]
            return to[:, i, half * HALF:(half + 1) * HALF]

        @block.scalar
        def _(act):
            for n in [*range(KP), *range(KP, len(parts), 2)]:
                act.wait_ge(kv_ready, n + 1)
                act.activation(part_of(kT[0] if n < KP else v, n), psum[:, n % 8, :], ACT.Copy).then_inc(kv_act, 1)
            with act.Fori(0, B) as b:
                S0 = b * U
                for m in range(AH // 2):
                    act.wait_ge(q_ready, b * 4 + m + 1)
                    act.activation(qT[0][:, 2 * m:2 * m + 2, :], psum[:, 6 + m % 2, :].rearrange("p (j t) -> p j t", j=2),
                                   ACT.Copy, scale=SHARPEN * AD ** -0.5).then_inc(q_high, 1)

                def exps(k):
                    act.wait_ge(max_ready, S0 + k + 1)
                    if k >= 2:
                        act.wait_ge(turned, 2 * (S0 + k - 1))
                    act.activation(weights[k % 2][:], psum[:, 2 * (k % 2):2 * (k % 2) + 2, :].rearrange("p a n -> p (a n)"),
                                   ACT.Exp, bias=negmax[:, k:k + 1], accum_out=sums[:, k:k + 1]).then_inc(exp_done, 1)

                def take_half(k):
                    act.wait_ge(turned, 2 * (S0 + k) + 2)
                    if k >= 2:
                        act.wait_ge(summed, S0 + k - 1)
                    act.activation(turned_w[:, k % 2, HALF:KEYS], psum[:, 5, :], ACT.Copy).then_inc(half_taken[1], 1)

                for k in range(U):
                    exps(k)
                    if k >= 1:
                        take_half(k - 1)
                take_half(U - 1)
                take_turned_output(act, psum, oT, o_turned, o_turned_taken, b)

        @block.vector
        def _(dve):
            for n in range(KP):
                dve.wait_ge(kv_act, n + 1)
                dve.tensor_tensor(part_of(kT[1], n), psum[:, n % 8, :], part_of(kT[0], n).bitcast(F32), ALU.subtract)\
                   .then_inc(kv_dve, 1)
            for n in range(KP + 1, len(parts), 2):
                dve.wait_ge(kv_ready, n + 1)
                dve.tensor_copy(part_of(v, n), psum[:, n % 8, :]).then_inc(kv_dve, 1)
            with dve.Fori(0, B) as b:
                step = Steps(dve, own, b * (U + 1), U + 1)
                S0 = b * U
                dve.wait_ge(out_taken, b)
                x_b = x_all[:, bass.ds(b * TT, TT), :]
                step.did(dve.tensor_tensor(x_b, x_b, bo[:].unsqueeze(1).to_broadcast([P, TT, D]), ALU.add))
                for m in range(AH // 2):
                    dve.wait_ge(q_high, b * 4 + m + 1)
                    dve.scalar_tensor_tensor(qT[1][:, 2 * m:2 * m + 2, :], psum[:, 6 + m % 2, :].rearrange("p (j t) -> p j t", j=2),
                                             SHARPEN * AD ** -0.5, qT[0][:, 2 * m:2 * m + 2, :].bitcast(F32), ALU.mult,
                                             ALU.subtract).then_inc(q_taken, 1)

                def row_max(k):
                    dve.wait_ge(scored, S0 + k + 1)
                    dve.tensor_reduce(negmax[:, k:k + 1], psum[:, 2 * (k % 2):2 * (k % 2) + 2, :].rearrange("p a n -> p (a n)"),
                                      AX.X, ALU.max, negate=True).then_inc(max_ready, 1)

                def take_half(k):
                    dve.wait_ge(turned, 2 * (S0 + k) + 1)
                    if k >= 2:
                        dve.wait_ge(summed, S0 + k - 1)
                    dve.tensor_copy(turned_w[:, k % 2, 0:HALF], psum[:, 4, :]).then_inc(half_taken[0], 1)

                def take_head(k):
                    h, t = k // TT, k % TT
                    dve.wait_ge(exp_done, S0 + k + 1)
                    step.link(dve.reciprocal(sums[:, k:k + 1], sums[:, k:k + 1]))
                    dve.wait_ge(summed, S0 + k + 1)
                    dve.tensor_scalar(o[:, t, h * AD:(h + 1) * AD], psum[:, 6 + k % 2, 0:AD], sums[:, k:k + 1], None,
                                      ALU.mult).then_inc(head_taken, 1)

                for k in range(U):
                    row_max(k)
                    if k >= 1:
                        take_half(k - 1)
                    if k >= 2:
                        take_head(k - 2)
                take_half(U - 1)
                take_head(U - 2)
                take_head(U - 1)
                step.wait()
                dve.wait_ge(out_ready, b + 1)
                dve.tensor_tensor(x_b, psum[:, 4, :].rearrange("p (t d) -> p t d", t=TT), x_b, ALU.add).then_inc(out_taken, 1)
                step.end()


CH, CD = 16, 64
MASKED = -1e9


CROSS_BESIDE = {1: [("qk", 6, HERE)], 2: [("qk", 7, HERE)], 3: [("turn", 2, OLD), ("v", 2, HERE)],
                4: [("turn", 3, OLD), ("v", 3, HERE)], 5: [("qk", 0, AHEAD)], 6: [("qk", 1, AHEAD)], 7: [("out", 0, OLD)],
                9: [("qk", 2, AHEAD)], 10: [("qk", 3, AHEAD)], 11: [("turn", 0, HERE), ("v", 0, AHEAD)],
                12: [("turn", 1, HERE), ("v", 1, AHEAD)], 13: [("qk", 4, AHEAD)], 14: [("qk", 5, AHEAD)]}


def cross_attention1(nc, norm, x_all, xnT_all, ident, psum, a):
    with ExitStack() as stack:
        s = Scope(nc, stack, "x1")
        HD = CH * CD
        QK, V, TURNS = HD // P, 4, 4
        HALF = HD // 2
        wq, wk, wv = (s.sb(n, [P, CC, HD]) for n in ("wq", "wk", "wv"))
        wo, bo = s.sb("wo", [P, HD // P, D]), s.sb("bo", [P, D])
        mask_i, mask = s.sb("mask_i", [P, TT, T], I32), s.sb("mask", [P, TT, T])
        ctxT = s.sb("ctxT", [P, CC, T])
        qT, kT = ([s.sb(f"{n}_{part}", [P, HD // P, T], F32R) for part in ("hi", "lo")] for n in ("qT", "kT"))
        v = s.sb("v", [P, TT, HD])
        masked_s, weights, turned_w = (s.sb(n, [P, 2, TT, T]) for n in ("masked_s", "weights", "turned_w"))
        rowmax, negmax, sums = (s.sb(n, [P, CH, TT]) for n in ("rowmax", "negmax", "sums"))
        o, oT = s.sb("o", [P, TT, HD]), s.sb("oT", [P, TT, HD // P, P])
        loaded, ctx_here, own_setup, passed = (s.sem(n) for n in ("loaded", "ctx_here", "own_setup", "passed"))
        qk_ready, qk_high, qk_taken, v_ready, v_taken = (
            s.sem(n) for n in ("qk_ready", "qk_high", "qk_taken", "v_ready", "v_taken"))
        scored, maxed, max_ready, exp_done, turned, turned_taken, summed, inverted, head_taken = (
            s.sem(n) for n in ("scored", "maxed", "max_ready", "exp_done", "turned", "turned_taken", "summed",
                               "inverted", "head_taken"))
        o_turned, oT_ready, x_biased, out_ready, out_taken = (
            s.sem(n) for n in ("o_turned", "oT_ready", "x_biased", "out_ready", "out_taken"))
        loads = [(wv[:], chunked(a["wv"])), (wq[:], chunked(a["wq"])), (wk[:], chunked(a["wk"])),
                 (wo[:], chunked(a["wo"])), (bo[:], over_partitions(a["bo"], D)), (mask_i[:], chunked(a["mask"]))]
        normalise(nc, norm, x_all, xnT_all, ident, psum, loads, loaded)
        block = stack.enter_context(nc.Block())
        beside, ending = psum[:, 2, :], psum[:, 3, :]
        batch_of = {HERE: 0, AHEAD: 1, OLD: -1}
        scale_of = (CD ** -0.5, 1.0)

        @block.sync
        def _(sp):
            with sp.Fori(0, B) as b:
                sp.wait_ge(v_ready, b * V)
                sp.dma_start(ctxT[:], a["ctxT"][bass.ds(b * D, D), :].rearrange("(k p) n -> p k n", p=P))\
                  .then_inc(ctx_here, 16)

        @block.tensor
        def _(pe):
            pe.wait_ge(loaded, 16 * len(loads))
            free = None

            def beside_head(b, kind, i, when):
                nonlocal free
                bb = b + batch_of[when]
                if kind in ("qk", "v"):
                    for sem, value in free:
                        wait(pe, sem, value)
                if kind == "qk":
                    if i % 2:
                        pe.wait_ge(ctx_here, bb * 16 + 16)
                    for j in range(2):
                        lo = (i // 2 * 2 + j) * P
                        for c in range(CC):
                            src = ctxT[:, c, :] if i % 2 else xnT_all[:, bass.ds(bb, 1), c, :]
                            ins = pe.matmul(beside[:, j * T:(j + 1) * T], (wq, wk)[i % 2][:, c, lo:lo + P], src,
                                            start=(c == 0), stop=(c == CC - 1))
                    ins.then_inc(qk_ready, 1)
                    free = [(qk_taken, bb * QK + i + 1)]
                elif kind == "v":
                    t, half = i % 2, i // 2
                    pe.wait_ge(ctx_here, bb * 16 + 16)
                    for c in range(CC):
                        ins = pe.matmul(beside, ctxT[:, c, t * P:(t + 1) * P], wv[:, c, half * HALF:(half + 1) * HALF],
                                        start=(c == 0), stop=(c == CC - 1))
                    ins.then_inc(v_ready, 1)
                    free = [(v_taken, bb * V + i + 1)]
                elif kind == "turn":
                    t, half = i % 2, i // 2
                    pe.wait_ge(head_taken, bb * CH + 8 * half + 8)
                    wait(pe, oT_ready, bb * TURNS + i)
                    if i == 0:
                        wait(pe, out_taken, bb)
                    for k in range(4):
                        lo = (4 * half + k) * P
                        ins = pe.transpose(ending[:, k * P:(k + 1) * P], o[:, t, lo:lo + P], ident[:])
                    ins.then_inc(o_turned, 1)
                else:
                    pe.wait_ge(oT_ready, bb * TURNS + TURNS)
                    for t in range(TT):
                        for k in range(HD // P):
                            ins = pe.matmul(ending[:, t * D:(t + 1) * D], oT[:, t, k, :], wo[:, k, :], start=(k == 0),
                                            stop=(k == HD // P - 1))
                    ins.then_inc(out_ready, 1)

            def body(b, new, ahead, old):
                nonlocal free
                exists = {HERE: new, AHEAD: ahead, OLD: old}
                free = [(qk_taken, b * QK + 6)] if new else []
                turning, valuing = list(units(b, 1, new, old)), list(units(b, 2, new, old))
                for j in range(CH):
                    n = b * CH + j
                    if new:
                        if j % 4 == 0:
                            pe.wait_ge(qk_taken, b * QK + j // 2 + 2)
                        wait(pe, max_ready, n - 1)
                        r0 = CD * (j % 2)
                        for t in range(TT):
                            ins = split_product(pe, psum[:, 6 + j % 2, t * T:(t + 1) * T],
                                                [q[r0:r0 + CD, j // 2, t * P:(t + 1) * P] for q in qT],
                                                [k[r0:r0 + CD, j // 2, :] for k in kT], True, True)
                        ins.then_inc(scored, 1)
                    for kind, i, when in CROSS_BESIDE.get(j, []):
                        if exists[when]:
                            beside_head(b, kind, i, when)
                    if valuing[j]:
                        k, n = valuing[j]
                        if k % 8 == 0:
                            pe.wait_ge(v_taken, (b if j >= 2 else b - 1) * V + k // 4 + 2)
                        pe.wait_ge(turned_taken, n + 1)
                        wait(pe, head_taken, n - 1)
                        for t in range(TT):
                            for half in range(TT):
                                ins = pe.matmul(psum[:, k % 2, t * CD:(t + 1) * CD],
                                                turned_w[:, k % 2, half, t * P:(t + 1) * P], v[:, half, k * CD:(k + 1) * CD],
                                                start=(half == 0), stop=(half == TT - 1))
                        ins.then_inc(summed, 1)
                    if turning[j]:
                        k, n = turning[j]
                        pe.wait_ge(exp_done, n + 1)
                        wait(pe, turned_taken, n - 1)
                        for half in range(TT):
                            for t in range(TT):
                                lo = half * T + t * P
                                ins = pe.transpose(psum[:, 4 + k % 2, lo:lo + P],
                                                   weights[:, k % 2, t, half * P:(half + 1) * P], ident[:])
                        ins.then_inc(turned, 1)

            over_batches(pe, body)

        @block.scalar
        def _(act):
            def body(b, new, ahead, old):
                exists = {HERE: new, AHEAD: ahead, OLD: old}
                turning = list(units(b, 1, new, old))
                for j in range(CH):
                    n = b * CH + j
                    if new:
                        act.wait_ge(max_ready, n + 1)
                        wait(act, turned, n - 1)
                        for t in range(TT):
                            ins = act.activation(weights[:, j % 2, t, :], masked_s[:, j % 2, t, :], ACT.Exp,
                                                 bias=negmax[:, j, t:t + 1], accum_out=sums[:, j, t:t + 1])
                        ins.then_inc(exp_done, 1)
                    for kind, i, when in CROSS_BESIDE.get(j, []):
                        if not exists[when]:
                            continue
                        bb = b + batch_of[when]
                        if kind == "qk":
                            act.wait_ge(qk_ready, bb * QK + i + 1)
                            m = i // 2
                            act.activation((qT, kT)[i % 2][0][:, 2 * m:2 * m + 2, :],
                                           beside.rearrange("p (j t) -> p j t", j=2),
                                           ACT.Copy, scale=scale_of[i % 2]).then_inc(qk_high, 1)
                        elif kind == "turn":
                            act.wait_ge(o_turned, bb * TURNS + i + 1)
                            t, half = i % 2, i // 2
                            act.activation(oT[:, t, 4 * half:4 * half + 4, :], ending.rearrange("p (k n) -> p k n", k=4),
                                           ACT.Copy).then_inc(oT_ready, 1)
                    if turning[j]:
                        k, n = turning[j]
                        act.wait_ge(turned, n + 1)
                        wait(act, summed, n - 1)
                        act.activation(turned_w[:, k % 2], psum[:, 4 + k % 2, :].rearrange("p (j t) -> p j t", j=TT),
                                       ACT.Copy).then_inc(turned_taken, 1)

            over_batches(act, body)

        @block.vector
        def _(dve):
            dve.wait_ge(loaded, 16 * len(loads))
            step = Steps(dve, own_setup)
            step.link(dve.tensor_copy(mask[:], mask_i[:]))
            step.link(dve.tensor_scalar(mask[:], mask[:], 0.0, MASKED, ALU.is_equal, ALU.mult))

            def body(b, new, ahead, old):
                exists = {HERE: new, AHEAD: ahead, OLD: old}
                finishing = list(units(b, 3, new, old))
                for j in range(CH):
                    n = b * CH + j
                    if new:
                        wait(dve, exp_done, n - 1)
                        alone(dve, scored, n + 1, passed)
                        for t in range(TT):
                            ins = dve.tensor_tensor_reduce(masked_s[:, j % 2, t, :], psum[:, 6 + j % 2, t * T:(t + 1) * T],
                                                           mask[:, t, :], 1.0, -3e38, ALU.add, ALU.max, rowmax[:, j, t:t + 1])
                        ins.then_inc(maxed, 1)
                        dve.wait_ge(maxed, n + 1)
                        dve.tensor_scalar(negmax[:, j, :], rowmax[:, j, :], -1.0, None, ALU.mult).then_inc(max_ready, 1)
                    if finishing[j]:
                        k, n = finishing[j]
                        bb = b if j >= 3 else b - 1
                        dve.wait_ge(exp_done, n + 1)
                        dve.reciprocal(sums[:, k, :], sums[:, k, :]).then_inc(inverted, 1)
                        dve.wait_ge(summed, n + 1)
                        dve.wait_ge(inverted, n + 1)
                        if k % 8 == 0:
                            wait(dve, o_turned, (bb - 1) * TURNS + k // 4 + 2)
                        dve.tensor_tensor(o[:, :, k * CD:(k + 1) * CD],
                                          psum[:, k % 2, 0:TT * CD].rearrange("p (t d) -> p t d", t=TT),
                                          sums[:, k, :].unsqueeze(2).to_broadcast([P, TT, CD]), ALU.mult).then_inc(head_taken, 1)
                    for kind, i, when in CROSS_BESIDE.get(j, []):
                        bb = b + batch_of[when]
                        if exists[when] and kind == "qk":
                            m = i // 2
                            dve.wait_ge(qk_high, bb * QK + i + 1)
                            hi, lo = (part[:, 2 * m:2 * m + 2, :] for part in (qT, kT)[i % 2])
                            dve.scalar_tensor_tensor(lo, beside.rearrange("p (j t) -> p j t", j=2), scale_of[i % 2],
                                                     hi.bitcast(F32), ALU.mult, ALU.subtract).then_inc(qk_taken, 1)
                        if exists[when] and kind == "v":
                            t, half = i % 2, i // 2
                            dve.wait_ge(v_ready, bb * V + i + 1)
                            dve.tensor_copy(v[:, t, half * HALF:(half + 1) * HALF], beside).then_inc(v_taken, 1)
                    if old:
                        x_b = x_all[:, bass.ds((b - 1) * TT, TT), :]
                    if old and j == 5:
                        dve.tensor_tensor(x_b, x_b, bo[:].unsqueeze(1).to_broadcast([P, TT, D]), ALU.add).then_inc(x_biased, 1)
                    if old and j == 8:
                        dve.wait_ge(out_ready, b)
                        dve.wait_ge(x_biased, b)
                        dve.tensor_tensor(x_b, ending.rearrange("p (t d) -> p t d", t=TT), x_b, ALU.add).then_inc(out_taken, 1)

            over_batches(dve, body)


HID, NE, NGR = 512, 8, 2
PER_GROUP = NE // NGR


def experts(nc, norm, x_all, xnT_all, ident, psum, a):
    with ExitStack() as stack:
        s = Scope(nc, stack, "f1")
        KH = HID // P
        w_in, w1 = s.sb("w_in", [P, CC, 2 * HID]), s.sb("w1", [P, CC, 2 * HID])
        w_out, w2 = s.sb("w_out", [P, KH, D]), s.sb("w2", [P, KH // 2, NE * D])
        wg = s.sb("wg", [P, CC, NGR + NE])
        bg, rev = s.sb("bg", [P, NGR + NE]), s.sb("rev", [P, NE])
        xnT = s.sb("xnT", [P, CC, T])
        silu = s.sb("silu", [P, 2, T])
        hidden = s.sb("hidden", [P, 4, T])
        pair = lambda name, shape: tuple(s.sb(f"{name}_{part}", [P] + shape, F32R) for part in ("hi", "lo"))
        hid_pairs = [pair("w_in", [CC, 2 * HID]), pair("w1", [CC, 2 * HID])]
        out_pairs = [pair("w_out", [KH, D]), pair("w2", [KH, NE * D])]
        half = lambda n: tuple(w[:, n * KH // 2:(n + 1) * KH // 2, :] for w in out_pairs[1])
        split = [(w2, half(0))] + [(w, tuple(part[:] for part in parts)) for w, parts in (
            (w_in, hid_pairs[0]), (w1, hid_pairs[1]), (w_out, out_pairs[0]))] + [(w2, half(1))]
        hidden_hi, hidden_lo = pair("hidden", [2, KH, T])
        xnT_hi, xnT_lo = pair("xnT", [CC, T])
        parts = lambda halves, *at: tuple(half[at] for half in halves)
        high, low = s.sem("high"), s.sem("low")
        logits, top = s.sb("logits", [P, TT, NGR + NE]), s.sb("top", [P, TT, 1 + NGR])
        expd = s.sb("expd", [P, TT, NGR + NE])
        total = s.sb("total", [P, TT, 1 + NGR])
        chosen_group, group_p = s.sb("chosen_group", [P, TT, NGR]), s.sb("group_p", [P, TT])
        p, mask, eq, rest = (s.sb(n, [P, TT, NE]) for n in ("p", "mask", "eq", "rest"))
        red = s.sb("red", [P, TT])
        acc = s.sb("acc", [P, TT, D])
        loaded, x_here, projected, silu_done, hidden_taken = (
            s.sem(n) for n in ("loaded", "x_here", "projected", "silu_done", "hidden_taken"))
        gates_ready, shifted, exp_done, own = s.sem("gates_ready"), s.sem("shifted"), s.sem("exp_done"), s.sem("own")
        routed_ready, routed_taken = s.sem("routed_ready"), s.sem("routed_taken")
        loads = [(wg[:], chunked(a["wg"])), (w_in[:], chunked(a["w_in"])), (w1[:], chunked(a["w1"])),
                 (w_out[:], chunked(a["w_out"])), (w2[:], chunked(a["w2"])[:, 0:KH // 2, :]), (bg[:], over_partitions(a["bg"], NGR + NE)),
                 (rev[:], over_partitions(a["rev"], NE))]
        normalise(nc, norm, x_all, xnT_all, ident, psum, loads, loaded)
        block = stack.enter_context(nc.Block())
        NHID = 2 * KH
        WS = len(split)
        x_split = lambda b: WS + b * (1 + NHID) + 1
        hidden_split = lambda b, n: x_split(b) + n + 1
        NR = NE // 2 + 1

        @block.sync
        def _(sp):
            sp.wait_ge(low, 1)
            sp.dma_start(w2[:], chunked(a["w2"])[:, KH // 2:KH, :]).then_inc(loaded, 16)
            with sp.Fori(0, B) as b:
                sp.wait_ge(low, b * (1 + NHID))
                sp.dma_start(xnT[:], xnT_all[:, bass.ds(b, 1), :, :]).then_inc(x_here, 16)

        @block.tensor
        def _(pe):
            pe.wait_ge(loaded, 16 * len(loads))
            with pe.Fori(0, B) as b:
                pe.wait_ge(x_here, b * 16 + 16)
                pe.wait_ge(shifted, b)
                for t in range(TT):
                    for c in range(CC):
                        ins = pe.matmul(psum[:, 7, t * 16:t * 16 + NGR + NE], xnT[:, c, t * P:(t + 1) * P], wg[:, c, :],
                                        start=(c == 0), stop=(c == CC - 1))
                ins.then_inc(gates_ready, 1)
                for n in range(NHID):
                    j = n % KH
                    w = hid_pairs[n // KH]
                    bank = psum[:, 4 + n % 3, :]
                    if n == 0:
                        pe.wait_ge(low, x_split(b))
                    if n >= 3:
                        pe.wait_ge(hidden_taken, b * NHID + n - 2)
                    else:
                        pe.wait_ge(hidden_taken, b * NHID)
                    for part in range(2):
                        lo = part * HID + j * P
                        for c in range(CC):
                            ins = split_product(pe, bank[:, part * T:(part + 1) * T],
                                                parts(w, slice(None), c, slice(lo, lo + P)),
                                                (xnT_hi[:, c, :], xnT_lo[:, c, :]), c == 0, c == CC - 1)
                    ins.then_inc(projected, 1)
                for t in range(TT):
                    for r in range(NR):
                        n = t * NR + r
                        if n >= 4:
                            pe.wait_ge(routed_taken, b * TT * NR + n - 3)
                        else:
                            pe.wait_ge(routed_taken, b * TT * NR)
                        if n < 2:
                            pe.wait_ge(low, hidden_split(b, (n + 1) * KH - 1))
                        for k in range(KH):
                            cols = slice(0, D) if r == 0 else slice((r - 1) * 512, r * 512)
                            ins = split_product(pe, psum[:, n % 4, 0:D if r == 0 else 512],
                                                parts((hidden_hi, hidden_lo), slice(None), min(r, 1), k, slice(t * P, (t + 1) * P)),
                                                parts(out_pairs[min(r, 1)], slice(None), k, cols), k == 0, k == KH - 1)
                        ins.then_inc(routed_ready, 1)

        @block.scalar
        def _(act):
            act.wait_ge(loaded, 16 * len(loads))

            def round_hidden(b, n):
                act.wait_ge(hidden_taken, b * NHID + n + 1)
                act.activation(hidden_hi[:, n // KH, n % KH, :], hidden[:, n % 4, :], ACT.Copy).then_inc(high, 1)

            for n, (w, (hi, lo)) in enumerate(split):
                if n == WS - 1:
                    act.wait_ge(loaded, 16 * (len(loads) + 1))
                act.activation(hi, w[:], ACT.Copy).then_inc(high, 1)
            with act.Fori(0, B) as b:
                act.wait_ge(x_here, b * 16 + 16)
                act.activation(xnT_hi[:], xnT[:], ACT.Copy).then_inc(high, 1)
                act.wait_ge(shifted, b + 1)
                act.activation(expd[:], logits[:], ACT.Exp).then_inc(exp_done, 1)
                for n in range(NHID):
                    act.wait_ge(projected, b * NHID + n + 1)
                    if n >= 2:
                        act.wait_ge(hidden_taken, b * NHID + n - 1)
                    act.activation(silu[:, n % 2, :], psum[:, 4 + n % 3, 0:T], ACT.Silu).then_inc(silu_done, 1)
                    if n >= 1:
                        round_hidden(b, n - 1)
                round_hidden(b, NHID - 1)

        @block.vector
        def _(dve):
            dve.wait_ge(loaded, 16 * len(loads))
            for n, (w, (hi, lo)) in enumerate(split):
                dve.wait_ge(high, n + 1)
                dve.tensor_tensor(lo, w[:], hi.bitcast(F32), ALU.subtract).then_inc(low, 1)
            with dve.Fori(0, B) as b:
                dve.wait_ge(high, x_split(b))
                dve.tensor_tensor(xnT_lo[:], xnT[:], xnT_hi[:].bitcast(F32), ALU.subtract).then_inc(low, 1)
                per = 14 + TOP2_STEPS + TT * NE // 2
                step = Steps(dve, own, b * per, per)
                step.wait()
                dve.wait_ge(routed_taken, b * TT * NR)
                dve.wait_ge(gates_ready, b + 1)
                step.link(dve.tensor_tensor(logits[:], psum[:, 7, 0:TT * 16].rearrange("p (t n) -> p t n", t=TT)[:, :, 0:NGR + NE],
                                            bg[:].unsqueeze(1).to_broadcast([P, TT, NGR + NE]), ALU.add))
                by_group = lambda v: v[:, :, NGR:NGR + NE].rearrange("p t (g e) -> p t g e", g=NGR)
                step.did(dve.tensor_reduce(top[:, :, 0], logits[:, :, 0:NGR], AX.X, ALU.max))
                step.link(dve.tensor_reduce(top[:, :, 1:1 + NGR], by_group(logits), AX.X, ALU.max))
                dve.tensor_tensor(logits[:, :, 0:NGR], logits[:, :, 0:NGR], top[:, :, 0:1].to_broadcast([P, TT, NGR]), ALU.subtract)
                dve.tensor_tensor(by_group(logits), by_group(logits),
                                  top[:, :, 1:1 + NGR].unsqueeze(3).to_broadcast([P, TT, NGR, PER_GROUP]),
                                  ALU.subtract).then_inc(shifted, 1)

                def hidden_rest(b, n):
                    dve.wait_ge(high, hidden_split(b, n))
                    dve.tensor_tensor(hidden_lo[:, n // KH, n % KH, :], hidden[:, n % 4, :],
                                      hidden_hi[:, n // KH, n % KH, :].bitcast(F32), ALU.subtract).then_inc(low, 1)

                for n in range(NHID):
                    dve.wait_ge(low, hidden_split(b, n - 4) if n >= 4 else x_split(b))
                    dve.wait_ge(silu_done, b * NHID + n + 1)
                    dve.tensor_tensor(hidden[:, n % 4, :], silu[:, n % 2, :], psum[:, 4 + n % 3, T:2 * T],
                                      ALU.mult).then_inc(hidden_taken, 1)
                    if n >= 2:
                        hidden_rest(b, n - 2)
                hidden_rest(b, NHID - 2)
                hidden_rest(b, NHID - 1)
                dve.wait_ge(exp_done, b + 1)
                step.did(dve.tensor_reduce(total[:, :, 0], expd[:, :, 0:NGR], AX.X, ALU.add))
                step.link(dve.tensor_reduce(total[:, :, 1:1 + NGR], by_group(expd), AX.X, ALU.add))
                step.link(dve.reciprocal(total[:], total[:]))
                step.link(dve.tensor_tensor(expd[:, :, 0:NGR], expd[:, :, 0:NGR], total[:, :, 0:1].to_broadcast([P, TT, NGR]), ALU.mult))
                step.did(dve.tensor_tensor(chosen_group[:, :, 0], expd[:, :, 0], expd[:, :, 1], ALU.is_ge))
                step.link(dve.tensor_tensor(chosen_group[:, :, 1], expd[:, :, 1], expd[:, :, 0], ALU.is_gt))
                step.link(dve.tensor_reduce(group_p[:], expd[:, :, 0:NGR], AX.X, ALU.max))
                step.link(dve.tensor_tensor(chosen_group[:], chosen_group[:], group_p[:].unsqueeze(2).to_broadcast([P, TT, NGR]),
                                            ALU.mult))
                p4 = p[:].rearrange("p t (g e) -> p t g e", g=NGR)
                step.link(dve.tensor_tensor(p4, by_group(expd), total[:, :, 1:1 + NGR].unsqueeze(3).to_broadcast(
                    [P, TT, NGR, PER_GROUP]), ALU.mult))
                step.link(dve.tensor_tensor(p4, p4, chosen_group[:].unsqueeze(3).to_broadcast([P, TT, NGR, PER_GROUP]),
                                            ALU.mult))
                top2(dve, step, p[:], mask[:], (eq[:], rest[:]), red[:], rev[:], TT)
                step.link(dve.tensor_tensor(p[:], p[:], mask[:], ALU.mult))
                for t in range(TT):
                    R0 = (b * TT + t) * NR
                    x_t = x_all[:, bass.ds(b * TT + t, 1), :].rearrange("p a d -> p (a d)")
                    for r in range(NR):
                        bank = psum[:, (t * NR + r) % 4, :]
                        dve.wait_ge(routed_ready, R0 + r + 1)
                        if r == 0:
                            dve.tensor_tensor(acc[:, t, :], bank[:, 0:D], x_t, ALU.add).then_inc(routed_taken, 1)
                            continue
                        for half in range(2):
                            e = 2 * (r - 1) + half
                            dve.wait_ge(routed_taken, R0 + r) if half == 0 else step.wait()
                            ins = dve.scalar_tensor_tensor(x_t if e == NE - 1 else acc[:, t, :], bank[:, half * D:(half + 1) * D],
                                                           p[:, t, e:e + 1], acc[:, t, :], ALU.mult, ALU.add)
                            if half == 0:
                                step.did(ins)
                        ins.then_inc(routed_taken, 1)
                step.end()


STAGES = (("a0", attention0), ("x0", linear_attention), ("f0", switch_attention),
          ("a1", attention1), ("x1", cross_attention1), ("f1", experts))


def build(nc, inputs, out):
    with ExitStack() as stack:
        Scope.semaphores = stack
        s = Scope(nc, stack, "all")
        x_all = s.sb("x_all", [P, TILES, D])
        xnT_all = s.sb("xnT_all", [P, B, CC, T])
        ident = s.sb("ident", [P, P])
        psum = stack.enter_context(nc.psum_tensor("psum", [P, 8, 512], F32))
        x_loaded, stored = s.sem("x_loaded"), s.sem("stored")
        norm = Norm(Scope(nc, stack, "ln"))
        with nc.Block() as block:
            @block.sync
            def _(sp):
                sp.dma_start(ident[:], inputs["ident"]).then_inc(x_loaded, 16)
                sp.dma_start(x_all[:], inputs["x"].rearrange("b (t p) d -> p (b t) d", p=P)).then_inc(x_loaded, 16)
                sp.wait_ge(x_loaded, 32)
        for prefix, stage in STAGES:
            own = {k[len(prefix) + 1:]: v for k, v in inputs.items() if k.startswith(prefix + "_")}
            stage(nc, norm, x_all, xnT_all, ident, psum, own)
        with nc.Block() as block:
            @block.sync
            def _(sp):
                sp.dma_start(out.rearrange("b (t p) d -> p (b t) d", p=P), x_all[:]).then_inc(stored, 16)
                sp.wait_ge(stored, 16)


def _rope_tables():
    inv_freq = (1.0 / 10000.0 ** (np.arange(0, DH, 2, dtype=np.float32) / DH)).astype(np.float32)
    freqs = np.arange(T, dtype=np.float32)[:, None] * inv_freq[None, :]
    cos, sin = np.cos(freqs).T.astype(np.float32), np.sin(freqs).T.astype(np.float32)
    cos = np.tile(np.concatenate([cos, cos]), (P // DH, 1))
    sin = np.tile(np.concatenate([-sin, sin]), (P // DH, 1))
    return np.ascontiguousarray(np.stack([cos, sin], axis=1))


def _blocks(width):
    i = np.arange(P) // width
    return (i[:, None] == i[None, :]).astype(np.float32)


def _layouts(n):
    half = DH // 2
    plain = np.concatenate([np.arange(0, DH, 2), np.arange(1, DH, 2)])
    swapped = np.roll(plain, half)
    cols = {v: (np.arange(BR * NH)[:, None] * DH + p[None, :]).ravel() for v, p in (("", plain), ("s", swapped))}
    out = {"ident": np.eye(P, dtype=np.float32), "x": n["x"]}
    W, bias = n["L0_attn_W_Q"], n["L0_attn_b_Q"]
    out["a0_wq"], out["a0_wqs"] = W[:, cols[""]], W[:, cols["s"]]
    out["a0_bq"] = np.stack([bias[cols[v]].reshape(8, P).T for v in ("", "s")], axis=1)
    W, bias = n["L0_attn_W_K"], n["L0_attn_b_K"]
    out["a0_wk"], out["a0_wks"] = W[:, cols[""][:D]], W[:, cols["s"][:D]]
    out["a0_bk"] = np.stack([bias[cols[v][:D]].reshape(CC, P).T for v in ("", "s")], axis=1)
    out["a0_wv"], out["a0_bv"] = n["L0_attn_W_V"], n["L0_attn_b_V"]
    out["a0_wo"] = n["L0_attn_W_O"].reshape(BR * D, D)
    out["a0_bo"] = n["L0_attn_W_O_bias"].reshape(-1)
    out["a0_vnull"] = n["L0_attn_v_nulls"].reshape(-1)
    out["a0_sinks"] = n["L0_attn_sink_scalars"]
    out["a0_rope"] = _rope_tables()
    out["a0_same_head"] = _blocks(DH)
    out["a0_head_mask"] = np.ascontiguousarray(_blocks(DH)[:, ::DH])
    for name in ("q", "k", "v"):
        out[f"x0_w{name}"], out[f"x0_b{name}"] = n[f"L0_xattn_W{name}"], n[f"L0_xattn_b{name}"]
    out["x0_scale"] = n["L0_xattn_scale"].reshape(-1)
    out["x0_same_head"], out["x0_head_mask"] = out["a0_same_head"], out["a0_head_mask"]
    out["x0_ctxT"] = n["ctx_1024"].transpose(0, 2, 1).reshape(B * D, T)
    out["f0_wg"] = np.concatenate([n["L0_ffn_Ws"].reshape(-1, D), n["L0_ffn_Wd"].reshape(-1, D)]).T
    out["f0_wv"] = n["L0_ffn_Wv"].reshape(-1, D).T
    out["f0_wq"], out["f0_wk"] = n["L0_ffn_Wq"].reshape(-1, D).T, n["L0_ffn_Wk"].reshape(-1, D).T
    out["f0_wo"] = n["L0_ffn_Wo"].transpose(0, 2, 1).reshape(-1, D)
    out["f0_rev"] = np.arange(8, 0, -1, dtype=np.float32)
    out["a1_ctxT"] = n["L1_attn_context"].reshape(KEYS, CTX).T
    out["a1_wq"], out["a1_wk"], out["a1_wv"] = n["L1_attn_Wq"], n["L1_attn_Wk"], n["L1_attn_Wv"]
    out["a1_wo"], out["a1_bo"] = n["L1_attn_Wout"], n["L1_attn_bout"]
    for name in ("q", "k", "v"):
        out[f"x1_w{name}"] = n[f"L1_xattn_w_{name}"]
    out["x1_wo"], out["x1_bo"] = n["L1_xattn_out_w"].T, n["L1_xattn_out_b"]
    out["x1_mask"], out["x1_ctxT"] = n["mask_SxS2_ik0"], out["x0_ctxT"]
    out["f1_w_in"], out["f1_w1"], out["f1_w_out"] = n["L1_ffn_w_in"].T, n["L1_ffn_w1"].T, n["L1_ffn_w_out"].T
    out["f1_w2"] = n["L1_ffn_w2"].transpose(2, 0, 1).reshape(HID, NE * D)
    out["f1_wg"] = np.concatenate([n["L1_ffn_wg"], n["L1_ffn_we"]]).T
    out["f1_bg"] = np.concatenate([n["L1_ffn_gb"], n["L1_ffn_eb"]])
    out["f1_rev"] = out["f0_rev"]
    return out


def kernel(**inputs):
    import concourse.bacc as bacc
    from concourse.bass_utils import run_bass_kernel_spmd

    nc = bacc.Bacc("TRN2", target_bir_lowering=False, num_devices=1)
    arrays, tensors = {}, {}
    for name, value in _layouts({k: np.asarray(v) for k, v in inputs.items()}).items():
        value = np.ascontiguousarray(value)
        arrays[f"in_{name}"] = value
        tensors[name] = nc.dram_tensor(f"in_{name}", value.shape, mybir.dt.from_np(value.dtype), kind="ExternalInput").ap()
    out = nc.dram_tensor("out", (B, T, D), F32, kind="ExternalOutput").ap()
    build(nc, tensors, out)
    return run_bass_kernel_spmd(nc, [arrays], core_ids=[0]).results[0]["out"]
```
